# Optimizing a Trainium2 kernel written in Bass

```python
import numpy as np
import jax
import jax.numpy as jnp

def _softmax(x, axis=-1):
    return jax.nn.softmax(x, axis=axis)

def _gelu(x):
    return jax.nn.gelu(x, approximate=True)

def _silu(x):
    return jax.nn.silu(x)

def _sigmoid(x):
    return jax.nn.sigmoid(x)

def _layernorm(x, axis=-1, eps=1e-05):
    m = jnp.mean(x, axis=axis, keepdims=True)
    v = jnp.var(x, axis=axis, keepdims=True)
    return (x - m) / jnp.sqrt(v + eps)

def _scatter_add(tgt, idx, src, axis=0):
    return tgt.at[idx].add(src)

def _segment_sum(src, seg, n):
    return jax.ops.segment_sum(src, seg, n)
kernel_name = 'mk_adaln_attn_ffn_d1_seqx_r4_4f79ca'

def setup_inputs(seed: int=0):
    np.random.seed(seed)
    _w = jnp.asarray

    def _rec_inputs():
        import jax
        import jax.numpy as jnp
        _rk = jax.random.key(seed)
        x = 7.22e-05 + 1 * jax.random.normal(jax.random.fold_in(_rk, 1), (8, 512, 256), jnp.float32)
        _lenS = 512 - jax.random.randint(jax.random.fold_in(_rk, 7), (8,), 0, max(1, 512 // 4) + 1, jnp.int32)
        _lenS2 = 512 - jax.random.randint(jax.random.fold_in(_rk, 8), (8,), 0, max(1, 512 // 4) + 1, jnp.int32)
        cond_256 = 0.000887014 + 1.03683 * jax.random.normal(jax.random.fold_in(_rk, 11), (8, 64), jnp.float32)
        return (x, cond_256)
    x, cond_256 = _rec_inputs()

    def _L0_cond_setup():
        import jax, jax.numpy as jnp
        import numpy as np
        D_MODEL = 256
        D_T = 64
        N_HEADS = 16
        HIDDEN = 4 * D_MODEL
        EPS = 1e-06

        def _tc_rmsnorm(x, t, gw, gb, bw, bb):
            g = (t @ gw.T + gb)[:, None, :]
            b = (t @ bw.T + bb)[:, None, :]
            inv_rms = jax.lax.rsqrt(jnp.mean(x * x, axis=-1, keepdims=True) + EPS)
            return g * x * inv_rms + b

        def _attention(x, Wq, Wk, Wv, Wo):
            B, L, D = x.shape
            H = N_HEADS
            dh = D // H
            scale = np.sqrt(dh).astype(np.float32)
            q = (x @ Wq.T).reshape(B, L, H, dh)
            k = (x @ Wk.T).reshape(B, L, H, dh)
            v = (x @ Wv.T).reshape(B, L, H, dh)
            attn = jnp.einsum('blhd,bmhd->bhlm', q, k) / scale
            p = jax.nn.softmax(attn, axis=-1)
            o = jnp.einsum('bhlm,bmhd->blhd', p, v).reshape(B, L, D)
            return o @ Wo.T

        def _swiglu(x, gate_w, hid_w, out_w):
            return jax.nn.silu(x @ gate_w.T) * (x @ hid_w.T) @ out_w.T
        key = jax.random.key(seed)
        ks = jax.random.split(key, 20)
        B, L = (8, 256)
        s_d = 1.0 / np.sqrt(D_MODEL)
        s_t = 1.0 / np.sqrt(D_T)
        s_h = 1.0 / np.sqrt(HIDDEN)
        return {'x': jax.random.normal(ks[0], (B, L, D_MODEL), jnp.float32), 't': jax.random.normal(ks[1], (B, D_T), jnp.float32), 'Wq': jax.random.normal(ks[2], (D_MODEL, D_MODEL), jnp.float32) * s_d, 'Wk': jax.random.normal(ks[3], (D_MODEL, D_MODEL), jnp.float32) * s_d, 'Wv': jax.random.normal(ks[4], (D_MODEL, D_MODEL), jnp.float32) * s_d, 'Wo': jax.random.normal(ks[5], (D_MODEL, D_MODEL), jnp.float32) * s_d, 'g1w': jax.random.normal(ks[6], (D_MODEL, D_T), jnp.float32) * s_t, 'g1b': jnp.ones((D_MODEL,), jnp.float32), 'b1w': jax.random.normal(ks[7], (D_MODEL, D_T), jnp.float32) * s_t, 'b1b': jnp.zeros((D_MODEL,), jnp.float32), 'g2w': jax.random.normal(ks[8], (D_MODEL, D_T), jnp.float32) * s_t, 'g2b': jnp.ones((D_MODEL,), jnp.float32), 'b2w': jax.random.normal(ks[9], (D_MODEL, D_T), jnp.float32) * s_t, 'b2b': jnp.zeros((D_MODEL,), jnp.float32), 'gate_w': jax.random.normal(ks[10], (HIDDEN, D_MODEL), jnp.float32) * s_d, 'hid_w': jax.random.normal(ks[11], (HIDDEN, D_MODEL), jnp.float32) * s_d, 'out_w': jax.random.normal(ks[12], (D_MODEL, HIDDEN), jnp.float32) * s_h}
    _L0_cond_all = _L0_cond_setup()
    _L0_cond_in = {k: v for k, v in _L0_cond_all.items() if k in ('Wq', 'Wk', 'Wv', 'Wo', 'g1w', 'g1b', 'b1w', 'b1b', 'g2w', 'g2b', 'b2w', 'b2b', 'gate_w', 'hid_w', 'out_w')}
    del _L0_cond_all

    def _L0_attn_setup():
        import jax, jax.numpy as jnp
        import numpy as np
        HEADS = 16
        LOCAL_HEADS = 4
        DIM = 256
        DH = DIM // HEADS
        WINDOW = 128
        BLINDSPOT = 64

        def _look_around(x, buckets):
            pad_cfg = ((0, 0), (1, 0)) + ((0, 0),) * (x.ndim - 2)
            pv = -1.0 if jnp.issubdtype(x.dtype, jnp.floating) else -1
            p = jnp.pad(x, pad_cfg, constant_values=pv)
            return jnp.concatenate([p[:, :buckets], p[:, 1:buckets + 1]], axis=2)

        def _local_attn(q, k, v):
            b, lh, t, e = q.shape
            bm = b * lh
            buckets = t // WINDOW
            bq = q.reshape(bm, buckets, WINDOW, e)
            bk = k.reshape(bm, buckets, WINDOW, e)
            bv = v.reshape(bm, buckets, WINDOW, e)
            bk2 = _look_around(bk, buckets)
            bv2 = _look_around(bv, buckets)
            ticker = jnp.arange(t, dtype=jnp.int32).reshape(1, buckets, WINDOW)
            bq_k = _look_around(ticker, buckets)
            dots = jnp.einsum('buie,buje->buij', bq, bk2) * e ** (-0.5)
            mask_value = -jnp.finfo(dots.dtype).max
            causal_mask = ticker[:, :, :, None] < bq_k[:, :, None, :]
            pad_mask = bq_k[:, :, None, :] == -1
            dots = jnp.where(causal_mask | pad_mask, mask_value, dots)
            attn = jax.nn.softmax(dots, axis=-1)
            out = jnp.einsum('buij,buje->buie', attn, bv2)
            return out.reshape(b, lh, t, e)

        def _causal_linear_attn(q, k, v):
            b, h, n, e = q.shape
            u = n // BLINDSPOT
            q = jax.nn.softmax(q, axis=-1)
            k = jax.nn.elu(k) + 1.0
            bq = q.reshape(b, h, u, BLINDSPOT, e)
            bk = k.reshape(b, h, u, BLINDSPOT, e)
            bv = v.reshape(b, h, u, BLINDSPOT, e)
            bk_cumsum = jnp.cumsum(bk.sum(axis=-2), axis=-2)
            ctx = jnp.einsum('bhund,bhune->bhude', bk, bv)
            ctx = jnp.cumsum(ctx, axis=2)
            ctx = ctx / (bk_cumsum[..., None] + 1e-06)
            ctx = jnp.pad(ctx, ((0, 0), (0, 0), (1, 0), (0, 0), (0, 0)))[:, :, :u]
            attn = jnp.einsum('bhund,bhude->bhune', bq, ctx)
            return attn.reshape(b, h, n, e)
        key = jax.random.key(seed)
        ks = jax.random.split(key, 6)
        s = 1.0 / np.sqrt(DIM)
        x = jax.random.normal(ks[0], (4, 2048, DIM), dtype=jnp.float32)
        Wq = jax.random.normal(ks[1], (DIM, DIM), dtype=jnp.float32) * s
        Wk = jax.random.normal(ks[2], (DIM, DIM), dtype=jnp.float32) * s
        Wv = jax.random.normal(ks[3], (DIM, DIM), dtype=jnp.float32) * s
        Wo = jax.random.normal(ks[4], (DIM, DIM), dtype=jnp.float32) * s
        bo = jax.random.normal(ks[5], (DIM,), dtype=jnp.float32) * 0.01
        return {'x': x, 'Wq': Wq, 'Wk': Wk, 'Wv': Wv, 'Wo': Wo, 'bo': bo}
    _L0_attn_all = _L0_attn_setup()
    _L0_attn_in = {k: v for k, v in _L0_attn_all.items() if k in ('Wq', 'Wk', 'Wv', 'Wo', 'bo')}
    del _L0_attn_all

    def _L0_cond2_setup():
        import jax, jax.numpy as jnp
        import numpy as np
        EPS = 1e-08

        def hamilton(q1, q2):
            w1, x1, y1, z1 = (q1[..., i, :] for i in range(4))
            w2, x2, y2, z2 = (q2[..., i, :] for i in range(4))
            w = w1 * w2 - x1 * x2 - y1 * y2 - z1 * z2
            x = w1 * x2 + x1 * w2 + y1 * z2 - z1 * y2
            y = w1 * y2 - x1 * z2 + y1 * w2 + z1 * x2
            z = w1 * z2 + x1 * y2 - y1 * x2 + z1 * w2
            return jnp.stack([w, x, y, z], axis=-2)

        def _normalize(q):
            return q / jnp.sqrt(jnp.sum(q * q, axis=0, keepdims=True) + EPS)
        key = jax.random.key(seed)
        k1, k2, k3, k4 = jax.random.split(key, 4)
        B, T, d_model = (4, 1024, 256)
        quat_dim = d_model // 4
        x = jax.random.normal(k1, (B, T, d_model), dtype=jnp.float32)
        q_left = jax.random.normal(k2, (4, quat_dim), dtype=jnp.float32)
        q_right = jax.random.normal(k3, (4, quat_dim), dtype=jnp.float32)
        spectral_gate = jax.random.uniform(k4, (1, 1, 1, quat_dim), dtype=jnp.float32)
        return {'x': x, 'q_left': q_left, 'q_right': q_right, 'spectral_gate': spectral_gate}
    _L0_cond2_all = _L0_cond2_setup()
    _L0_cond2_in = {k: v for k, v in _L0_cond2_all.items() if k in ('q_right', 'spectral_gate')}
    del _L0_cond2_all

    def _L0_ffn_setup():
        import jax, jax.numpy as jnp
        import numpy as np
        NQ, NK, H, DH = (256, 128, 8, 64)
        key = jax.random.key(seed)
        ks = jax.random.split(key, 8)
        b, n, d, g = (4, 1024, 256, 4)
        di = H * DH
        s = lambda fan: 1.0 / np.sqrt(fan)
        return {'x': jax.random.normal(ks[0], (b, n, d), jnp.float32), 'w_qr': jax.random.normal(ks[1], (g, d), jnp.float32) * s(d), 'w_kvr': jax.random.normal(ks[2], (g, d), jnp.float32) * s(d), 'w_q': jax.random.normal(ks[3], (g, di, d), jnp.float32) * s(d), 'w_kv': jax.random.normal(ks[4], (g, 2 * di, d), jnp.float32) * s(d), 'w_out': jax.random.normal(ks[5], (g, d, di), jnp.float32) * s(di), 'null_kv': jax.random.normal(ks[6], (2, g, H, 1, DH), jnp.float32), 'null_token': jax.random.normal(ks[7], (1, 1, d), jnp.float32)}
    _L0_ffn_all = _L0_ffn_setup()
    _L0_ffn_in = {k: v for k, v in _L0_ffn_all.items() if k in ('w_qr', 'w_kvr', 'w_q', 'w_kv', 'w_out', 'null_kv', 'null_token')}
    del _L0_ffn_all
    return {'x': x, 'cond_256': cond_256, 'L0_cond_Wq': _L0_cond_in['Wq'], 'L0_cond_Wk': _L0_cond_in['Wk'], 'L0_cond_Wv': _L0_cond_in['Wv'], 'L0_cond_Wo': _L0_cond_in['Wo'], 'L0_cond_g1w': _L0_cond_in['g1w'], 'L0_cond_g1b': _L0_cond_in['g1b'], 'L0_cond_b1w': _L0_cond_in['b1w'], 'L0_cond_b1b': _L0_cond_in['b1b'], 'L0_cond_g2w': _L0_cond_in['g2w'], 'L0_cond_g2b': _L0_cond_in['g2b'], 'L0_cond_b2w': _L0_cond_in['b2w'], 'L0_cond_b2b': _L0_cond_in['b2b'], 'L0_cond_gate_w': _L0_cond_in['gate_w'], 'L0_cond_hid_w': _L0_cond_in['hid_w'], 'L0_cond_out_w': _L0_cond_in['out_w'], 'L0_attn_Wq': _L0_attn_in['Wq'], 'L0_attn_Wk': _L0_attn_in['Wk'], 'L0_attn_Wv': _L0_attn_in['Wv'], 'L0_attn_Wo': _L0_attn_in['Wo'], 'L0_attn_bo': _L0_attn_in['bo'], 'L0_cond2_q_right': _L0_cond2_in['q_right'], 'L0_cond2_spectral_gate': _L0_cond2_in['spectral_gate'], 'L0_ffn_w_qr': _L0_ffn_in['w_qr'], 'L0_ffn_w_kvr': _L0_ffn_in['w_kvr'], 'L0_ffn_w_q': _L0_ffn_in['w_q'], 'L0_ffn_w_kv': _L0_ffn_in['w_kv'], 'L0_ffn_w_out': _L0_ffn_in['w_out'], 'L0_ffn_null_kv': _L0_ffn_in['null_kv'], 'L0_ffn_null_token': _L0_ffn_in['null_token']}

def reference(x, cond_256, L0_cond_Wq, L0_cond_Wk, L0_cond_Wv, L0_cond_Wo, L0_cond_g1w, L0_cond_g1b, L0_cond_b1w, L0_cond_b1b, L0_cond_g2w, L0_cond_g2b, L0_cond_b2w, L0_cond_b2b, L0_cond_gate_w, L0_cond_hid_w, L0_cond_out_w, L0_attn_Wq, L0_attn_Wk, L0_attn_Wv, L0_attn_Wo, L0_attn_bo, L0_cond2_q_right, L0_cond2_spectral_gate, L0_ffn_w_qr, L0_ffn_w_kvr, L0_ffn_w_q, L0_ffn_w_kv, L0_ffn_w_out, L0_ffn_null_kv, L0_ffn_null_token):
    import jax
    import jax.numpy as jnp

    def _L0_cond_ref(x, t, Wq, Wk, Wv, Wo, g1w, g1b, b1w, b1b, g2w, g2b, b2w, b2b, gate_w, hid_w, out_w):
        import jax, jax.numpy as jnp
        import numpy as np
        D_MODEL = 256
        D_T = 64
        N_HEADS = 16
        HIDDEN = 4 * D_MODEL
        EPS = 1e-06

        def _tc_rmsnorm(x, t, gw, gb, bw, bb):
            g = (t @ gw.T + gb)[:, None, :]
            b = (t @ bw.T + bb)[:, None, :]
            inv_rms = jax.lax.rsqrt(jnp.mean(x * x, axis=-1, keepdims=True) + EPS)
            return g * x * inv_rms + b

        def _attention(x, Wq, Wk, Wv, Wo):
            B, L, D = x.shape
            H = N_HEADS
            dh = D // H
            scale = np.sqrt(dh).astype(np.float32)
            q = (x @ Wq.T).reshape(B, L, H, dh)
            k = (x @ Wk.T).reshape(B, L, H, dh)
            v = (x @ Wv.T).reshape(B, L, H, dh)
            attn = jnp.einsum('blhd,bmhd->bhlm', q, k) / scale
            p = jax.nn.softmax(attn, axis=-1)
            o = jnp.einsum('bhlm,bmhd->blhd', p, v).reshape(B, L, D)
            return o @ Wo.T

        def _swiglu(x, gate_w, hid_w, out_w):
            return jax.nn.silu(x @ gate_w.T) * (x @ hid_w.T) @ out_w.T
        x = x + _attention(_tc_rmsnorm(x, t, g1w, g1b, b1w, b1b), Wq, Wk, Wv, Wo)
        return x + _swiglu(_tc_rmsnorm(x, t, g2w, g2b, b2w, b2b), gate_w, hid_w, out_w)

    def _L0_attn_ref(x, Wq, Wk, Wv, Wo, bo):
        import jax, jax.numpy as jnp
        import numpy as np
        HEADS = 16
        LOCAL_HEADS = 4
        DIM = 256
        DH = DIM // HEADS
        WINDOW = 128
        BLINDSPOT = 64

        def _look_around(x, buckets):
            pad_cfg = ((0, 0), (1, 0)) + ((0, 0),) * (x.ndim - 2)
            pv = -1.0 if jnp.issubdtype(x.dtype, jnp.floating) else -1
            p = jnp.pad(x, pad_cfg, constant_values=pv)
            return jnp.concatenate([p[:, :buckets], p[:, 1:buckets + 1]], axis=2)

        def _local_attn(q, k, v):
            b, lh, t, e = q.shape
            bm = b * lh
            buckets = t // WINDOW
            bq = q.reshape(bm, buckets, WINDOW, e)
            bk = k.reshape(bm, buckets, WINDOW, e)
            bv = v.reshape(bm, buckets, WINDOW, e)
            bk2 = _look_around(bk, buckets)
            bv2 = _look_around(bv, buckets)
            ticker = jnp.arange(t, dtype=jnp.int32).reshape(1, buckets, WINDOW)
            bq_k = _look_around(ticker, buckets)
            dots = jnp.einsum('buie,buje->buij', bq, bk2) * e ** (-0.5)
            mask_value = -jnp.finfo(dots.dtype).max
            causal_mask = ticker[:, :, :, None] < bq_k[:, :, None, :]
            pad_mask = bq_k[:, :, None, :] == -1
            dots = jnp.where(causal_mask | pad_mask, mask_value, dots)
            attn = jax.nn.softmax(dots, axis=-1)
            out = jnp.einsum('buij,buje->buie', attn, bv2)
            return out.reshape(b, lh, t, e)

        def _causal_linear_attn(q, k, v):
            b, h, n, e = q.shape
            u = n // BLINDSPOT
            q = jax.nn.softmax(q, axis=-1)
            k = jax.nn.elu(k) + 1.0
            bq = q.reshape(b, h, u, BLINDSPOT, e)
            bk = k.reshape(b, h, u, BLINDSPOT, e)
            bv = v.reshape(b, h, u, BLINDSPOT, e)
            bk_cumsum = jnp.cumsum(bk.sum(axis=-2), axis=-2)
            ctx = jnp.einsum('bhund,bhune->bhude', bk, bv)
            ctx = jnp.cumsum(ctx, axis=2)
            ctx = ctx / (bk_cumsum[..., None] + 1e-06)
            ctx = jnp.pad(ctx, ((0, 0), (0, 0), (1, 0), (0, 0), (0, 0)))[:, :, :u]
            attn = jnp.einsum('bhund,bhude->bhune', bq, ctx)
            return attn.reshape(b, h, n, e)
        b, t, dim = x.shape
        q = x @ Wq
        k = x @ Wk
        v = x @ Wv
        mh = lambda z: z.reshape(b, t, HEADS, DH).transpose(0, 2, 1, 3)
        q, k, v = (mh(q), mh(k), mh(v))
        lq, gq = (q[:, :LOCAL_HEADS], q[:, LOCAL_HEADS:])
        lk, gk = (k[:, :LOCAL_HEADS], k[:, LOCAL_HEADS:])
        lv, gv = (v[:, :LOCAL_HEADS], v[:, LOCAL_HEADS:])
        local_out = _local_attn(lq, lk, lv)
        global_out = _causal_linear_attn(gq, gk, gv)
        attn = jnp.concatenate([local_out, global_out], axis=1)
        attn = attn.transpose(0, 2, 1, 3).reshape(b, t, dim)
        return attn @ Wo + bo

    def _L0_cond2_ref(x, q_left, q_right, spectral_gate):
        import jax, jax.numpy as jnp
        import numpy as np
        EPS = 1e-08

        def hamilton(q1, q2):
            w1, x1, y1, z1 = (q1[..., i, :] for i in range(4))
            w2, x2, y2, z2 = (q2[..., i, :] for i in range(4))
            w = w1 * w2 - x1 * x2 - y1 * y2 - z1 * z2
            x = w1 * x2 + x1 * w2 + y1 * z2 - z1 * y2
            y = w1 * y2 - x1 * z2 + y1 * w2 + z1 * x2
            z = w1 * z2 + x1 * y2 - y1 * x2 + z1 * w2
            return jnp.stack([w, x, y, z], axis=-2)

        def _normalize(q):
            return q / jnp.sqrt(jnp.sum(q * q, axis=0, keepdims=True) + EPS)
        B, T, d_model = x.shape
        quat_dim = d_model // 4
        x_quat = x.reshape(B, T, 4, quat_dim)
        x_spectral = jnp.fft.fft(x_quat, axis=1)
        x_filtered = jnp.fft.ifft(x_spectral * spectral_gate, axis=1).real.astype(x.dtype)
        q_left_n = _normalize(q_left)
        q_right_n = _normalize(q_right)
        conj_sign = jnp.array([1.0, -1.0, -1.0, -1.0], dtype=x.dtype)[:, None]
        q_right_conj = q_right_n * conj_sign
        x_right = hamilton(x_filtered, q_right_conj)
        x_rotated = hamilton(q_left_n, x_right)
        return x_rotated.reshape(B, T, d_model)

    def _L0_ffn_ref(x, w_qr, w_kvr, w_q, w_kv, w_out, null_kv, null_token):
        import jax, jax.numpy as jnp
        import numpy as np
        NQ, NK, H, DH = (256, 128, 8, 64)
        b, n, d = x.shape
        g = w_qr.shape[0]
        bidx = jnp.arange(b)[:, None, None]
        q_logits = jnp.einsum('bnd,gd->bgn', x, w_qr)
        q_top, q_idx = jax.lax.top_k(q_logits, NQ)
        q_scores = jax.nn.sigmoid(q_top)[..., None]
        queries = x[bidx, q_idx]
        kv_logits = jnp.einsum('bnd,gd->bgn', x, w_kvr)
        kv_top, kv_idx = jax.lax.top_k(kv_logits, NK)
        kv_scores = jax.nn.sigmoid(kv_top)[:, :, None, :, None]
        key_values = x[bidx, kv_idx]
        q = jnp.einsum('bgnd,ged->bgne', queries, w_q)
        kv = jnp.einsum('bgnd,ged->bgne', key_values, w_kv)
        k, v = jnp.split(kv, 2, axis=-1)
        heads = lambda t: t.reshape(b, g, -1, H, DH).transpose(0, 1, 3, 2, 4)
        q, k, v = (heads(q), heads(k), heads(v))
        v = v * kv_scores
        nk = jnp.broadcast_to(null_kv[0][None], (b, g, H, 1, DH))
        nv = jnp.broadcast_to(null_kv[1][None], (b, g, H, 1, DH))
        k = jnp.concatenate([nk, k], axis=-2)
        v = jnp.concatenate([nv, v], axis=-2)
        attn = jax.nn.softmax(jnp.einsum('bghid,bghjd->bghij', q, k) * DH ** (-0.5), axis=-1)
        o = jnp.einsum('bghij,bghjd->bghid', attn, v)
        o = o.transpose(0, 1, 3, 2, 4).reshape(b, g, NQ, H * DH)
        o = jnp.einsum('bgne,gde->bgnd', o, w_out)
        o = o * q_scores
        flat_idx = q_idx.reshape(b, g * NQ)
        flat_o = o.reshape(b, g * NQ, d)
        b2 = jnp.arange(b)[:, None]
        summed = jnp.zeros_like(x).at[b2, flat_idx].add(flat_o)
        counts = jnp.zeros((b, n), x.dtype).at[b2, flat_idx].add(1.0)[..., None]
        meaned = summed / jnp.clip(counts, 1e-05)
        return jnp.where(counts > 0, meaned, null_token)
    x = x + _L0_attn_ref(_L0_cond_ref(x, cond_256, L0_cond_Wq, L0_cond_Wk, L0_cond_Wv, L0_cond_Wo, L0_cond_g1w, L0_cond_g1b, L0_cond_b1w, L0_cond_b1b, L0_cond_g2w, L0_cond_g2b, L0_cond_b2w, L0_cond_b2b, L0_cond_gate_w, L0_cond_hid_w, L0_cond_out_w), L0_attn_Wq, L0_attn_Wk, L0_attn_Wv, L0_attn_Wo, L0_attn_bo)
    x = x + _L0_ffn_ref(_L0_cond2_ref(x, cond_256, L0_cond2_q_right, L0_cond2_spectral_gate), L0_ffn_w_qr, L0_ffn_w_kvr, L0_ffn_w_q, L0_ffn_w_kv, L0_ffn_w_out, L0_ffn_null_kv, L0_ffn_null_token)
    return x

_drawn_inputs = setup_inputs


def setup_inputs(seed=0):
    import zlib

    import numpy as np

    out = dict(_drawn_inputs(seed))
    spreads = {'L0_cond_g1b': (1.0, 0.2),
     'L0_cond_b1b': (0.0, 0.1),
     'L0_cond_g2b': (1.0, 0.2),
     'L0_cond_b2b': (0.0, 0.1)}
    factors = {'L0_attn_bo': 8.0, 'L0_ffn_w_q': 4.874, 'L0_ffn_null_kv': 8.0}
    for name, (base, spread) in spreads.items():
        noise = np.random.default_rng([zlib.crc32(name.encode()), seed]).standard_normal(out[name].shape)
        drawn = base * np.exp(spread * noise) if base else spread * noise
        out[name] = jnp.asarray(drawn.astype(out[name].dtype))
    for name, factor in factors.items():
        out[name] = (out[name] * factor).astype(out[name].dtype)
    return out
```

```python
from contextlib import ExitStack

import numpy as np
import concourse.bass as bass
from concourse import mybir

F32 = mybir.dt.float32
F32R = mybir.dt.float32r
BF16 = mybir.dt.bfloat16
ALU = mybir.AluOpType
ACT = mybir.ActivationFunctionType
AX = mybir.AxisListType.X

P = 128
NB, L, D = 8, 512, 256
NT, ND = L // P, D // P
H, DH = 16, 16
STRIP = 32
HG = H * STRIP // P
HID = 4 * D
NM = HID // P
NLOC, NLIN = 4, 12
LH = NLIN // 2
LW = LH * DH
BLK = 64
NU = L // BLK - 1
CW = DH + 1
G, NQ, NK = 4, 256, 128
FH, FD = 8, 64
E = FH * FD
NE = E // P
SROW = 4 * DH
KST = 96
BANK = 512
CBIG = 1e30



def columns(parts):
    at, out = 0, {}
    for name, n in parts:
        out[name] = (at, at + n)
        at += n
    return out, at


WA, WA_N = columns([("wq", ND * D), ("wk", ND * D), ("wv", ND * D), ("wo", HG * D),
                    ("gate", ND * HID), ("hid", ND * HID), ("down", NM * D)])
WB, WB_N = columns([("lq", ND * P), ("lk", ND * P), ("lin", ND * 2 * NLIN * DH), ("wv", ND * D),
                    ("wo_loc", D), ("wo_lin", 2 * D)])
WC, WC_N = columns([("wq", ND * E), ("wk", ND * E), ("wv", ND * E), ("wo", NE * D), ("nk", NE),
                    ("nv", NE * FH)])
CO, CO_N = columns([("ident", P), ("causal", P), ("all", P), ("hmask", NLOC), ("dsel", 4),
                    ("cmask", 64), ("bmask", LH), ("qleft", NB), ("qright", 4), ("sg", 1),
                    ("sign", 4), ("wr", ND * 2 * G), ("cb", 4 * ND), ("cond", NB)])
CR, CR_N = columns([("iota", NQ), ("part", 2), ("before", P), ("ones", P), ("kvec", 2 * NB * G)])
CW4 = 4 * D


def phase_dense(nc, t, dr):
    with ExitStack() as ctx:
        def sb(name, shape, dt=F32):
            return ctx.enter_context(nc.sbuf_tensor(name, shape, dt))

        def sem(name):
            return ctx.enter_context(nc.semaphore(name))

        ps = t["ps"]

        def bank(k, n=1):
            return ps[:, k * BANK:(k + n) * BANK]

        co = t["co"]

        def const(name):
            return co[:, CO[name][0]:CO[name][1]]

        ident = const("ident")
        wa = sb("wa", [P, WA_N])
        wb = sb("wb", [P, WB_N])
        bo = sb("bo", [P, D])
        stack_q = sb("stack_q", [KST, H, L], F32R)
        stack_k = sb("stack_k", [KST, H, L], F32R)
        qk_hi = sb("qk_hi", [P, 2, L], F32R)
        qk_lo = sb("qk_lo", [P, 2, L], F32R)
        pt = sb("pt", [P, 8 * L])
        big = sb("big", [P, NM * L])
        va = sb("va", [P, NT, H, STRIP])
        heads_t = sb("heads_t", [P, HG, L])
        x_in = sb("x_in", [P, NT, D])
        xm = sb("xm", [P, NT, D])
        xc = sb("xc", [P, NT, D])
        hn = sb("hn", [P, NT, D])
        hT = sb("hT", [P, ND, L])
        temp = sb("temp", [P, 2 * NU * (LH * CW + LW)])
        mrow = sb("mrow", [H, L], F32R)
        small = sb("small", [P, 448])
        causal_b = sb("causal_b", [P, P], BF16)
        all_b = sb("all_b", [P, P], BF16)
        ident_b = sb("ident_b", [P, P], BF16)
        rot = sb("rot", [P, ND, 4, 64])
        wc = sb("wc", [P, ND, 2 * G])

        def w(pack, cols, name, k):
            a, b = cols[name]
            return pack[:, a:b].rearrange("p (k n) -> p k n", k=k)

        wq, wk, wv = (w(wa, WA, n, ND) for n in ("wq", "wk", "wv"))
        wo, wdown = w(wa, WA, "wo", HG), w(wa, WA, "down", NM)
        wgate, whid = w(wa, WA, "gate", ND), w(wa, WA, "hid", ND)
        blq, blk, blin, bwv = (w(wb, WB, n, ND) for n in ("lq", "lk", "lin", "wv"))
        bwo_loc = wb[:, WB["wo_loc"][0]:WB["wo_loc"][1]]
        bwo_lin = w(wb, WB, "wo_lin", 2)

        p_t = pt[:, :].rearrange("p (s j n) -> p s j n", s=2, j=4)
        lpT = pt[:, :].rearrange("p (h u c n) -> p h u c n", h=NLOC, u=NT, c=2)
        gT = big[:, :].rearrange("p (m n) -> p m n", m=NM)
        lp = big[:, 0:2048].rearrange("p (s u n) -> p s u n", s=2, u=NT)
        q_e = big[:, 2048:2816].rearrange("p (t n) -> p t n", t=NT)
        k_e = big[:, 2816:3584].rearrange("p (t n) -> p t n", t=NT)
        lkT = big[:, 3584:4096]
        locT = big[:, 0:512]
        logit = big[0:2 * G, 512:1024]
        cw = big[0:64, 0:CW4]
        rot_t = big[:, CW4:CW4 + ND * D].rearrange("p (k i c) -> p k i c", k=ND, i=4)
        kk = xm[:, :, 0:NLIN * DH]
        osb = temp[:, 0:1024].rearrange("p (s n) -> p s n", s=2)
        tg = temp[:, 1024:2048].rearrange("p (s n) -> p s n", s=2)
        cum = temp[0:LW, 0:2 * NU * LH * CW].rearrange("p (u n) -> p u n", u=NU)
        ctxn = temp[0:LW, 2 * NU * LH * CW:].rearrange("p (v n) -> p v n", v=2 * NU)
        lqm = heads_t
        q_n = hn[:, :, 0:NLIN * DH]
        qlT = xc[0:LW, :, :].rearrange("p t n -> p (t n)").rearrange("p (a n) -> p a n", a=2)
        linT = hT[0:LW, :, :]
        x1 = xm
        x2 = hn
        tg2 = xc[:, :, :].rearrange("p (s a) n -> p s (a n)", s=2)
        rspread = xc[:, 0:2, :].rearrange("p a n -> p (a n)")
        mtok = small[:, 0:64].rearrange("p (t h) -> p t h", t=NT)
        ms, msn, inv, half = (small[:, 64 + 4 * k:68 + 4 * k] for k in range(4))
        rden = small[:, 80:96]
        eps = small[:, 420:424]
        gb = small[:, 96:160].rearrange("p (k b) -> p k b", b=NB)
        gbc = small[:, 160:168]
        lmax, lneg, lden, lrec = (small[:, 168 + 16 * k:184 + 16 * k] for k in range(4))
        qmx, qsum = small[:, 232:280], small[:, 280:328]
        qrec = small[:, 328:376]
        ks = small[0:LW, 376:390]
        krec = small[0:LW, 390:404]
        rl, nrm, lrot = small[:, 404:408], small[:, 408:412], small[:, 412:416]
        rrot = small[:, 416:420]
        kmask = sb("kmask", [LW, 2 * NU, LH])
        kmask2 = sb("kmask2", [LW, 2 * NU, LH])
        coef = sb("coef", [P, 4, 4, 4])

        s = {n: sem(n) for n in (
            "loaded", "casts", "setup", "setup_pe", "setup_pool", "zeros_stored", "cleared",
            "x_loaded", "squares", "inv_tmp", "inv_ready", "hn_ready", "hT_ps", "hT_ready",
            "qk_ps", "v_ps", "hi_ready", "lo_ready", "va_ready", "parts_stored", "stacked",
            "row_clear", "s_ps", "smax", "m_ps", "mrow_ready", "mrow_stored", "mrow_back",
            "st_ps", "exp_done", "pv_done", "osb_ready", "den_ps", "rden_ready", "rspread_ready", "rb_ps",
            "oT_ready", "ao_ps", "xm_ready", "gh_ps", "tg_ready", "tg2_ready", "sg_done",
            "dn_ps", "xc_ready", "yT_ps", "yT_ready", "lq_ps", "lk_ps", "lin_ps", "lv_ps",
            "lqm_ready", "lk_ready", "link", "qs_ready", "kmin_ready", "qe_ready", "ke_ready",
            "qn_ready", "kk_ready", "lv_ready", "ls_ps", "lneg_ready", "lexp", "lnorm", "lt_ps",
            "lt_ready", "lo_ps", "locT_ready", "ctx_ps", "ctx_ready", "ql_ps", "ql_ready",
            "lin_out_ps", "linT_ready", "bo_added", "y_ps", "x1_ready", "x1T_ps", "x1T_ready",
            "x2_ps", "x2_ready", "lg_ps", "lg_ready", "stored", "act_link", "pool_link")}

        block = ctx.enter_context(nc.Block())

        @block.sync
        def _(sp):
            sp.dma_start(co[:, :], dr["co"]).then_inc(s["loaded"], 16)
            sp.dma_start(cw[:, :], dr["cw"]).then_inc(s["loaded"], 16)
            sp.dma_start(wa[:, :], dr["wa"]).then_inc(s["loaded"], 16)
            sp.dma_start(wb[:, :], dr["wb"]).then_inc(s["loaded"], 16)
            sp.dma_start(bo[:, :], dr["bo"].to_broadcast([P, D])).then_inc(s["loaded"], 16)
            sp.wait_ge(s["cleared"], 4)
            sp.dma_start(dr["zero"], mrow[:, :].bitcast(F32)).then_inc(s["zeros_stored"], 16)
            sp.wait_ge(s["zeros_stored"], 16)
            with sp.Fori(0, NB) as i:
                sp.wait_ge(s["x1_ready"], i * 2)
                sp.dma_start(x_in[:, :, :], dr["x"][bass.ds(i, 1)].rearrange("a (t p) d -> p (a t) d", p=P))\
                    .then_inc(s["x_loaded"], 16)
                sp.wait_ge(s["st_ps"], i * 32)
                sp.dma_start(stack_q[SROW:SROW + 1, :, :].bitcast(F32), dr["zero"][None, :, :])\
                    .then_inc(s["row_clear"], 16)
                for o in range(2):
                    sp.wait_ge(s["hi_ready"], i * 4 + 2 * o + 2)
                    sp.dma_start(dr["parts"][o, 0].rearrange("(m p) n -> p m n", p=P),
                                 qk_hi[:, :, :].bitcast(F32)).then_inc(s["parts_stored"], 16)
                    sp.wait_ge(s["lo_ready"], i * 4 + 2 * o + 2)
                    sp.dma_start(dr["parts"][o, 1].rearrange("(m p) n -> p m n", p=P),
                                 qk_lo[:, :, :].bitcast(F32)).then_inc(s["parts_stored"], 16)
                    sp.wait_ge(s["parts_stored"], i * 64 + 32 * o + 32)
                    for r, part in enumerate(((0, 1, 0, 1), (0, 1, 1, 0))[o]):
                        sp.dma_start((stack_q, stack_k)[o][DH * r:DH * r + DH, :, :].bitcast(F32),
                                     dr["parts"][o, part].rearrange("(h d) n -> d h n", d=DH))\
                            .then_inc(s["stacked"], 16)
                sp.wait_ge(s["mrow_ready"], i + 1)
                sp.dma_start(dr["maxima"], mrow[:, :].bitcast(F32)).then_inc(s["mrow_stored"], 16)
                sp.wait_ge(s["mrow_stored"], i * 16 + 16)
                sp.dma_start(stack_q[SROW:SROW + 1, :, :].bitcast(F32), dr["maxima"][None, :, :])\
                    .then_inc(s["mrow_back"], 16)
                sp.wait_ge(s["x1_ready"], i * 2 + 2)
                sp.dma_start(dr["x1"][bass.ds(i, 1)].rearrange("a (t p) d -> p (a t) d", p=P), x1[:, :, :])\
                    .then_inc(s["stored"], 16)
                sp.wait_ge(s["x2_ready"], i * 2 + 2)
                sp.dma_start(dr["x2"][bass.ds(i, 1)].rearrange("a (t p) d -> p (a t) d", p=P), x2[:, :, :])\
                    .then_inc(s["stored"], 16)
                sp.wait_ge(s["lg_ready"], i + 1)
                for c in range(2):
                    sp.dma_start(dr["logits"][c, bass.ds(i, 1)].rearrange("a g n -> (a g) n"),
                                 logit[G * c:G * c + G, :]).then_inc(s["stored"], 16)
            sp.wait_ge(s["stored"], NB * 64)

        @block.gpsimd
        def _(pool):
            pool.memset(va[:, :, :, :], 1.0).then_inc(s["setup_pool"], 1)
            pool.memset(eps, 1e-6)
            pool.memset(half[:, :], -0.5).then_inc(s["setup_pool"], 1)
            pool.wait_ge(s["loaded"], 80)
            pool.wait_ge(s["setup"], 2)
            pool.wait_ge(s["setup_pool"], 2)
            pool.tensor_tensor(nrm[:, 2:4], nrm[:, 0:2], half[:, 0:2], ALU.pow)\
                .then_inc(s["setup_pool"], 1)
            with pool.Fori(0, NB) as i:
                for r in range(2):
                    pool.wait_ge(s["squares"], i * 8 + 4 * r + 4)
                    pool.tensor_tensor(msn, ms, eps, ALU.add)\
                        .then_inc(s["inv_tmp"], 1)
                    pool.wait_ge(s["inv_tmp"], i * 2 + r + 1)
                    pool.tensor_tensor(inv, msn, half, ALU.pow).then_inc(s["inv_ready"], 1)
                pool.wait_ge(s["xm_ready"], i * 2 + 2)
                for k in range(NT):
                    pool.tensor_tensor(x_in[:, k, :], x_in[:, k, :], bo[:, :], ALU.add)\
                        .then_inc(s["pool_link"], 1)

        @block.scalar
        def _(act):
            act.wait_ge(s["loaded"], 80)
            act.wait_ge(s["setup_pool"], 2)
            with act.Fori(0, NB) as i:
                def inverse_norms(src, r):
                    for k in range(NT):
                        act.activation(hn[:, k, :], src[:, k, :], ACT.Square, scale=D ** -0.5,
                                       accum_out=ms[:, k:k + 1]).then_inc(s["squares"], 1)
                    act.wait_ge(s["inv_ready"], i * 2 + r + 1)
                    for k in range(NT):
                        act.activation(hn[:, k, :], src[:, k, :], ACT.Copy, scale=inv[:, k:k + 1])\
                            .then_inc(s["hn_ready"], 1)

                act.wait_ge(s["x_loaded"], i * 16 + 16)
                act.wait_ge(s["stored"], i * 64)
                inverse_norms(x_in, 0)
                for o in range(4):
                    act.wait_ge(s["qk_ps"], i * 4 + o + 1)
                    if o >= 2:
                        act.wait_ge(s["parts_stored"], i * 64 + 32)
                    act.activation(qk_hi[:, o % 2, :], bank(2 + o), ACT.Copy).then_inc(s["hi_ready"], 1)
                act.wait_ge(s["m_ps"], i + 1)
                act.activation(mrow[:, :], bank(0)[0:H, :], ACT.Copy).then_inc(s["mrow_ready"], 1)

                def heads_out(g):
                    act.wait_ge(s["pv_done"], i * 16 + 4 * g + 4)
                    if g >= 2:
                        act.wait_ge(s["oT_ready"], i * 4 + g - 1)
                    act.activation(osb[:, g % 2, :], bank(6 + g % 2), ACT.Copy)\
                        .then_inc(s["osb_ready"], 1)

                for step in range(16):
                    for c in range(2):
                        u = 2 * step + c
                        act.wait_ge(s["st_ps"], i * 32 + u + 1)
                        if step >= 2 and c == 0:
                            act.wait_ge(s["pv_done"], i * 16 + step - 1)
                        act.activation(p_t[:, step % 2, 2 * c:2 * c + 2, :],
                                       bank(2 * (u % 3), 2).rearrange("p (a n) -> p a n", a=2),
                                       ACT.Exp, scale=0.25).then_inc(s["exp_done"], 1)
                    if step % 4 == 1 and step > 4:
                        heads_out(step // 4 - 1)
                heads_out(3)
                act.wait_ge(s["xm_ready"], i * 2 + 2)
                inverse_norms(xm, 1)
                for m in range(NM):
                    act.wait_ge(s["gh_ps"], i * NM + m + 1)
                    if m >= 2:
                        act.wait_ge(s["tg2_ready"], i * NM + m - 1)
                    act.activation(tg[:, m % 2, :], bank(4 + 2 * (m % 2)), ACT.Tanh, scale=0.5)\
                        .then_inc(s["tg_ready"], 1)
                for d in range(ND):
                    act.wait_ge(s["yT_ps"], i * 2 + d + 1)
                    act.activation(hT[:, d, :], bank(2 + d), ACT.Copy).then_inc(s["yT_ready"], 1)
                act.wait_ge(s["lq_ps"], i + 1)
                for h in range(NLOC):
                    act.activation(lqm[:, h, :], bank(4), ACT.Copy, scale=const("hmask")[:, h:h + 1])\
                        .then_inc(s["lqm_ready"], 1)
                act.wait_ge(s["lk_ps"], i + 1)
                act.activation(lkT, bank(5), ACT.Copy).then_inc(s["lk_ready"], 1)
                act.wait_ge(s["qs_ready"], i + 1)
                act.activation(q_e, q_e, ACT.Exp).then_inc(s["qe_ready"], 1)
                act.wait_ge(s["kmin_ready"], i + 1)
                act.activation(k_e, k_e, ACT.Exp).then_inc(s["ke_ready"], 1)
                for h in range(NLOC):
                    act.wait_ge(s["lneg_ready"], i * NLOC + h + 1)
                    if h >= 2:
                        act.wait_ge(s["lt_ps"], i * NLOC + h - 1)
                    for u in range(NT):
                        c = NT * h + u
                        act.activation(lp[:, h % 2, u, :],
                                       bank(4 + 2 * (h % 2), 2)[:, 2 * P * u:2 * P * u + 2 * P],
                                       ACT.Exp, scale=0.25, bias=lneg[:, c:c + 1],
                                       accum_out=lden[:, c:c + 1]).then_inc(s["lexp"], 1)
                for a in range(2):
                    act.wait_ge(s["ql_ps"], i * 2 + a + 1)
                    act.activation(qlT[:, a, :], bank(a)[0:LW, :], ACT.Copy).then_inc(s["ql_ready"], 1)
                act.wait_ge(s["lo_ps"], i + 1)
                act.activation(locT[:, :], bank(4), ACT.Copy).then_inc(s["locT_ready"], 1)
                for d in range(ND):
                    act.wait_ge(s["x1T_ps"], i * 2 + d + 1)
                    act.activation(hT[:, d, :], bank(2 + d), ACT.Copy).then_inc(s["x1T_ready"], 1)
                for c in range(2):
                    act.wait_ge(s["x2_ps"], i * 2 + c + 1)
                    act.activation(x2[:, 2 * c:2 * c + 2, :],
                                   bank(4 + c).rearrange("p (a n) -> p a n", a=2), ACT.Copy)\
                        .then_inc(s["x2_ready"], 1)
                act.wait_ge(s["lg_ps"], i + 1)
                act.activation(logit[:, :], bank(6)[0:2 * G, :], ACT.Copy).then_inc(s["lg_ready"], 1)

        @block.tensor
        def _(pe):
            def transposes(src, base, ready):
                for d in range(ND):
                    for k in range(NT):
                        last = pe.transpose(bank(base + d)[:, k * P:(k + 1) * P],
                                            src[:, k, d * P:(d + 1) * P], ident)
                    last.then_inc(s[ready], 1)

            pe.wait_ge(s["loaded"], 80)
            for c in range(4 * ND):
                last = pe.matmul(bank(0)[:, c * NB:(c + 1) * NB], cw[:, c * P:(c + 1) * P],
                                 co[0:64, CO["cond"][0]:CO["cond"][1]], start=True, stop=True)
            last.then_inc(s["setup_pe"], 1)
            pe.wait_ge(s["setup"], 3)
            wr = const("wr").rearrange("p (k n) -> p k n", k=ND)
            for d in range(ND):
                for k in range(ND):
                    last = pe.matmul(bank(1)[:, d * 2 * G:(d + 1) * 2 * G],
                                     rot_t[:, k, :, :].rearrange("p i c -> p (i c)")[:, d * P:(d + 1) * P],
                                     wr[:, k, :], start=(k == 0), stop=(k == ND - 1))
            last.then_inc(s["setup_pe"], 1)
            pe.wait_ge(s["setup"], 5)
            with pe.Fori(0, NB) as i:
                pe.wait_ge(s["hn_ready"], i * 8 + 4)
                transposes(hn, 0, "hT_ps")
                pe.wait_ge(s["hT_ready"], i * 4 + 2)
                for o in range(4):
                    for k in range(ND):
                        last = pe.matmul(bank(2 + o), (wq, wk)[o // 2][:, k, (o % 2) * P:(o % 2 + 1) * P],
                                         hT[:, k, :], start=(k == 0), stop=(k == ND - 1))
                    last.then_inc(s["qk_ps"], 1)
                for c in range(2):
                    for b in range(2):
                        for k in range(ND):
                            last = pe.matmul(bank(6 + c)[:, b * D:(b + 1) * D],
                                             hT[:, k, (2 * c + b) * P:(2 * c + b + 1) * P], wv[:, k, :],
                                             start=(k == 0), stop=(k == ND - 1))
                    last.then_inc(s["v_ps"], 1)
                pe.wait_ge(s["stacked"], i * 128 + 128)
                pe.wait_ge(s["row_clear"], i * 16 + 16)
                pe.wait_ge(s["va_ready"], i * 2 + 2)
                for n in range(2 * H):
                    h, c = n // 2, n % 2
                    if n >= 4:
                        pe.wait_ge(s["smax"], i * 32 + n - 3)
                    for b in range(2):
                        last = pe.matmul(bank(2 * (n % 4) + b),
                                         stack_q[:, h, (2 * c + b) * P:(2 * c + b + 1) * P],
                                         stack_k[:, h, :], start=True, stop=True)
                    last.then_inc(s["s_ps"], 1)
                pe.wait_ge(s["smax"], i * 32 + 32)
                for k in range(NT):
                    last = pe.transpose(bank(0)[0:H, k * P:(k + 1) * P], mtok[:, k, :], ident)
                last.then_inc(s["m_ps"], 1)
                pe.wait_ge(s["mrow_back"], i * 16 + 16)

                def weigh(step):
                    g, kt = step // 4, step % 4
                    pe.wait_ge(s["exp_done"], i * 32 + 2 * step + 2)
                    if kt == 0 and g >= 2:
                        pe.wait_ge(s["oT_ready"], i * 4 + g - 1)
                    for j in range(4):
                        last = pe.matmul(bank(6 + g % 2)[STRIP * j:STRIP * (j + 1), :],
                                         va[:, kt, 4 * g + j, :], p_t[:, step % 2, j, :],
                                         start=(kt == 0), stop=(kt == NT - 1))
                    last.then_inc(s["pv_done"], 1)

                def sums(g):
                    pe.wait_ge(s["osb_ready"], i * 4 + g + 1)
                    for k in range(NT):
                        last = pe.matmul(bank(6 + g % 2)[:, 4 * k:4 * k + 4],
                                         osb[:, g % 2, k * P:(k + 1) * P], const("dsel"),
                                         start=True, stop=True)
                    last.then_inc(s["den_ps"], 1)

                def spread(g):
                    pe.wait_ge(s["rspread_ready"], i * 4 + g + 1)
                    for k in range(NT):
                        last = pe.matmul(bank(6 + g % 2)[:, k * P:(k + 1) * P],
                                         rspread[:, k * P:(k + 1) * P], ident, start=True, stop=True)
                    last.then_inc(s["rb_ps"], 1)

                for step in range(16):
                    g, kt = step // 4, step % 4
                    for c in range(2):
                        u = 2 * step + c
                        if u >= 3:
                            pe.wait_ge(s["exp_done"], i * 32 + u - 2)
                        for b in range(2):
                            h = 4 * g + 2 * c + b
                            last = pe.matmul(bank(2 * (u % 3) + b), stack_k[:, h, kt * P:(kt + 1) * P],
                                             stack_q[:, h, :], start=True, stop=True)
                        last.then_inc(s["st_ps"], 1)
                    if step:
                        weigh(step - 1)
                    if step % 4 == 2 and g:
                        sums(g - 1)
                    if step % 4 == 3 and g:
                        spread(g - 1)
                weigh(15)
                sums(3)
                spread(3)
                pe.wait_ge(s["oT_ready"], i * 4 + 4)
                for c in range(2):
                    for b in range(2):
                        k = 2 * c + b
                        for g in range(HG):
                            last = pe.matmul(bank(c)[:, b * D:(b + 1) * D],
                                             heads_t[:, g, k * P:(k + 1) * P], wo[:, g, :],
                                             start=(g == 0), stop=(g == HG - 1))
                    last.then_inc(s["ao_ps"], 1)
                pe.wait_ge(s["hn_ready"], i * 8 + 8)
                transposes(hn, 2, "hT_ps")
                pe.wait_ge(s["hT_ready"], i * 4 + 4)
                for m in range(NM):
                    if m >= 2:
                        pe.wait_ge(s["sg_done"], i * NM + m - 1)
                    for b, wt in enumerate((wgate, whid)):
                        for k in range(ND):
                            last = pe.matmul(bank(4 + 2 * (m % 2) + b), wt[:, k, m * P:(m + 1) * P],
                                             hT[:, k, :], start=(k == 0), stop=(k == ND - 1))
                    last.then_inc(s["gh_ps"], 1)
                pe.wait_ge(s["sg_done"], i * NM + NM)
                for c in range(2):
                    for b in range(2):
                        k = 2 * c + b
                        for m in range(NM):
                            last = pe.matmul(bank(c)[:, b * D:(b + 1) * D], gT[:, m, k * P:(k + 1) * P],
                                             wdown[:, m, :], start=(m == 0), stop=(m == NM - 1))
                    last.then_inc(s["dn_ps"], 1)
                pe.wait_ge(s["xc_ready"], i * 2 + 2)
                transposes(xc, 2, "yT_ps")
                pe.wait_ge(s["yT_ready"], i * 2 + 2)
                for o, (wt, ready) in enumerate(((blq, "lq_ps"), (blk, "lk_ps"))):
                    for k in range(ND):
                        last = pe.matmul(bank(4 + o), wt[:, k, :], hT[:, k, :],
                                         start=(k == 0), stop=(k == ND - 1))
                    last.then_inc(s[ready], 1)
                for b in range(NT):
                    for k in range(ND):
                        last = pe.matmul(bank(b)[:, 0:2 * NLIN * DH], hT[:, k, b * P:(b + 1) * P],
                                         blin[:, k, :], start=(k == 0), stop=(k == ND - 1))
                last.then_inc(s["lin_ps"], 1)
                for c in range(2):
                    for b in range(2):
                        for k in range(ND):
                            last = pe.matmul(bank(6 + c)[:, b * D:(b + 1) * D],
                                             hT[:, k, (2 * c + b) * P:(2 * c + b + 1) * P], bwv[:, k, :],
                                             start=(k == 0), stop=(k == ND - 1))
                    last.then_inc(s["lv_ps"], 1)

                def local_scores(h):
                    if h >= 2:
                        pe.wait_ge(s["lt_ready"], i * NLOC + h - 1)
                    for u in range(NT):
                        out = bank(4 + 2 * (h % 2), 2)[:, 2 * P * u:2 * P * (u + 1)]
                        q = lqm[:, h, u * P:(u + 1) * P]
                        if u:
                            pe.matmul(out, q, lkT[:, (u - 1) * P:(u + 1) * P], start=True, stop=False)
                            last = pe.matmul(out[:, P:], ident_b[:, :], causal_b[:, :],
                                             start=False, stop=True)
                        else:
                            pe.matmul(out[:, 0:P], ident_b[:, :], all_b[:, :], start=True, stop=True)
                            pe.matmul(out[:, P:], q, lkT[:, 0:P], start=True, stop=False)
                            last = pe.matmul(out[:, P:], ident_b[:, :], causal_b[:, :],
                                             start=False, stop=True)
                    last.then_inc(s["ls_ps"], 1)

                def local_transposes(h):
                    pe.wait_ge(s["lnorm"], i * 16 + 4 * h + 4)
                    for u in range(NT):
                        for c in range(2):
                            last = pe.transpose(bank(4 + 2 * (h % 2), 2)[:, (2 * u + c) * P:(2 * u + c + 1) * P],
                                                lp[:, h % 2, u, c * P:(c + 1) * P], ident)
                    last.then_inc(s["lt_ps"], 1)

                pe.wait_ge(s["lqm_ready"], i * NLOC + NLOC)
                pe.wait_ge(s["lk_ready"], i + 1)
                local_scores(0)
                pe.wait_ge(s["lv_ready"], i * 2 + 2)
                local_scores(1)
                pe.wait_ge(s["kk_ready"], i + 1)
                for u in range(NU):
                    for a in range(2):
                        r = BLK * (u % 2)
                        c = (2 * (u // 2 % 2) + a) * LH * CW
                        last = pe.matmul(bank(2 * (u % 2) + u // 4)[0:LW, c:c + LH * CW],
                                         kk[r:r + BLK, u // 2, a * LW:(a + 1) * LW],
                                         va[r:r + BLK, u // 2, NLOC + LH * a:NLOC + LH * (a + 1), 0:CW],
                                         start=True, stop=True)
                last.then_inc(s["ctx_ps"], 1)
                local_transposes(0)
                local_scores(2)
                local_transposes(1)
                local_scores(3)
                pe.wait_ge(s["qn_ready"], i + 1)
                pe.wait_ge(s["ctx_ready"], i + 1)
                for a in range(2):
                    for k in range(NT):
                        last = pe.transpose(bank(a)[0:LW, k * P:(k + 1) * P],
                                            q_n[:, k, a * LW:(a + 1) * LW], ident)
                    last.then_inc(s["ql_ps"], 1)
                local_transposes(2)
                local_transposes(3)
                pe.wait_ge(s["ql_ready"], i * 2 + 2)
                for a in range(2):
                    for u in range(NU):
                        last = pe.matmul(bank(2 + a)[0:LW, BLK * (u + 1):BLK * (u + 2)],
                                         ctxn[:, 2 * u + a, :], qlT[:, a, BLK * (u + 1):BLK * (u + 2)],
                                         start=True, stop=True)
                    last.then_inc(s["lin_out_ps"], 1)
                pe.wait_ge(s["lt_ready"], i * NLOC + NLOC)
                for u in range(NT):
                    for c in ((0, 1) if u else (1,)):
                        for h in range(NLOC):
                            last = pe.matmul(bank(4)[STRIP * h:STRIP * (h + 1), u * P:(u + 1) * P],
                                             va[:, u - 1 + c, h, :], lpT[:, h, u, c, :],
                                             start=(c == 0 or u == 0), stop=(c == 1))
                last.then_inc(s["lo_ps"], 1)
                pe.wait_ge(s["linT_ready"], i * 2 + 2)
                pe.wait_ge(s["locT_ready"], i + 1)
                for c in range(2):
                    for b in range(2):
                        k = 2 * c + b
                        out = bank(c)[:, b * D:(b + 1) * D]
                        pe.matmul(out, locT[:, k * P:(k + 1) * P], bwo_loc, start=True, stop=False)
                        pe.matmul(out, linT[:, 0, k * P:(k + 1) * P], bwo_lin[0:LW, 0, :],
                                  start=False, stop=False)
                        last = pe.matmul(out, linT[:, 1, k * P:(k + 1) * P], bwo_lin[0:LW, 1, :],
                                         start=False, stop=True)
                    last.then_inc(s["y_ps"], 1)
                pe.wait_ge(s["x1_ready"], i * 2 + 2)
                transposes(x1, 2, "x1T_ps")
                pe.wait_ge(s["x1T_ready"], i * 2 + 2)
                for c in range(2):
                    for b in range(2):
                        k = 2 * c + b
                        for d in range(ND):
                            last = pe.matmul(bank(4 + c)[:, b * D:(b + 1) * D], hT[:, d, k * P:(k + 1) * P],
                                             rot[:, d, :, :].rearrange("p i c -> p (i c)"),
                                             start=(d == 0), stop=(d == ND - 1))
                    last.then_inc(s["x2_ps"], 1)
                for d in range(ND):
                    last = pe.matmul(bank(6)[0:2 * G, :], wc[:, d, :], hT[:, d, :],
                                     start=(d == 0), stop=(d == ND - 1))
                last.then_inc(s["lg_ps"], 1)

        @block.vector
        def _(dve):
            n_link = [0]

            def link(ins):
                n_link[0] += 1
                ins.then_inc(s["link"], 1)
                dve.wait_ge(s["link"], n_link[0])

            dve.memset(mrow[:, :].bitcast(F32), 0.0).then_inc(s["cleared"], 1)
            for st in (stack_q, stack_k):
                dve.memset(st[SROW:KST, :, :].bitcast(F32), 0.0).then_inc(s["cleared"], 1)
            link(dve.memset(small[:, 0:64], 0.0))
            dve.wait_ge(s["cleared"], 3)
            dve.memset(stack_k[SROW:SROW + 1, :, :].bitcast(F32), -1.0).then_inc(s["cleared"], 1)
            dve.wait_ge(s["loaded"], 80)
            ql, qr = const("qleft"), const("qright")
            link(dve.tensor_tensor(temp[:, 0:NB], ql, ql, ALU.mult))
            link(dve.tensor_tensor(temp[:, NB:NB + 4], qr, qr, ALU.mult))
            link(dve.tensor_reduce(nrm[:, 0:1], temp[:, 0:NB], AX, ALU.add))
            link(dve.tensor_reduce(nrm[:, 1:2], temp[:, NB:NB + 4], AX, ALU.add))
            dve.tensor_scalar(nrm[:, 0:1], nrm[:, 0:1], 1e-8, None, ALU.add).then_inc(s["setup"], 1)
            dve.tensor_scalar(nrm[:, 1:2], nrm[:, 1:2], 1e-8, None, ALU.add).then_inc(s["setup"], 1)
            dve.wait_ge(s["setup_pool"], 3)
            link(dve.tensor_scalar(lrot, ql[:, 0:4], nrm[:, 2:3], None, ALU.mult))
            link(dve.tensor_scalar(rrot, qr, nrm[:, 3:4], const("sg"), ALU.mult, ALU.mult))
            link(dve.tensor_tensor(rrot, rrot, const("sign"), ALU.mult))
            w_, x_, y_, z_ = range(4)
            left = (((w_, 1), (x_, -1), (y_, -1), (z_, -1)), ((x_, 1), (w_, 1), (z_, -1), (y_, 1)),
                    ((y_, 1), (z_, 1), (w_, 1), (x_, -1)), ((z_, 1), (y_, -1), (x_, 1), (w_, 1)))
            right = (((w_, 1), (x_, -1), (y_, -1), (z_, -1)), ((x_, 1), (w_, 1), (z_, 1), (y_, -1)),
                     ((y_, 1), (z_, -1), (w_, 1), (x_, 1)), ((z_, 1), (y_, 1), (x_, -1), (w_, 1)))
            for m, (table, src) in enumerate(((left, lrot), (right, rrot))):
                for a in range(4):
                    for b in range(4):
                        q, sgn = table[a][b]
                        last = dve.tensor_scalar(coef[:, m, a, b:b + 1], src[:, q:q + 1], float(sgn), None, ALU.mult)
            link(last)
            for k in range(4):
                o = coef[:, 2 if k == 0 else 3, :, :]
                link(dve.tensor_tensor(o, coef[:, 0, :, k:k + 1].to_broadcast([P, 4, 4]),
                                       coef[:, 1, k:k + 1, :].to_broadcast([P, 4, 4]), ALU.mult))
                if k:
                    link(dve.tensor_tensor(coef[:, 2, :, :], coef[:, 2, :, :], coef[:, 3, :, :], ALU.add))
            for k in range(ND):
                for hh in range(2):
                    p = slice(64 * hh, 64 * hh + 64)
                    j = 2 * k + hh
                    cm = co[p, CO["cmask"][0]:CO["cmask"][1]]
                    for o in range(4):
                        dve.tensor_scalar(rot[p, k, o, :], cm, coef[p, 2, o, j:j + 1], None, ALU.mult)
                        last = dve.tensor_scalar(rot_t[p, k, o, :], cm, coef[p, 2, j, o:o + 1], None, ALU.mult)
            last.then_inc(s["setup"], 1)
            dve.wait_ge(s["setup_pe"], 1)
            link(dve.tensor_tensor(gb, bank(0)[:, 0:4 * ND * NB].rearrange("p (k b) -> p k b", b=NB),
                                   const("cb")[:, :, None].to_broadcast([P, 4 * ND, NB]), ALU.add))
            dve.wait_ge(s["setup_pe"], 2)
            dve.tensor_copy(wc[:, :, :], bank(1)[:, 0:4 * G].rearrange("p (k n) -> p k n", k=ND))\
                .then_inc(s["setup"], 1)
            link(dve.tensor_copy(kmask[:, :, :], co[0:LW, None, CO["bmask"][0]:CO["bmask"][1]]
                                 .to_broadcast([LW, 2 * NU, LH])))
            dve.tensor_copy(causal_b[:, :], const("causal"))
            dve.tensor_copy(all_b[:, :], const("all"))
            dve.tensor_copy(ident_b[:, :], ident).then_inc(s["setup"], 1)
            n0 = n_link[0]
            LINKS = 23
            with dve.Fori(0, NB) as i:
                at = [0]

                def link(ins):
                    at[0] += 1
                    ins.then_inc(s["link"], 1)
                    dve.wait_ge(s["link"], i * LINKS + n0 + at[0])

                link(dve.tensor_copy(gbc[:, :], gb[:, :, bass.ds(i, 1)].rearrange("p k b -> p (k b)")))

                def scale_shift(base, r):
                    for d in range(ND):
                        dve.wait_ge(s["hT_ps"], i * 4 + 2 * r + d + 1)
                        dve.tensor_scalar(hT[:, d, :], bank(base + d), gbc[:, 4 * r + d:4 * r + d + 1],
                                          gbc[:, 4 * r + 2 + d:4 * r + 3 + d], ALU.mult, ALU.add)\
                            .then_inc(s["hT_ready"], 1)

                def values(base, ps_sem, ready, r):
                    for c in range(2):
                        dve.wait_ge(s[ps_sem], i * 2 + c + 1)
                        dve.tensor_copy(va[:, 2 * c:2 * c + 2, :, 0:DH],
                                        bank(base + c).rearrange("p (t h d) -> p t h d", t=2, h=H))\
                            .then_inc(s[ready], 1)

                scale_shift(0, 0)
                for o in range(4):
                    dve.wait_ge(s["hi_ready"], i * 4 + o + 1)
                    if o == 2:
                        dve.wait_ge(s["parts_stored"], i * 64 + 32)
                    dve.tensor_tensor(qk_lo[:, o % 2, :], bank(2 + o), qk_hi[:, o % 2, :].bitcast(F32),
                                      ALU.subtract).then_inc(s["lo_ready"], 1)
                values(6, "v_ps", "va_ready", 0)
                for n in range(2 * H):
                    dve.wait_ge(s["s_ps"], i * 32 + n + 1)
                    dve.tensor_reduce(mtok[:, 2 * (n % 2):2 * (n % 2) + 2, n // 2],
                                      bank(2 * (n % 4), 2).rearrange("p (a n) -> p a n", a=2), AX, ALU.max)\
                        .then_inc(s["smax"], 1)
                for g in range(HG):
                    dve.wait_ge(s["den_ps"], i * 4 + g + 1)
                    dve.reciprocal(rden, bank(6 + g % 2)[:, 0:16]).then_inc(s["rden_ready"], 1)
                    dve.wait_ge(s["rden_ready"], i * 4 + g + 1)
                    dve.tensor_copy(rspread.rearrange("p (c n) -> p c n", n=STRIP),
                                    rden[:, :, None].to_broadcast([P, 16, STRIP])).then_inc(s["rspread_ready"], 1)
                    dve.wait_ge(s["rb_ps"], i * 4 + g + 1)
                    dve.tensor_tensor(heads_t[:, g, :], osb[:, g % 2, :], bank(6 + g % 2), ALU.mult)\
                        .then_inc(s["oT_ready"], 1)
                for c in range(2):
                    dve.wait_ge(s["ao_ps"], i * 2 + c + 1)
                    dve.tensor_tensor(xm[:, 2 * c:2 * c + 2, :], x_in[:, 2 * c:2 * c + 2, :],
                                      bank(c).rearrange("p (a n) -> p a n", a=2), ALU.add)\
                        .then_inc(s["xm_ready"], 1)
                scale_shift(2, 1)
                for m in range(NM):
                    dve.wait_ge(s["tg_ready"], i * NM + m + 1)
                    if m >= 2:
                        dve.wait_ge(s["sg_done"], i * NM + m - 1)
                    dve.scalar_tensor_tensor(tg2[:, m % 2, :], tg[:, m % 2, :], 1.0, bank(4 + 2 * (m % 2)),
                                             ALU.add, ALU.mult).then_inc(s["tg2_ready"], 1)
                    dve.wait_ge(s["tg2_ready"], i * NM + m + 1)
                    dve.scalar_tensor_tensor(gT[:, m, :], tg2[:, m % 2, :], 0.5, bank(5 + 2 * (m % 2)),
                                             ALU.mult, ALU.mult).then_inc(s["sg_done"], 1)
                for c in range(2):
                    dve.wait_ge(s["dn_ps"], i * 2 + c + 1)
                    dve.tensor_tensor(xc[:, 2 * c:2 * c + 2, :], xm[:, 2 * c:2 * c + 2, :],
                                      bank(c).rearrange("p (a n) -> p a n", a=2), ALU.add)\
                        .then_inc(s["xc_ready"], 1)
                dve.wait_ge(s["lin_ps"], i + 1)
                flat = bank(0, 4).rearrange("p (t n) -> p t n", t=NT)
                q_ps = flat[:, :, 0:NLIN * DH].rearrange("p t (h d) -> p t h d", d=DH)
                q4 = q_e.rearrange("p t (h d) -> p t h d", d=DH)
                qn4 = q_n.rearrange("p t (h d) -> p t h d", d=DH)
                m4 = qmx.rearrange("p (t h) -> p t h", t=NT)
                link(dve.tensor_reduce(m4, q_ps, AX, ALU.max))
                dve.tensor_tensor(q4, q_ps, m4[:, :, :, None].to_broadcast([P, NT, NLIN, DH]),
                                  ALU.subtract).then_inc(s["qs_ready"], 1)
                dve.tensor_scalar(k_e, flat[:, :, NLIN * DH:2 * NLIN * DH], 0.0, None, ALU.min)\
                    .then_inc(s["kmin_ready"], 1)
                values(6, "lv_ps", "lv_ready", 1)
                dve.wait_ge(s["ke_ready"], i + 1)
                dve.scalar_tensor_tensor(kk[:, :, :], flat[:, :, NLIN * DH:2 * NLIN * DH], 0.0, k_e,
                                         ALU.max, ALU.add).then_inc(s["kk_ready"], 1)
                dve.wait_ge(s["qe_ready"], i + 1)
                link(dve.tensor_reduce(qsum, q4, AX, ALU.add))
                link(dve.reciprocal(qrec, qsum))
                dve.tensor_tensor(qn4, q4, qrec.rearrange("p (t h) -> p t h", t=NT)[:, :, :, None]
                                  .to_broadcast([P, NT, NLIN, DH]), ALU.mult).then_inc(s["qn_ready"], 1)

                def local_max(h):
                    dve.wait_ge(s["ls_ps"], i * NLOC + h + 1)
                    c = slice(NT * h, NT * h + NT)
                    link(dve.tensor_reduce(lmax[:, c], bank(4 + 2 * (h % 2), 2)
                                           .rearrange("p (u n) -> p u n", u=NT), AX, ALU.max))
                    dve.tensor_scalar(lneg[:, c], lmax[:, c], -0.25, None, ALU.mult)\
                        .then_inc(s["lneg_ready"], 1)

                def local_norm(h):
                    dve.wait_ge(s["lexp"], i * 16 + 4 * h + 4)
                    link(dve.reciprocal(lrec[:, NT * h:NT * h + NT], lden[:, NT * h:NT * h + NT]))
                    for u in range(NT):
                        dve.tensor_scalar(lp[:, h % 2, u, :], lp[:, h % 2, u, :],
                                          lrec[:, NT * h + u:NT * h + u + 1], None, ALU.mult)\
                            .then_inc(s["lnorm"], 1)

                def local_back(h):
                    dve.wait_ge(s["lt_ps"], i * NLOC + h + 1)
                    dve.tensor_copy(lpT[:, h, :, :, :], bank(4 + 2 * (h % 2), 2)
                                    .rearrange("p (u c n) -> p u c n", u=NT, c=2)).then_inc(s["lt_ready"], 1)

                local_max(0)
                local_max(1)
                local_norm(0)
                dve.wait_ge(s["ctx_ps"], i + 1)
                cw_ = 2 * LH * CW
                for u in range(NU):
                    src = bank(2 * (u % 2) + u // 4)[0:LW, (u // 2 % 2) * cw_:(u // 2 % 2 + 1) * cw_]
                    if u:
                        link(dve.tensor_tensor(cum[:, u, :], src, cum[:, u - 1, :], ALU.add))
                    else:
                        link(dve.tensor_copy(cum[:, 0, :], src))
                cum5 = cum.rearrange("p u (a h c) -> p (u a) h c", a=2, h=LH)
                link(dve.tensor_scalar(ks, cum5[:, :, 0, DH], 1e-6, None, ALU.add))
                link(dve.reciprocal(krec, ks))
                link(dve.tensor_tensor(kmask2[:, :, :], kmask[:, :, :],
                                       krec[:, :, None].to_broadcast([LW, 2 * NU, LH]), ALU.mult))
                dve.tensor_tensor(ctxn.rearrange("p v (h c) -> p v h c", h=LH), cum5[:, :, :, 0:DH],
                                  kmask2[:, :, :, None].to_broadcast([LW, 2 * NU, LH, DH]),
                                  ALU.mult).then_inc(s["ctx_ready"], 1)
                local_back(0)
                local_norm(1)
                local_max(2)
                local_back(1)
                local_norm(2)
                local_max(3)
                local_norm(3)
                local_back(2)
                local_back(3)
                link(dve.memset(hT[0:LW, :, 0:BLK], 0.0))
                for a in range(2):
                    dve.wait_ge(s["lin_out_ps"], i * 2 + a + 1)
                    dve.tensor_copy(linT[:, a, BLK:], bank(2 + a)[0:LW, BLK:]).then_inc(s["linT_ready"], 1)
                dve.wait_ge(s["pool_link"], i * NT + NT)
                for c in range(2):
                    dve.wait_ge(s["y_ps"], i * 2 + c + 1)
                    dve.tensor_tensor(x1[:, 2 * c:2 * c + 2, :], x_in[:, 2 * c:2 * c + 2, :],
                                      bank(c).rearrange("p (a n) -> p a n", a=2), ALU.add)\
                        .then_inc(s["x1_ready"], 1)
                assert at[0] == LINKS, at[0]


def phase_route(nc, t, dr):
    R = 2 * NB * G
    RQ = NB * G
    with ExitStack() as ctx:
        def sb(name, shape, dt=F32):
            return ctx.enter_context(nc.sbuf_tensor(name, shape, dt))

        def sem(name):
            return ctx.enter_context(nc.semaphore(name))

        ps, co, cr, place = t["ps"], t["co"], t["cr"], t["place"]

        def const(name):
            if name in CR:
                return cr[:, CR[name][0]:CR[name][1]]
            return co[:, CO[name][0]:CO[name][1]]

        def bank(k):
            return ps[:, k * BANK:(k + 1) * BANK]

        ident = const("ident")
        logits = sb("logits", [R, L])
        left = sb("left", [R, L])
        top = sb("top", [R, NQ // 8, 8])
        limit = sb("limit", [R, 1])
        above = sb("above", [R, L])
        equal = sb("equal", [R, L])
        both = sb("both", [P, 2, NT, R])
        need = sb("need", [P, R])
        pick = sb("pick", [P, NT, R])
        rows = sb("rows", [R, L])

        loaded, vec, flags_ps, both_ready, count_ps, pick_ready, order_ps, place_ready, rows_ps, \
            rows_ready, stored = (sem(n) for n in (
                "r_loaded", "r_vec", "r_flags_ps", "r_both", "r_count_ps", "r_pick", "r_order_ps",
                "r_place", "r_rows_ps", "r_rows", "r_stored"))

        block = ctx.enter_context(nc.Block())

        @block.sync
        def _(sp):
            for c in range(2):
                sp.dma_start(logits[RQ * c:RQ * c + RQ, :], dr["logits"][c].rearrange("b g n -> (b g) n"))\
                    .then_inc(loaded, 16)
            sp.dma_start(cr[:, :], dr["cr"]).then_inc(loaded, 16)
            sp.wait_ge(rows_ready, 1)
            sp.dma_start(dr["place"], rows[0:RQ, :]).then_inc(stored, 16)
            sp.wait_ge(stored, 16)

        @block.vector
        def _(dve):
            n = [0]

            def link(ins):
                n[0] += 1
                ins.then_inc(vec, 1)
                dve.wait_ge(vec, n[0])

            dve.wait_ge(loaded, 48)
            link(dve.tensor_copy(left[:, :], logits[:, :]))
            for k in range(NQ // 8):
                r = R if k < NK // 8 else RQ
                link(dve.max(top[0:r, k, :], left[0:r, :]))
                if k < NQ // 8 - 1:
                    link(dve.match_replace(left[0:r, :], top[0:r, k, :], left[0:r, :], -3.0e38))
            dve.tensor_copy(limit[0:RQ, :], top[0:RQ, NQ // 8 - 1, 7:8])
            link(dve.tensor_copy(limit[RQ:R, :], top[RQ:R, NK // 8 - 1, 7:8]))
            link(dve.tensor_scalar(above[:, :], logits[:, :], limit[:, 0:1], None, ALU.is_gt))
            link(dve.tensor_scalar(equal[:, :], logits[:, :], limit[:, 0:1], None, ALU.is_equal))
            dve.wait_ge(flags_ps, 1)
            dve.tensor_copy(both[:, :, :, :], bank(0)[:, 0:2 * NT * R].rearrange("p (a t r) -> p a t r", a=2, t=NT))\
                .then_inc(both_ready, 1)
            dve.wait_ge(count_ps, 1)
            link(dve.tensor_tensor(need[:, :], const("kvec"), bank(1)[:, 0:R], ALU.subtract))
            link(dve.tensor_tensor(pick[:, :, :], bank(2)[:, 0:NT * R].rearrange("p (t r) -> p t r", t=NT),
                                   need[:, None, :].to_broadcast([P, NT, R]), ALU.is_lt))
            link(dve.tensor_tensor(pick[:, :, :], pick[:, :, :], both[:, 1, :, :], ALU.mult))
            dve.tensor_tensor(pick[:, :, :], pick[:, :, :], both[:, 0, :, :], ALU.add).then_inc(pick_ready, 1)
            dve.wait_ge(order_ps, 1)
            link(dve.scalar_tensor_tensor(place[:, :, :], bank(3)[:, 0:NT * R].rearrange("p (t r) -> p t r", t=NT),
                                          1.0, pick[:, :, :], ALU.add, ALU.mult))
            dve.tensor_scalar(place[:, :, :], place[:, :, :], 1.0, None, ALU.subtract).then_inc(place_ready, 1)
            dve.wait_ge(rows_ps, 1)
            dve.tensor_copy(rows[:, :], bank(4)[0:R, :]).then_inc(rows_ready, 1)

        @block.tensor
        def _(pe):
            pe.wait_ge(vec, 1 + 2 * (NQ // 8) - 1 + 3)
            for a, src in enumerate((above, equal)):
                for k in range(NT):
                    c = (a * NT + k) * R
                    last = pe.transpose(bank(0)[:, c:c + R], src[:, k * P:(k + 1) * P], ident[0:R, 0:R])
            last.then_inc(flags_ps, 1)

            def before(out, src):
                for k in range(NT):
                    for m in range(k + 1):
                        last = pe.matmul(out[:, k * R:(k + 1) * R], const("ones") if m < k else const("before"),
                                         src(m), start=(m == 0), stop=(m == k))
                return last

            pe.wait_ge(both_ready, 1)
            for k in range(NT):
                pe.matmul(bank(1)[:, 0:R], const("ones"), both[:, 0, k, :], start=(k == 0), stop=(k == NT - 1))
            before(bank(2), lambda m: both[:, 1, m, :]).then_inc(count_ps, 1)
            pe.wait_ge(pick_ready, 1)
            before(bank(3), lambda m: pick[:, m, :]).then_inc(order_ps, 1)
            pe.wait_ge(place_ready, 1)
            for k in range(NT):
                last = pe.transpose(bank(4)[0:R, k * P:(k + 1) * P], place[:, k, :], ident)
            last.then_inc(rows_ps, 1)


def phase_routed(nc, t, dr):
    with ExitStack() as ctx:
        def sb(name, shape, dt=F32):
            return ctx.enter_context(nc.sbuf_tensor(name, shape, dt))

        def sem(name):
            return ctx.enter_context(nc.semaphore(name))

        ps, co, cr, place = t["ps"], t["co"], t["cr"], t["place"]

        def const(name):
            if name in CR:
                return cr[:, CR[name][0]:CR[name][1]]
            return co[:, CO[name][0]:CO[name][1]]

        def bank(k, n=1):
            return ps[:, k * BANK:(k + n) * BANK]

        ident = const("ident")
        wr = const("wr").rearrange("p (k n) -> p k n", k=ND)
        W2 = NQ + NK
        wall = sb("wall", [P, G, WC_N])
        nvw = sb("nvw", [FH, G, D])
        x1 = sb("c_x1", [P, NT, D])
        x2 = sb("c_x2", [P, NT, D])
        outs = sb("outs", [P, NT, D])
        null = sb("null", [P, D])
        prow = sb("prow", [P, G, L])
        pl = sb("pl", [P, NT, 2, G])
        hot = sb("hot", [P, NT, W2])
        xg = sb("xg", [P, ND, W2])
        score = sb("score", [P, 4])
        qT = sb("qT", [P, NE, NQ])
        kT = sb("kT", [P, NE, 2, NK + 1])
        v = sb("v", [P, E])
        p = sb("p", [P, 2, FH, NK + 1])
        pT = sb("pT", [P, FH, NQ])
        pnT = sb("pnT", [FH, NQ])
        oT = sb("oT", [P, NE, NQ])
        oq = sb("oq", [P, 2, D])
        hot_t = sb("hot_t", [P, 2, L])
        fmax = sb("fmax", [P, 16])
        fneg = sb("fneg", [P, 16])
        fden = sb("fden", [P, 16])
        frec = sb("frec", [P, 16])
        seen = sb("seen", [P, NT, G])
        cnt = sb("cnt", [P, 4, NT])

        def wg(g, name, k):
            a, b = WC[name]
            return wall[:, g, a:b].rearrange("p (k n) -> p k n", k=k)

        s = {n: sem("c_" + n) for n in (
            "loaded", "x1_loaded", "kT_clear", "nvw_ps", "nvw_ready", "x_loaded", "place_back", "pl_ready", "hot",
            "xg_ps", "xg_ready", "score_ps", "tanh_ready", "score_ready", "q_ps", "k_ps", "v_ps",
            "qT_ready", "kT_ready", "v_ready", "s_ps", "fmax_link", "fneg_ready", "exp_done",
            "frec_link", "p_ready", "pT_ps", "pT_ready", "pn_ps", "pn_ready", "o_ps", "oT_ready",
            "out_ps", "oq_ready", "hot_t", "sum_ps", "cnt_link", "cnt_ready", "fin_link", "fin",
            "stored", "nk_ready")}

        block = ctx.enter_context(nc.Block())

        @block.sync
        def _(sp):
            for g in range(G):
                sp.dma_start(wall[:, g, :], dr["wc"][g]).then_inc(s["loaded"], 16)
            sp.dma_start(null[:, :], dr["null"].to_broadcast([P, D])).then_inc(s["loaded"], 16)
            with sp.Fori(0, NB) as i:
                sp.wait_ge(s["sum_ps"], i * G)
                sp.dma_start(x2[:, :, :], dr["x2"][bass.ds(i, 1)].rearrange("a (t p) d -> p (a t) d", p=P))\
                    .then_inc(s["x_loaded"], 16)
                sp.wait_ge(s["hot_t"], i * 2 * G)
                sp.dma_start(prow[:, :, :], dr["place"].rearrange("(b g) n -> b g n", b=NB)[bass.ds(i, 1)]
                             .to_broadcast([P, G, L])).then_inc(s["place_back"], 16)
                sp.wait_ge(s["fin"], i * NT)
                sp.dma_start(x1[:, :, :], dr["x1"][bass.ds(i, 1)].rearrange("a (t p) d -> p (a t) d", p=P))\
                    .then_inc(s["x1_loaded"], 16)
                sp.wait_ge(s["fin"], i * NT + NT)
                sp.dma_start(dr["out"][bass.ds(i, 1)].rearrange("a (t p) d -> p (a t) d", p=P), outs[:, :, :])\
                    .then_inc(s["stored"], 16)
            sp.wait_ge(s["stored"], NB * 16)

        @block.gpsimd
        def _(pool):
            pool.memset(kT[:, :, :, :], 0.0).then_inc(s["kT_clear"], 1)
            pool.wait_ge(s["kT_clear"], 1)
            pool.wait_ge(s["loaded"], 80)
            with pool.Fori(0, NB) as i:
                for g in range(G):
                    for c in range(2):
                        pool.wait_ge(s["frec_link"], i * 2 * G + 2 * g + c + 1)
                        pool.tensor_tensor(p[:, c, :, :], p[:, c, :, :],
                                           frec[:, FH * c:FH * c + FH, None].to_broadcast([P, FH, NK + 1]),
                                           ALU.mult).then_inc(s["p_ready"], 1)

        @block.scalar
        def _(act):
            act.wait_ge(s["nvw_ps"], 1)
            act.activation(nvw[:, :, :], bank(0, 2)[0:FH, :].rearrange("p (g n) -> p g n", g=G), ACT.Copy)\
                .then_inc(s["nvw_ready"], 1)
            act.wait_ge(s["kT_clear"], 1)
            act.wait_ge(s["loaded"], 80)
            with act.Fori(0, NB) as i:
                for g in range(G):
                    n = i * G + g
                    act.wait_ge(s["s_ps"], n * 4)
                    for hh in range(2):
                        r = slice(64 * hh, 64 * hh + 64)
                        act.activation(kT[r, :, hh, NK:NK + 1], wg(g, "nk", NE)[r, :, :], ACT.Copy)\
                            .then_inc(s["nk_ready"], 1)
                    for d in range(ND):
                        act.wait_ge(s["xg_ps"], n * ND + d + 1)
                        act.activation(xg[:, d, :], bank(d)[:, 0:W2], ACT.Copy).then_inc(s["xg_ready"], 1)
                    act.wait_ge(s["score_ps"], n + 1)
                    act.wait_ge(s["oq_ready"], n * 2)
                    act.activation(score[:, 0:3], bank(0)[:, 0:3], ACT.Tanh, scale=0.5)\
                        .then_inc(s["tanh_ready"], 1)
                    for c in range(2):
                        act.wait_ge(s["q_ps"], n * 2 + c + 1)
                        act.activation(qT[:, 2 * c:2 * c + 2, :], bank(2 + c).rearrange("p (a n) -> p a n", a=2),
                                       ACT.Copy).then_inc(s["qT_ready"], 1)
                    act.wait_ge(s["score_ready"], n + 1)
                    act.wait_ge(s["v_ps"], n + 1)
                    act.activation(v[:, :], bank(5), ACT.Copy, scale=score[:, 2:3]).then_inc(s["v_ready"], 1)
                    for u in range(4):
                        act.wait_ge(s["fneg_ready"], n * 4 + u + 1)
                        for a in range(4):
                            h = 4 * (u % 2) + a
                            c = 4 * u + a
                            act.activation(p[:, u // 2, h, :],
                                           bank(2 * (u % 3) + a // 2)[:, (a % 2) * (NK + 1):(a % 2 + 1) * (NK + 1)],
                                           ACT.Exp, scale=FD ** -0.5, bias=fneg[:, c:c + 1],
                                           accum_out=fden[:, c:c + 1]).then_inc(s["exp_done"], 1)
                    act.wait_ge(s["pn_ps"], n + 1)
                    act.activation(pnT[:, :], bank(0)[0:FH, 0:NQ], ACT.Copy).then_inc(s["pn_ready"], 1)
                    for c in range(2):
                        act.wait_ge(s["o_ps"], n * 2 + c + 1)
                        act.activation(oT[:, 2 * c:2 * c + 2, :], bank(c).rearrange("p (a n) -> p a n", a=2),
                                       ACT.Copy).then_inc(s["oT_ready"], 1)

        @block.tensor
        def _(pe):
            pe.wait_ge(s["loaded"], 80)
            for g in range(G):
                for e in range(NE):
                    last = pe.matmul(bank(g // 2)[0:FH, (g % 2) * D:(g % 2 + 1) * D], wg(g, "nv", NE)[:, e, :],
                                     wg(g, "wo", NE)[:, e, :], start=(e == 0), stop=(e == NE - 1))
            last.then_inc(s["nvw_ps"], 1)
            pe.wait_ge(s["nvw_ready"], 1)
            with pe.Fori(0, NB) as i:
                for g in range(G):
                    n = i * G + g
                    if g == 0:
                        pe.wait_ge(s["x_loaded"], i * 16 + 16)
                    pe.wait_ge(s["hot"], (n + 1) * 8)
                    for d in range(ND):
                        for k in range(NT):
                            last = pe.matmul(bank(d)[:, 0:W2], x2[:, k, d * P:(d + 1) * P], hot[:, k, :],
                                             start=(k == 0), stop=(k == NT - 1))
                        last.then_inc(s["xg_ps"], 1)
                    pe.wait_ge(s["xg_ready"], n * 2 + 2)
                    for c in range(3):
                        r = g if c < 2 else G + g
                        for d in range(ND):
                            last = pe.matmul(bank(0)[:, c:c + 1], xg[:, d, c * P:(c + 1) * P],
                                             wr[:, d, r:r + 1], start=(d == 0), stop=(d == ND - 1))
                    last.then_inc(s["score_ps"], 1)
                    for c in range(2):
                        for b in range(2):
                            e = 2 * c + b
                            for d in range(ND):
                                last = pe.matmul(bank(2 + c)[:, b * NQ:(b + 1) * NQ],
                                                 wg(g, "wq", ND)[:, d, e * P:(e + 1) * P], xg[:, d, 0:NQ],
                                                 start=(d == 0), stop=(d == ND - 1))
                        last.then_inc(s["q_ps"], 1)
                    for e in range(NE):
                        for d in range(ND):
                            last = pe.matmul(bank(4)[:, e * NK:(e + 1) * NK],
                                             wg(g, "wk", ND)[:, d, e * P:(e + 1) * P], xg[:, d, NQ:W2],
                                             start=(d == 0), stop=(d == ND - 1))
                    last.then_inc(s["k_ps"], 1)
                    for d in range(ND):
                        last = pe.matmul(bank(5), xg[:, d, NQ:W2], wg(g, "wv", ND)[:, d, :],
                                         start=(d == 0), stop=(d == ND - 1))
                    last.then_inc(s["v_ps"], 1)
                    pe.wait_ge(s["qT_ready"], n * 2 + 2)
                    pe.wait_ge(s["kT_ready"], n * 2 + 2)
                    pe.wait_ge(s["nk_ready"], n * 2 + 2)
                    pe.wait_ge(s["tanh_ready"], n + 1)
                    for u in range(4):
                        if u == 2:
                            pe.wait_ge(s["v_ready"], n + 1)
                        if u == 3:
                            pe.wait_ge(s["exp_done"], n * 16 + 4)
                        for b in range(2):
                            e = 2 * (u % 2) + b
                            last = pe.matmul(bank(2 * (u % 3) + b)[:, 0:2 * (NK + 1)],
                                             qT[:, e, (u // 2) * P:(u // 2 + 1) * P],
                                             kT[:, e, :, :].rearrange("p a n -> p (a n)"), start=True, stop=True)
                        last.then_inc(s["s_ps"], 1)
                    for u in range(4):
                        c = u // 2
                        pe.wait_ge(s["p_ready"], n * 2 + c + 1)
                        if u == 0:
                            pe.wait_ge(s["exp_done"], n * 16 + 12)
                        for a in range(4):
                            h = 4 * (u % 2) + a
                            last = pe.transpose(bank(2 + u)[:, a * P:(a + 1) * P], p[:, c, h, 0:NK], ident)
                        last.then_inc(s["pT_ps"], 1)
                    pe.wait_ge(s["exp_done"], n * 16 + 16)
                    for c in range(2):
                        last = pe.transpose(bank(0)[0:FH, c * P:(c + 1) * P], p[:, c, :, NK], ident)
                    last.then_inc(s["pn_ps"], 1)
                    pe.wait_ge(s["pT_ready"], n * 4 + 4)
                    pe.wait_ge(s["pn_ready"], n + 1)
                    for c in range(2):
                        for b in range(2):
                            for hh in range(2):
                                h = 2 * (2 * c + b) + hh
                                last = pe.matmul(bank(c)[64 * hh:64 * hh + 64, b * NQ:(b + 1) * NQ],
                                                 v[:, h * FD:(h + 1) * FD], pT[:, h, :], start=True, stop=True)
                        last.then_inc(s["o_ps"], 1)
                    pe.wait_ge(s["oT_ready"], n * 2 + 2)
                    for c in range(2):
                        out = bank(2)[:, c * D:(c + 1) * D]
                        for e in range(NE):
                            pe.matmul(out, oT[:, e, c * P:(c + 1) * P], wg(g, "wo", NE)[:, e, :],
                                      start=(e == 0), stop=False)
                        last = pe.matmul(out, pnT[:, c * P:(c + 1) * P], nvw[:, g, :], start=False, stop=True)
                    last.then_inc(s["out_ps"], 1)
                    if g == 0:
                        pe.wait_ge(s["fin"], i * NT)
                    pe.wait_ge(s["oq_ready"], n * 2 + 2)
                    pe.wait_ge(s["hot_t"], n * 2 + 2)
                    for k in range(NT):
                        for c in range(2):
                            last = pe.matmul(bank(6 + k // 2)[:, (k % 2) * D:(k % 2 + 1) * D],
                                             hot_t[:, c, k * P:(k + 1) * P], oq[:, c, :],
                                             start=(g == 0 and c == 0 and k % 2 == 0),
                                             stop=(g == G - 1 and c == 1 and k % 2 == 1),
                                             skip_group_check=True)
                    last.then_inc(s["sum_ps"], 1)

        @block.vector
        def _(dve):
            with dve.Fori(0, NB) as i:
                dve.wait_ge(s["fin"], i * NT)
                dve.tensor_copy(pl[:, :, :, :], place[:, :, :].rearrange("p t (c r) -> p t c r", c=2)
                                [:, :, :, bass.ds(i * G, G)]).then_inc(s["pl_ready"], 1)
                dve.wait_ge(s["pl_ready"], i + 1)
                dve.tensor_scalar(seen[:, :, :], pl[:, :, 0, :], 0.0, None, ALU.is_ge).then_inc(s["cnt_link"], 1)
                dve.wait_ge(s["cnt_link"], i * 3 + 1)
                dve.tensor_reduce(cnt[:, 0, :], seen[:, :, :], AX, ALU.add).then_inc(s["cnt_link"], 1)
                dve.wait_ge(s["cnt_link"], i * 3 + 2)
                dve.tensor_scalar(cnt[:, 1, :], cnt[:, 0, :], 1e-5, None, ALU.max).then_inc(s["cnt_link"], 1)
                dve.tensor_scalar(cnt[:, 3, :], cnt[:, 0, :], 0.0, None, ALU.is_equal).then_inc(s["cnt_ready"], 1)
                dve.wait_ge(s["cnt_link"], i * 3 + 3)
                dve.reciprocal(cnt[:, 2, :], cnt[:, 1, :]).then_inc(s["cnt_ready"], 1)
                for g in range(G):
                    n = i * G + g
                    if g:
                        dve.wait_ge(s["xg_ps"], n * ND)
                    for k in range(NT):
                        dve.tensor_scalar(hot[:, k, 0:NQ], const("iota"), pl[:, k, 0, g:g + 1], None,
                                          ALU.is_equal).then_inc(s["hot"], 1)
                        dve.tensor_scalar(hot[:, k, NQ:W2], const("iota")[:, 0:NK], pl[:, k, 1, g:g + 1], None,
                                          ALU.is_equal).then_inc(s["hot"], 1)
                    if g == 0:
                        dve.wait_ge(s["place_back"], i * 16 + 16)
                    dve.wait_ge(s["sum_ps"], n)
                    for c in range(2):
                        dve.tensor_scalar(hot_t[:, c, :], prow[:, g, :], const("part")[:, c:c + 1], None,
                                          ALU.is_equal).then_inc(s["hot_t"], 1)
                    dve.wait_ge(s["tanh_ready"], n + 1)
                    dve.tensor_scalar(score[:, 0:3], score[:, 0:3], 1.0, 0.5, ALU.add, ALU.mult)\
                        .then_inc(s["score_ready"], 1)
                    dve.wait_ge(s["k_ps"], n + 1)
                    for hh in range(2):
                        r = slice(64 * hh, 64 * hh + 64)
                        dve.tensor_copy(kT[r, :, hh, 0:NK], bank(4)[r, :].rearrange("p (e n) -> p e n", e=NE))\
                            .then_inc(s["kT_ready"], 1)
                    for u in range(4):
                        dve.wait_ge(s["s_ps"], n * 4 + u + 1)
                        b = 2 * (u % 3)
                        dve.tensor_reduce(fmax[:, 4 * u:4 * u + 4].rearrange("p (a c) -> p a c", a=2),
                                          bank(b, 2).rearrange("p (a n) -> p a n", a=2)[:, :, 0:2 * (NK + 1)]
                                          .rearrange("p a (c n) -> p a c n", c=2), AX, ALU.max)\
                            .then_inc(s["fmax_link"], 1)
                        dve.wait_ge(s["fmax_link"], n * 4 + u + 1)
                        dve.tensor_scalar(fneg[:, 4 * u:4 * u + 4], fmax[:, 4 * u:4 * u + 4], -FD ** -0.5, None,
                                          ALU.mult).then_inc(s["fneg_ready"], 1)
                    for c in range(2):
                        dve.wait_ge(s["exp_done"], n * 16 + 8 * c + 8)
                        dve.reciprocal(frec[:, FH * c:FH * c + FH], fden[:, FH * c:FH * c + FH])\
                            .then_inc(s["frec_link"], 1)
                    for u in range(4):
                        dve.wait_ge(s["pT_ps"], n * 4 + u + 1)
                        dve.tensor_copy(pT[:, 4 * (u % 2):4 * (u % 2) + 4, (u // 2) * P:(u // 2 + 1) * P],
                                        bank(2 + u).rearrange("p (a n) -> p a n", a=4)).then_inc(s["pT_ready"], 1)
                    dve.wait_ge(s["out_ps"], n + 1)
                    for c in range(2):
                        dve.tensor_scalar(oq[:, c, :], bank(2)[:, c * D:(c + 1) * D], score[:, c:c + 1], None,
                                          ALU.mult).then_inc(s["oq_ready"], 1)
                dve.wait_ge(s["x1_loaded"], i * 16 + 16)
                dve.wait_ge(s["sum_ps"], i * G + G)
                dve.wait_ge(s["cnt_ready"], i * 2 + 2)
                dve.wait_ge(s["stored"], i * 16)
                for k in range(NT):
                    dve.scalar_tensor_tensor(x1[:, k, :], null[:, :], cnt[:, 3, k:k + 1], x1[:, k, :],
                                             ALU.mult, ALU.add).then_inc(s["fin_link"], 1)
                for k in range(NT):
                    dve.wait_ge(s["fin_link"], i * NT + k + 1)
                    dve.scalar_tensor_tensor(outs[:, k, :], bank(6 + k // 2)[:, (k % 2) * D:(k % 2 + 1) * D],
                                             cnt[:, 2, k:k + 1], x1[:, k, :], ALU.mult, ALU.add)\
                        .then_inc(s["fin"], 1)


def build(nc, x, co_d, cr_d, cw_d, wa_d, wb_d, bo_d, wc_d, null_d, out):
    def scratch(name, shape):
        return nc.dram_tensor(name, shape, F32).ap()

    dr = dict(x=x, co=co_d, cr=cr_d, cw=cw_d, wa=wa_d, wb=wb_d, bo=bo_d, wc=wc_d, null=null_d, out=out,
              zero=scratch("zero", (H, L)), parts=scratch("parts", (2, 2, D, L)),
              maxima=scratch("maxima", (H, L)), x1=scratch("x1_d", (NB, L, D)),
              x2=scratch("x2_d", (NB, L, D)), logits=scratch("logits_d", (2, NB, G, L)),
              place=scratch("place_d", (NB * G, L)))
    with ExitStack() as ctx:
        t = dict(ps=ctx.enter_context(nc.psum_tensor("ps", [P, 8 * BANK], F32)),
                 co=ctx.enter_context(nc.sbuf_tensor("co", [P, CO_N], F32)),
                 place=ctx.enter_context(nc.sbuf_tensor("place", [P, NT, 2 * NB * G], F32)))
        phase_dense(nc, t, dr)
        t["cr"] = ctx.enter_context(nc.sbuf_tensor("cr", [P, CR_N], F32))
        phase_route(nc, t, dr)
        phase_routed(nc, t, dr)




def by_tile(a):
    k = a.shape[0] // P
    return np.ascontiguousarray(a.reshape(k, P, a.shape[1]).transpose(1, 0, 2)).reshape(P, -1)


def strips_cols(a, heads):
    out = np.zeros((a.shape[0], heads, STRIP), np.float32)
    out[:, :, :DH] = a.reshape(a.shape[0], heads, DH)
    return out.reshape(a.shape[0], heads * STRIP)


def pack(cols, n, parts, lead=()):
    out = np.zeros((*lead, P, n), np.float32)
    for name, (a, b) in cols.items():
        v = parts[name]
        out[..., :v.shape[-2], a:b] = v
    return out


def kernel(**inputs):
    import concourse.bacc as bacc
    from concourse.bass_utils import run_bass_kernel_spmd

    f = {k: np.asarray(v) for k, v in inputs.items()}
    c, a, r = ({k[len(pre):]: v for k, v in f.items() if k.startswith(pre)}
               for pre in ("L0_cond_", "L0_attn_", "L0_ffn_"))
    wa = pack(WA, WA_N, dict(
        wq=by_tile(c["Wq"].T), wk=by_tile(c["Wk"].T), wv=by_tile(c["Wv"].T),
        wo=by_tile(strips_cols(c["Wo"], H).T), gate=by_tile(c["gate_w"].T), hid=by_tile(c["hid_w"].T),
        down=by_tile(c["out_w"].T)))
    lin = np.concatenate([a["Wq"][:, NLOC * DH:], a["Wk"][:, NLOC * DH:]], axis=1)
    wo_lin = a["Wo"][NLOC * DH:].reshape(2, LW, D).transpose(1, 0, 2).reshape(LW, 2 * D)
    wb = pack(WB, WB_N, dict(
        lq=by_tile(strips_cols(a["Wq"][:, :NLOC * DH], NLOC)),
        lk=by_tile(strips_cols(a["Wk"][:, :NLOC * DH], NLOC)), lin=by_tile(lin), wv=by_tile(a["Wv"]),
        wo_loc=strips_cols(np.ascontiguousarray(a["Wo"][:NLOC * DH].T), NLOC).T, wo_lin=wo_lin))
    wkv = r["w_kv"]
    nk, nv = r["null_kv"][:, :, :, 0, :]
    spread = np.zeros((G, FH, FD, FH), np.float32)
    for h in range(FH):
        spread[:, h, :, h] = nv[:, h]
    wc = np.stack([pack(WC, WC_N, dict(
        wq=by_tile(r["w_q"][g].T), wk=by_tile(wkv[g, :E].T), wv=by_tile(wkv[g, E:].T),
        wo=by_tile(r["w_out"][g].T), nk=by_tile(nk[g].reshape(E, 1)),
        nv=by_tile(spread[g].reshape(E, FH)))) for g in range(G)])
    row, part = np.arange(P), np.arange(P)
    tri = row[None, :] > part[:, None]
    cq = f["cond_256"]
    ks = np.zeros((P, 2 * NB * G), np.float32)
    ks[:, :NB * G], ks[:, NB * G:] = NQ, NK
    co = pack(CO, CO_N, dict(
        ident=np.eye(P), causal=np.where(tri, -CBIG, 0.0), all=np.full((P, P), -CBIG),
        hmask=(part[:, None] // STRIP == np.arange(NLOC)), dsel=(part[:, None] == STRIP * np.arange(4) + DH),
        cmask=(part[:, None] % 64 == np.arange(64)), bmask=(part[:, None] // DH == np.arange(LH)),
        qleft=np.tile(cq.T, (2, 1)),
        qright=np.tile(f["L0_cond2_q_right"].T, (2, 1)),
        sg=np.tile(f["L0_cond2_spectral_gate"].reshape(64, 1), (2, 1)),
        sign=np.tile(np.array([1, -1, -1, -1]), (P, 1)),
        wr=by_tile(np.concatenate([r["w_qr"], r["w_kvr"]]).T),
        cb=np.concatenate([c[n].reshape(ND, P).T for n in ("g1b", "b1b", "g2b", "b2b")], axis=1),
        cond=cq.T))
    cr = pack(CR, CR_N, dict(iota=np.tile(np.arange(NQ), (P, 1)), part=part[:, None] + P * np.arange(2),
                             before=tri, ones=np.ones((P, P)), kvec=ks))
    cw = np.concatenate([c[n].T for n in ("g1w", "b1w", "g2w", "b2w")], axis=1)
    arrays = dict(x=f["x"], co=co, cr=cr, cw=cw, wa=wa, wb=wb, bo=a["bo"].reshape(1, D), wc=wc,
                  null=r["null_token"].reshape(1, D))
    arrays = {f"in_{k}": np.ascontiguousarray(v) for k, v in arrays.items()}

    nc = bacc.Bacc("TRN2", target_bir_lowering=False, num_devices=1)
    args = [nc.dram_tensor(k, v.shape, mybir.dt.from_np(v.dtype), kind="ExternalInput").ap()
            for k, v in arrays.items()]
    out = nc.dram_tensor("out", (NB, L, D), F32, kind="ExternalOutput").ap()
    build(nc, *args, out)
    got = run_bass_kernel_spmd(nc, [arrays], core_ids=[0])
    return got.results[0]["out"]
```

```python
from contextlib import ExitStack

import numpy as np
import concourse.bass as bass
from concourse import mybir

F32 = mybir.dt.float32
F32R = mybir.dt.float32r
BF16 = mybir.dt.bfloat16
ALU = mybir.AluOpType
ACT = mybir.ActivationFunctionType
AX = mybir.AxisListType.X

P = 128
NB, L, D = 8, 512, 256
NT, ND = L // P, D // P
H, DH = 16, 16
STRIP = 32
HG = H * STRIP // P
HID = 4 * D
NM = HID // P
NLOC, NLIN = 4, 12
LH = NLIN // 2
LW = LH * DH
BLK = 64
NU = L // BLK - 1
CW = DH + 1
G, NQ, NK = 4, 256, 128
FH, FD = 8, 64
E = FH * FD
NE = E // P
SROW = 64 + 3 * DH
KST = SROW + 1
NV = 2 * NLOC
LOCAL0 = 5
BANK = 512
CBIG = 1e30



def columns(parts):
    at, out = 0, {}
    for name, n in parts:
        out[name] = (at, at + n)
        at += n
    return out, at


WA, WA_N = columns([("wq", ND * D), ("wk", ND * D), ("wv", ND * D), ("wo", HG * D),
                    ("gate", ND * HID), ("hid", ND * HID), ("down", NM * D)])
WB, WB_N = columns([("lq", ND * P), ("lk", ND * P), ("lin", ND * 2 * NLIN * DH), ("wv", ND * D),
                    ("wo_loc", D), ("wo_lin", 2 * D)])
WS, WS_N = columns([("wq", ND * E), ("wk", ND * E), ("wv", ND * E)])
WC, WC_N = columns([("wo", NE * D), ("nk", NE), ("nv", NE * FH)])
CO, CO_N = columns([("ident", P), ("causal", P), ("all", P), ("hmask", NLOC), ("dsel", 4),
                    ("cmask", 64), ("bmask", LH), ("qleft", NB), ("qright", 4), ("sg", 1),
                    ("sign", 4), ("wr", ND * 2 * G), ("cb", 4 * ND), ("cond", NB)])
CR, CR_N = columns([("iota", NQ), ("part", 2), ("before", P), ("ones", P), ("kvec", 2 * NB * G)])
CW4 = 4 * D


def phase_dense(nc, t, dr):
    with ExitStack() as ctx:
        def sb(name, shape, dt=F32):
            return ctx.enter_context(nc.sbuf_tensor(name, shape, dt))

        def sem(name):
            return ctx.enter_context(nc.semaphore(name))

        ps = t["ps"]

        def bank(k, n=1):
            return ps[:, k * BANK:(k + n) * BANK]

        def halves(ap):
            return ap.rearrange("p (a n) -> p a n", a=2)

        co = t["co"]

        def const(name):
            return co[:, CO[name][0]:CO[name][1]]

        ident = const("ident")
        wa = sb("wa", [P, WA_N])
        wb = sb("wb", [P, WB_N])
        bo = sb("bo", [P, D])
        stack_q = sb("stack_q", [KST, H, L], F32R)
        stack_k = sb("stack_k", [KST, H // 2, L], F32R)
        qk_hi = sb("qk_hi", [P, 2, L], F32R)
        qk_lo = sb("qk_lo", [P, 2, L], F32R)
        pt = sb("pt", [P, 8 * L])
        big = sb("big", [P, NM * L])
        va = sb("va", [P, NT, H, STRIP])
        vb = sb("vb", [P, NT, H, STRIP])
        heads_t = sb("heads_t", [P, HG, L])
        x_in = sb("x_in", [P, NT, D])
        x_next = sb("x_next", [P, NT, D])
        hn_a = sb("hn_a", [P, NT, D])
        xm = sb("xm", [P, NT, D])
        xc = sb("xc", [P, NT, D])
        x1 = sb("x1", [P, NT, D])
        hT = sb("hT", [P, ND, L])
        temp = sb("temp", [P, 2 * NU * (LH * CW + LW)])
        mrow = sb("mrow", [H, L], F32R)
        small = sb("small", [P, 448])
        causal_b = sb("causal_b", [P, P], BF16)
        all_b = sb("all_b", [P, P], BF16)
        ident_b = sb("ident_b", [P, P], BF16)
        rot = sb("rot", [P, ND, 4, 64])
        wc = sb("wc", [P, ND, 2 * G])

        def w(pack, cols, name, k):
            a, b = cols[name]
            return pack[:, a:b].rearrange("p (k n) -> p k n", k=k)

        wq, wk, wv = (w(wa, WA, n, ND) for n in ("wq", "wk", "wv"))
        wo, wdown = w(wa, WA, "wo", HG), w(wa, WA, "down", NM)
        wgate, whid = w(wa, WA, "gate", ND), w(wa, WA, "hid", ND)
        blq, blk, blin, bwv = (w(wb, WB, n, ND) for n in ("lq", "lk", "lin", "wv"))
        bwo_loc = wb[:, WB["wo_loc"][0]:WB["wo_loc"][1]]
        bwo_lin = w(wb, WB, "wo_lin", 2)

        p_t = pt[:, :].rearrange("p (s j n) -> p s j n", s=2, j=4)
        hT_a = pt[:, NT * D:2 * NT * D].rearrange("p (d n) -> p d n", d=ND)
        hn_b = pt[:, 2 * NT * D:3 * NT * D].rearrange("p (t d) -> p t d", t=NT)
        gT = big[:, :].rearrange("p (m n) -> p m n", m=NM)
        lp = big[:, 0:1024].rearrange("p (s u n) -> p s u n", s=2, u=2)
        locT = big[:, 1024:1536]
        logit = big[0:2 * G, 1536:2048]
        q_e = big[:, 2048:2816].rearrange("p (t n) -> p t n", t=NT)
        k_e = big[:, 2816:3584].rearrange("p (t n) -> p t n", t=NT)
        lkT = big[:, 3584:4096]
        cw = big[0:64, 0:CW4]
        rot_t = big[:, CW4:CW4 + ND * D].rearrange("p (k i c) -> p k i c", k=ND, i=4)
        osb = qk_hi[:, :, :].bitcast(F32)
        rspread = qk_lo[:, 0, :].bitcast(F32)
        tg = temp[:, 1024:2048].rearrange("p (s n) -> p s n", s=2)
        k_pos = temp[:, 0:NT * NLIN * DH].rearrange("p (t n) -> p t n", t=NT)
        cum = temp[0:LW, 0:2 * NU * LH * CW].rearrange("p (u n) -> p u n", u=NU)
        ctxn = temp[0:LW, 2 * NU * LH * CW:].rearrange("p (v n) -> p v n", v=2 * NU)
        qlT = xc[0:LW, :, :].rearrange("p t n -> p (t n)").rearrange("p (a n) -> p a n", a=2)
        linT = hT[0:LW, :, :]

        def lqm(h):
            return (xm, x1)[h // 2][:, 2 * (h % 2):2 * (h % 2) + 2, :].rearrange("p t n -> p (t n)")

        def lpT(v):
            out = big[:, 2048 + v * L:2048 + (v + 1) * L] if v < 3 else temp[:, (v - 3) * L:(v - 2) * L]
            return out.rearrange("p (u c n) -> p u c n", u=2, c=2)
        x2 = xc
        tg2 = xc[:, :, :].rearrange("p (s a) n -> p s (a n)", s=2)
        mtok = small[:, 0:64].rearrange("p (t h) -> p t h", t=NT)
        ms, msn, inv, half = (small[:, 64 + 4 * k:68 + 4 * k] for k in range(4))
        rden = small[:, 80:96]
        eps = small[:, 420:424]
        ms_b, msn_b, inv_b = (small[:, 424 + 4 * k:428 + 4 * k] for k in range(3))
        gb = small[:, 96:160].rearrange("p (k b) -> p k b", b=NB)
        gbc = small[:, 160:168]
        lmax, lneg, lden, lrec = (small[:, 168 + 16 * k:184 + 16 * k] for k in range(4))
        qmx, qsum = small[:, 232:280], small[:, 280:328]
        qrec = small[:, 328:376]
        ks = small[0:LW, 376:390]
        krec = small[0:LW, 390:404]
        nrm, lrot = small[:, 408:412], small[:, 412:416]
        rrot = small[:, 416:420]
        kmask = sb("kmask", [LW, 2 * NU, LH])
        kmask2 = sb("kmask2", [LW, 2 * NU, LH])
        coef = sb("coef", [P, 4, 4, 4])

        s = {n: sem(n) for n in (
            "consts", "w_first", "w_rest", "setup", "setup_pe", "setup_pool", "cleared", "link",
            "x_loaded", "next_loaded", "squares_a", "inv_a_tmp", "inv_a", "hn_a", "hTa_ps", "gbc_a", "hTa_ready",
            "qk_ps", "v_ps", "hi_ready", "lo_ready", "va_ready", "parts_stored", "stacked",
            "s_ps", "smax", "m_ps", "mrow_ready", "mrow_back", "st_ps", "exp_done", "pv_done",
            "osb_ready", "den_ps", "rden_ready", "rspread_ready", "rb_ps", "oT_ready", "ao_ps",
            "xm_ready",
            "x1_loaded", "squares_b", "inv_b_tmp", "inv_b", "hn_b", "hTb_ps", "gbc_b", "hTb_ready",
            "gh_ps", "tg_ready", "tg2_ready", "sg_done", "dn_ps", "xc_ready", "yT_ps",
            "yT_ready", "lqk_ps", "lqk_ready", "lin_ps", "k_parts", "lin_read", "lv_ps",
            "lv_ready", "ke_ready", "qe_ready", "kk_ready", "qn_ready", "ctx_ps", "ctx_read",
            "ctx_ready", "ql_ps", "ql_ready", "lin_out_ps", "linT_ready", "ls_ps", "lneg_ready",
            "lexp", "lnorm", "lt_ps", "lt_ready", "lo_ps", "locT_ready", "bias_added", "y_ps",
            "x1_ready", "x1T_ps", "x1T_ready", "x2_ps", "x2_ready", "lg_ps", "lg_ready",
            "x1_stored", "x2_stored", "lg_stored")}

        def need(eng, name, value):
            if not isinstance(value, int) or value > 0:
                eng.wait_ge(s[name], value)

        def batches(eng, body):
            body(0, None, True)
            with eng.Fori(0, NB - 2) as i:
                body(i + 1, i, True)
            body(NB - 1, NB - 2, False)
            body(None, NB - 1, False)

        def one(ap, i):
            return ap[i:i + 1] if isinstance(i, int) else ap[bass.ds(i, 1)]

        def tiles(ap, i):
            return one(ap, i).rearrange("a (t p) d -> p (a t) d", p=P)

        block = ctx.enter_context(nc.Block())

        @block.sync
        def _(sp):
            def load_x(a):
                need(sp, "xm_ready", a * 2)
                sp.dma_start(x_in[:, :, :], tiles(dr["x"], a)).then_inc(s["x_loaded"], 16)

            def load_next(a):
                need(sp, "hn_a", a * 4)
                sp.dma_start(x_next[:, :, :], tiles(dr["x"], a)).then_inc(s["next_loaded"], 16)

            def stacks(a):
                for o in range(2):
                    sp.wait_ge(s["hi_ready"], a * 4 + 2 * o + 2)
                    sp.dma_start(dr["parts"][o, 0].rearrange("(m p) n -> p m n", p=P),
                                 qk_hi[:, :, :].bitcast(F32)).then_inc(s["parts_stored"], 16)
                    sp.wait_ge(s["lo_ready"], a * 4 + 2 * o + 2)
                    sp.dma_start(dr["parts"][o, 1].rearrange("(m p) n -> p m n", p=P),
                                 qk_lo[:, :, :].bitcast(F32)).then_inc(s["parts_stored"], 16)
                    sp.wait_ge(s["parts_stored"], a * 64 + 32 * o + 32)
                    for r, part in enumerate(((0, 1, 0), (0, 0, 1))[o]):
                        for e in range(2):
                            row = 64 * e + DH * r
                            out = stack_k[row:row + DH, :, :] if o else stack_q[row:row + DH, e::2, :]
                            sp.dma_start(out.bitcast(F32), dr["parts"][o, part]
                                         .rearrange("(h e d) n -> e d h n", e=2, d=DH)[e])\
                                .then_inc(s["stacked"], 16)

            load_next(0)
            sp.dma_start(co[:, :], dr["co"]).then_inc(s["consts"], 16)
            sp.dma_start(cw[:, :], dr["cw"]).then_inc(s["consts"], 16)
            first = WA["wo"][0]
            sp.dma_start(wa[:, 0:first], dr["wa"][:, 0:first]).then_inc(s["w_first"], 16)
            load_x(0)
            sp.dma_start(wa[:, first:], dr["wa"][:, first:]).then_inc(s["w_rest"], 16)
            sp.dma_start(wb[:, :], dr["wb"]).then_inc(s["w_rest"], 16)
            sp.dma_start(bo[:, :], dr["bo"].to_broadcast([P, D])).then_inc(s["w_rest"], 16)
            sp.wait_ge(s["cleared"], 3)

            def body(a, b, more):
                if b is not None and a is not None:
                    load_x(a)
                if more:
                    load_next(a + 1)
                if a is not None:
                    stacks(a)
                    sp.wait_ge(s["mrow_ready"], a + 1)
                    sp.dma_start(stack_q[SROW:SROW + 1, :, :].bitcast(F32), mrow[:, :].bitcast(F32))\
                        .then_inc(s["mrow_back"], 16)
                if b is not None:
                    sp.wait_ge(s["ls_ps"], b * NV + NV)
                    sp.dma_start(x1[:, :, :], tiles(dr["x"], b)).then_inc(s["x1_loaded"], 16)
                    sp.wait_ge(s["x1_ready"], b * 2 + 2)
                    sp.dma_start(tiles(dr["x1"], b), x1[:, :, :]).then_inc(s["x1_stored"], 16)
                if b is not None:
                    sp.wait_ge(s["x2_ready"], b * 2 + 2)
                    sp.dma_start(tiles(dr["x2"], b), x2[:, :, :]).then_inc(s["x2_stored"], 16)
                    sp.wait_ge(s["lg_ready"], b + 1)
                    for c in range(2):
                        sp.dma_start(one(dr["logits"][c], b).rearrange("a g n -> (a g) n"),
                                     logit[G * c:G * c + G, :]).then_inc(s["lg_stored"], 16)

            batches(sp, body)
            sp.wait_ge(s["x1_stored"], NB * 16)
            sp.wait_ge(s["x2_stored"], NB * 16)
            sp.wait_ge(s["lg_stored"], NB * 32)

        @block.gpsimd
        def _(pool):
            pool.memset(eps, 1e-6).then_inc(s["setup_pool"], 1)
            pool.memset(half[:, :], -0.5).then_inc(s["setup_pool"], 1)
            pool.memset(va[:, :, :, :], 1.0).then_inc(s["setup_pool"], 1)
            pool.wait_ge(s["setup_pool"], 3)

            def inverse(i, side, mean, mean_eps, out):
                pool.wait_ge(s[f"squares_{side}"], i * 4 + 4)
                pool.tensor_tensor(mean_eps, mean, eps, ALU.add).then_inc(s[f"inv_{side}_tmp"], 1)
                pool.wait_ge(s[f"inv_{side}_tmp"], i + 1)
                pool.tensor_tensor(out, mean_eps, half, ALU.pow).then_inc(s[f"inv_{side}"], 1)

            def body(a, b, more):
                if more:
                    inverse(a + 1, "a", ms, msn, inv)
                if b is None:
                    pool.wait_ge(s["setup"], 2)
                    pool.tensor_tensor(nrm[:, 2:4], nrm[:, 0:2], half[:, 0:2], ALU.pow)\
                        .then_inc(s["setup_pool"], 1)
                if b is not None:
                    pool.wait_ge(s["x1_loaded"], b * 16 + 16)
                    for k in range(NT):
                        pool.tensor_tensor(x1[:, k, :], x1[:, k, :], bo[:, :], ALU.add)\
                            .then_inc(s["bias_added"], 1)
                if a is not None:
                    inverse(a, "b", ms_b, msn_b, inv_b)

            inverse(0, "a", ms, msn, inv)
            pool.memset(stack_q[:, :, :].bitcast(F32), 0.0).then_inc(s["cleared"], 1)
            pool.memset(vb[:, :, :, :], 1.0).then_inc(s["setup_pool"], 1)
            pool.wait_ge(s["w_rest"], 48)
            batches(pool, body)

        @block.scalar
        def _(act):
            def norm(i, side, src, out, mean, inverse):
                for k in range(NT):
                    act.activation(out[:, k, :], src[:, k, :], ACT.Square, scale=D ** -0.5,
                                   accum_out=mean[:, k:k + 1]).then_inc(s[f"squares_{side}"], 1)
                act.wait_ge(s[f"inv_{side}"], i + 1)
                for k in range(NT):
                    act.activation(out[:, k, :], src[:, k, :], ACT.Copy, scale=inverse[:, k:k + 1])\
                        .then_inc(s[f"hn_{side}"], 1)

            def norm_a(a):
                act.wait_ge(s["next_loaded"], a * 16 + 16)
                need(act, "hTa_ps", a * 2)
                norm(a, "a", x_next, hn_a, ms, inv)

            def norm_b(b):
                if b is None:
                    return
                act.wait_ge(s["xm_ready"], b * 2 + 2)
                norm(b, "b", xm, hn_b, ms_b, inv_b)

            def high_parts(a, o):
                if a is None:
                    return
                act.wait_ge(s["qk_ps"], a * 4 + o + 1)
                if o >= 2:
                    act.wait_ge(s["parts_stored"], a * 64 + 32)
                act.activation(qk_hi[:, o % 2, :], bank((2 + o) % 4), ACT.Copy).then_inc(s["hi_ready"], 1)

            def maxima_row(a):
                if a is None:
                    return
                act.wait_ge(s["m_ps"], a + 1)
                act.activation(mrow[:, :], bank(4)[0:H, :], ACT.Copy).then_inc(s["mrow_ready"], 1)

            def heads_out(a, g):
                if a is None:
                    return
                act.wait_ge(s["pv_done"], a * 16 + 4 * g + 4)
                if g >= 2:
                    act.wait_ge(s["oT_ready"], a * 4 + g - 1)
                act.activation(osb[:, g % 2, :], bank(4), ACT.Copy).then_inc(s["osb_ready"], 1)

            def exps(a, step):
                if a is None:
                    return
                for c in range(2):
                    u = 2 * step + c
                    act.wait_ge(s["st_ps"], a * 32 + u + 1)
                    if step >= 2 and c == 0:
                        act.wait_ge(s["pv_done"], a * 16 + step - 1)
                    act.activation(p_t[:, step % 2, 2 * c:2 * c + 2, :], halves(bank(2 * (u % 2), 2)),
                                   ACT.Exp, scale=0.25).then_inc(s["exp_done"], 1)

            def gate_tanh(b, m):
                if b is None:
                    return
                act.wait_ge(s["gh_ps"], b * 2 * NM + 2 * m + 1)
                if m >= 2:
                    act.wait_ge(s["tg2_ready"], b * NM + m - 1)
                act.activation(tg[:, m % 2, :], bank(6), ACT.Tanh, scale=0.5).then_inc(s["tg_ready"], 1)

            def turned(b, ps_name, ready):
                if b is None:
                    return
                for d in range(ND):
                    act.wait_ge(s[ps_name], b * 2 + d + 1)
                    act.activation(hT[:, d, :], bank(6 + d), ACT.Copy).then_inc(s[ready], 1)

            def local_qk(b):
                if b is None:
                    return
                act.wait_ge(s["lqk_ps"], b * 2 + 1)
                need(act, "x1_stored", b * 16)
                for h in range(NLOC):
                    act.activation(lqm(h), bank(6), ACT.Copy, scale=const("hmask")[:, h:h + 1])\
                        .then_inc(s["lqk_ready"], 1)
                act.wait_ge(s["lqk_ps"], b * 2 + 2)
                act.activation(lkT, bank(7), ACT.Copy).then_inc(s["lqk_ready"], 1)

            def linear_keys(b, u):
                if b is None:
                    return
                act.wait_ge(s["lin_ps"], b * NT + u + 1)
                k_ps = bank(6 + u % 2)[:, NLIN * DH:2 * NLIN * DH]
                act.activation(k_pos[:, u, :], k_ps, ACT.Relu)
                act.activation(k_e[:, u, :], k_ps, ACT.Relu, scale=-1.0).then_inc(s["k_parts"], 1)

            def key_exp(b):
                if b is None:
                    return
                act.wait_ge(s["k_parts"], b * NT + NT)
                act.activation(k_e, k_e, ACT.Exp, scale=-1.0).then_inc(s["ke_ready"], 1)

            def query_exp(b):
                if b is None:
                    return
                act.wait_ge(s["lin_read"], b * NT + NT)
                act.activation(q_e, q_e, ACT.Exp).then_inc(s["qe_ready"], 1)

            def linear_queries(b):
                if b is None:
                    return
                for a in range(2):
                    act.wait_ge(s["ql_ps"], b * 2 + a + 1)
                    act.activation(qlT[:, a, :], bank(6 + a)[0:LW, :], ACT.Copy).then_inc(s["ql_ready"], 1)

            def local_exp(b, v):
                if b is None:
                    return
                act.wait_ge(s["lneg_ready"], b * NV + v + 1)
                if v >= 2:
                    act.wait_ge(s["lt_ps"], b * NV + v - 1)
                for u in range(2):
                    c = 2 * v + u
                    act.activation(lp[:, v % 2, u, :], bank(6 + v % 2)[:, 2 * P * u:2 * P * u + 2 * P],
                                   ACT.Exp, scale=0.25, bias=lneg[:, c:c + 1],
                                   accum_out=lden[:, c:c + 1]).then_inc(s["lexp"], 1)

            def local_out(b):
                if b is None:
                    return
                act.wait_ge(s["lo_ps"], b + 1)
                act.activation(locT[:, :], bank(6), ACT.Copy).then_inc(s["locT_ready"], 1)

            def rotated(b):
                if b is None:
                    return
                for c in range(2):
                    act.wait_ge(s["x2_ps"], b * 2 + c + 1)
                    act.activation(x2[:, 2 * c:2 * c + 2, :], halves(bank(6 + c)), ACT.Copy)\
                        .then_inc(s["x2_ready"], 1)
                act.wait_ge(s["lg_ps"], b + 1)
                act.activation(logit[:, :], bank(5)[0:2 * G, :], ACT.Copy).then_inc(s["lg_ready"], 1)

            def body(a, b, more):
                for o in range(4):
                    high_parts(a, o)
                for m in range(NM):
                    gate_tanh(b, m)
                if more:
                    norm_a(a + 1)
                turned(b, "yT_ps", "yT_ready")
                local_qk(b)
                for u in range(NT):
                    linear_keys(b, u)
                key_exp(b)
                maxima_row(a)
                query_exp(b)
                for step in range(NT * HG):
                    exps(a, step)
                    if step % 4 == 0 and step:
                        heads_out(a, step // 4 - 1)
                    if step == 3:
                        linear_queries(b)
                    if LOCAL0 <= step < LOCAL0 + NV:
                        local_exp(b, step - LOCAL0)
                heads_out(a, HG - 1)
                local_out(b)
                turned(b, "x1T_ps", "x1T_ready")
                norm_b(a)
                rotated(b)

            norm_a(0)
            act.wait_ge(s["consts"], 32)
            batches(act, body)

        @block.tensor
        def _(pe):
            def transposes(i, src, base, ready):
                for d in range(ND):
                    for k in range(NT):
                        last = pe.transpose(bank(base + d)[:, k * P:(k + 1) * P],
                                            src[:, k, d * P:(d + 1) * P], ident)
                    last.then_inc(s[ready], 1)

            def normed_a(a):
                if a is None:
                    return
                pe.wait_ge(s["hn_a"], a * 4 + 4)
                need(pe, "xm_ready", a * 2)
                transposes(a, hn_a, 0, "hTa_ps")

            def queries_keys(a, o):
                if a is None:
                    return
                pe.wait_ge(s["hTa_ready"], a * 2 + 2)
                for k in range(ND):
                    last = pe.matmul(bank((2 + o) % 4), (wq, wk)[o // 2][:, k, (o % 2) * P:(o % 2 + 1) * P],
                                     hT_a[:, k, :], start=(k == 0), stop=(k == ND - 1))
                last.then_inc(s["qk_ps"], 1)

            def values_a(a):
                if a is None:
                    return
                for c in range(2):
                    if c:
                        need(pe, "lg_ready", a - 1)
                    for b in range(2):
                        for k in range(ND):
                            last = pe.matmul(bank(4 + c)[:, b * D:(b + 1) * D],
                                             hT_a[:, k, (2 * c + b) * P:(2 * c + b + 1) * P], wv[:, k, :],
                                             start=(k == 0), stop=(k == ND - 1))
                    last.then_inc(s["v_ps"], 1)

            def scores(a, n):
                if a is None:
                    return
                h, c = n // 2, n % 2
                if n == 0:
                    pe.wait_ge(s["stacked"], a * 192 + 192)
                if n >= 2:
                    pe.wait_ge(s["smax"], a * 32 + n - 1)
                for b in range(2):
                    last = pe.matmul(bank(2 * (n % 2) + b),
                                     stack_q[0:SROW, h, (2 * c + b) * P:(2 * c + b + 1) * P],
                                     stack_k[0:SROW, h // 2, :], start=True, stop=True)
                last.then_inc(s["s_ps"], 1)

            def maxima(a):
                if a is None:
                    return
                pe.wait_ge(s["smax"], a * 32 + 32)
                pe.wait_ge(s["va_ready"], a * 2 + 2)
                for k in range(NT):
                    last = pe.transpose(bank(4)[0:H, k * P:(k + 1) * P], mtok[:, k, :], ident)
                last.then_inc(s["m_ps"], 1)

            def scores_less_max(a, step):
                if a is None:
                    return
                g, kt = step // 4, step % 4
                if step == 0:
                    pe.wait_ge(s["mrow_back"], a * 16 + 16)
                for c in range(2):
                    u = 2 * step + c
                    if u >= 2:
                        pe.wait_ge(s["exp_done"], a * 32 + u - 1)
                    for b in range(2):
                        h = 4 * g + 2 * c + b
                        last = pe.matmul(bank(2 * (u % 2) + b), stack_k[:, h // 2, kt * P:(kt + 1) * P],
                                         stack_q[:, h, :], start=True, stop=True)
                    last.then_inc(s["st_ps"], 1)

            def weigh(a, step):
                if a is None:
                    return
                g, kt = step // 4, step % 4
                pe.wait_ge(s["exp_done"], a * 32 + 2 * step + 2)
                if kt == 0 and g:
                    pe.wait_ge(s["osb_ready"], a * 4 + g)
                for j in range(4):
                    last = pe.matmul(bank(4)[STRIP * j:STRIP * (j + 1), :],
                                     va[:, kt, 4 * g + j, :], p_t[:, step % 2, j, :],
                                     start=(kt == 0), stop=(kt == NT - 1))
                last.then_inc(s["pv_done"], 1)

            def sums(a, g):
                if a is None:
                    return
                pe.wait_ge(s["osb_ready"], a * 4 + g + 1)
                if g:
                    pe.wait_ge(s["oT_ready"], a * 4 + g)
                for k in range(NT):
                    last = pe.matmul(bank(5)[:, 4 * k:4 * k + 4], osb[:, g % 2, k * P:(k + 1) * P],
                                     const("dsel"), start=True, stop=True)
                last.then_inc(s["den_ps"], 1)

            def spread(a, g):
                if a is None:
                    return
                pe.wait_ge(s["rspread_ready"], a * 4 + g + 1)
                for k in range(NT):
                    last = pe.matmul(bank(5)[:, k * P:(k + 1) * P],
                                     rspread[:, k * P:(k + 1) * P], ident, start=True, stop=True)
                last.then_inc(s["rb_ps"], 1)

            def output_a(a, c):
                if a is None:
                    return
                pe.wait_ge(s["oT_ready"], a * 4 + 4)
                for b in range(2):
                    k = 2 * c + b
                    for g in range(HG):
                        last = pe.matmul(bank(c)[:, b * D:(b + 1) * D],
                                         heads_t[:, g, k * P:(k + 1) * P], wo[:, g, :],
                                         start=(g == 0), stop=(g == HG - 1))
                last.then_inc(s["ao_ps"], 1)

            def normed_b(b):
                if b is None:
                    return
                pe.wait_ge(s["hn_b"], b * 4 + 4)
                need(pe, "x2_ready", b * 2)
                transposes(b, hn_b, 6, "hTb_ps")

            def gate_hidden(b, m):
                if b is None:
                    return
                for wt, out in ((wgate, 6), (whid, 7)):
                    if m == 0:
                        pe.wait_ge(s["hTb_ready"], b * 2 + 2)
                    elif out == 6:
                        pe.wait_ge(s["tg2_ready"], b * NM + m)
                    else:
                        pe.wait_ge(s["sg_done"], b * NM + m)
                    for k in range(ND):
                        last = pe.matmul(bank(out), wt[:, k, m * P:(m + 1) * P],
                                         hT[:, k, :], start=(k == 0), stop=(k == ND - 1))
                    last.then_inc(s["gh_ps"], 1)

            def down(b, piece):
                if b is None:
                    return
                if piece == 0:
                    pe.wait_ge(s["sg_done"], b * NM + NM)
                k, m0 = piece // 4, 2 * (piece % 4)
                for m in (m0, m0 + 1):
                    last = pe.matmul(bank(6 + k // 2)[:, (k % 2) * D:(k % 2 + 1) * D], gT[:, m, k * P:(k + 1) * P],
                                     wdown[:, m, :], start=(m == 0), stop=(m == NM - 1))
                if piece % 8 == 7:
                    last.then_inc(s["dn_ps"], 1)

            def conditioned(b):
                if b is None:
                    return
                pe.wait_ge(s["xc_ready"], b * 2 + 2)
                transposes(b, xc, 6, "yT_ps")

            def local_proj(b, o):
                if b is None:
                    return
                pe.wait_ge(s["yT_ready"], b * 2 + 2)
                for k in range(ND):
                    last = pe.matmul(bank(6 + o), (blq, blk)[o][:, k, :], hT[:, k, :],
                                     start=(k == 0), stop=(k == ND - 1))
                last.then_inc(s["lqk_ps"], 1)

            def linear_proj(b, u):
                if b is None:
                    return
                if u == 0:
                    pe.wait_ge(s["lqk_ready"], b * (NLOC + 1) + NLOC)
                elif u == 1:
                    pe.wait_ge(s["lqk_ready"], b * (NLOC + 1) + NLOC + 1)
                else:
                    pe.wait_ge(s["lin_read"], b * NT + u - 1)
                for k in range(ND):
                    last = pe.matmul(bank(6 + u % 2)[:, 0:2 * NLIN * DH], hT[:, k, u * P:(u + 1) * P],
                                     blin[:, k, :], start=(k == 0), stop=(k == ND - 1))
                last.then_inc(s["lin_ps"], 1)

            def values_b(b, c):
                if b is None:
                    return
                pe.wait_ge(s["lin_read"], b * NT + 3 + c)
                for h in range(2):
                    for k in range(ND):
                        last = pe.matmul(bank(6 + c)[:, h * D:(h + 1) * D],
                                         hT[:, k, (2 * c + h) * P:(2 * c + h + 1) * P], bwv[:, k, :],
                                         start=(k == 0), stop=(k == ND - 1))
                last.then_inc(s["lv_ps"], 1)

            def contexts(b, r):
                if b is None:
                    return
                if r == 0:
                    pe.wait_ge(s["lv_ready"], b * 2 + 2)
                    pe.wait_ge(s["kk_ready"], b + 1)
                else:
                    pe.wait_ge(s["ctx_read"], b * 2 + 1)
                for u in range(4 * r, min(4 * r + 4, NU)):
                    for a in range(2):
                        row = BLK * (u % 2)
                        c = (2 * (u // 2 % 2) + a) * LH * CW
                        last = pe.matmul(bank(6 + u % 2)[0:LW, c:c + LH * CW],
                                         k_e[row:row + BLK, u // 2, a * LW:(a + 1) * LW],
                                         vb[row:row + BLK, u // 2, NLOC + LH * a:NLOC + LH * (a + 1), 0:CW],
                                         start=True, stop=True)
                last.then_inc(s["ctx_ps"], 1)

            def linear_queries(b):
                if b is None:
                    return
                pe.wait_ge(s["qn_ready"], b + 1)
                pe.wait_ge(s["ctx_read"], b * 2 + 2)
                for a in range(2):
                    for k in range(NT):
                        last = pe.transpose(bank(6 + a)[0:LW, k * P:(k + 1) * P],
                                            q_e[:, k, a * LW:(a + 1) * LW], ident)
                    last.then_inc(s["ql_ps"], 1)

            def linear_out(b):
                if b is None:
                    return
                pe.wait_ge(s["ql_ready"], b * 2 + 2)
                pe.wait_ge(s["ctx_ready"], b + 1)
                for a in range(2):
                    for u in range(NU):
                        last = pe.matmul(bank(6 + a)[0:LW, BLK * (u + 1):BLK * (u + 2)],
                                         ctxn[:, 2 * u + a, :], qlT[:, a, BLK * (u + 1):BLK * (u + 2)],
                                         start=True, stop=True)
                    last.then_inc(s["lin_out_ps"], 1)

            def local_scores(b, v):
                if b is None:
                    return
                if v < 2:
                    pe.wait_ge(s["linT_ready"], b * 2 + v + 1)
                else:
                    pe.wait_ge(s["lt_ready"], b * NV + v - 1)
                for u in (2 * (v % 2), 2 * (v % 2) + 1):
                    out = bank(6 + v % 2)[:, 2 * P * (u % 2):2 * P * (u % 2 + 1)]
                    q = lqm(v // 2)[:, u * P:(u + 1) * P]
                    if u:
                        pe.matmul(out, q, lkT[:, (u - 1) * P:(u + 1) * P], start=True, stop=False)
                    else:
                        pe.matmul(out[:, 0:P], ident_b[:, :], all_b[:, :], start=True, stop=True)
                        pe.matmul(out[:, P:], q, lkT[:, 0:P], start=True, stop=False)
                    last = pe.matmul(out[:, P:], ident_b[:, :], causal_b[:, :], start=False, stop=True)
                last.then_inc(s["ls_ps"], 1)

            def local_transposes(b, v):
                if b is None:
                    return
                pe.wait_ge(s["lnorm"], b * 2 * NV + 2 * v + 2)
                for u in range(2):
                    for c in range(2):
                        last = pe.transpose(bank(6 + v % 2)[:, (2 * u + c) * P:(2 * u + c + 1) * P],
                                            lp[:, v % 2, u, c * P:(c + 1) * P], ident)
                last.then_inc(s["lt_ps"], 1)

            def local_out(b):
                if b is None:
                    return
                pe.wait_ge(s["lt_ready"], b * NV + NV)
                for u in range(NT):
                    for c in ((0, 1) if u else (1,)):
                        for h in range(NLOC):
                            last = pe.matmul(bank(6)[STRIP * h:STRIP * (h + 1), u * P:(u + 1) * P],
                                             vb[:, u - 1 + c, h, :], lpT(2 * h + u // 2)[:, u % 2, c, :],
                                             start=(c == 0 or u == 0), stop=(c == 1))
                last.then_inc(s["lo_ps"], 1)

            def output_b(b, c):
                if b is None:
                    return
                pe.wait_ge(s["locT_ready"], b + 1)
                for j in range(2):
                    k = 2 * c + j
                    out = bank(7 - c)[:, j * D:(j + 1) * D]
                    pe.matmul(out, locT[:, k * P:(k + 1) * P], bwo_loc, start=True, stop=False)
                    pe.matmul(out, linT[:, 0, k * P:(k + 1) * P], bwo_lin[0:LW, 0, :],
                              start=False, stop=False)
                    last = pe.matmul(out, linT[:, 1, k * P:(k + 1) * P], bwo_lin[0:LW, 1, :],
                                     start=False, stop=True)
                last.then_inc(s["y_ps"], 1)

            def final_tokens(b):
                if b is None:
                    return
                pe.wait_ge(s["x1_ready"], b * 2 + 2)
                transposes(b, x1, 6, "x1T_ps")

            def rotation(b):
                if b is None:
                    return
                pe.wait_ge(s["x1T_ready"], b * 2 + 2)
                for c in range(2):
                    for j in range(2):
                        k = 2 * c + j
                        for d in range(ND):
                            last = pe.matmul(bank(6 + c)[:, j * D:(j + 1) * D], hT[:, d, k * P:(k + 1) * P],
                                             rot[:, d, :, :].rearrange("p i c -> p (i c)"),
                                             start=(d == 0), stop=(d == ND - 1))
                    last.then_inc(s["x2_ps"], 1)

            def logits(b):
                if b is None:
                    return
                for d in range(ND):
                    last = pe.matmul(bank(5)[0:2 * G, :], wc[:, d, :], hT[:, d, :],
                                     start=(d == 0), stop=(d == ND - 1))
                last.then_inc(s["lg_ps"], 1)

            def routing_weights():
                pe.wait_ge(s["setup"], 3)
                wr = const("wr").rearrange("p (k n) -> p k n", k=ND)
                for d in range(ND):
                    for k in range(ND):
                        last = pe.matmul(bank(7)[:, d * 2 * G:(d + 1) * 2 * G],
                                         rot_t[:, k, :, :].rearrange("p i c -> p (i c)")[:, d * P:(d + 1) * P],
                                         wr[:, k, :], start=(k == 0), stop=(k == ND - 1))
                last.then_inc(s["setup_pe"], 1)
                pe.wait_ge(s["w_rest"], 48)

            def body(a, b, more):
                queries_keys(a, 0)
                queries_keys(a, 1)
                normed_b(b)
                queries_keys(a, 2)
                queries_keys(a, 3)
                gate_hidden(b, 0)
                values_a(a)
                for m in range(1, NM):
                    gate_hidden(b, m)
                for n in range(2 * H):
                    scores(a, n)
                    if n < 16:
                        down(b, n)
                    elif n == 18:
                        conditioned(b)
                    elif n in (20, 22):
                        local_proj(b, (n - 20) // 2)
                    elif n >= 24 and n % 2 == 0:
                        linear_proj(b, (n - 24) // 2)
                maxima(a)
                values_b(b, 0)
                values_b(b, 1)
                for step in range(NT * HG):
                    scores_less_max(a, step)
                    if step:
                        weigh(a, step - 1)
                    if step % 4 == 2 and step > 4:
                        sums(a, step // 4 - 1)
                    if step % 4 == 3 and step > 4:
                        spread(a, step // 4 - 1)
                    if step < 2:
                        contexts(b, step)
                    elif step == 3:
                        linear_queries(b)
                    elif step == 4:
                        linear_out(b)
                    if b is None and step == 1:
                        routing_weights()
                    if LOCAL0 <= step < LOCAL0 + NV:
                        local_scores(b, step - LOCAL0)
                    if LOCAL0 < step <= LOCAL0 + NV:
                        local_transposes(b, step - LOCAL0 - 1)
                weigh(a, NT * HG - 1)
                local_out(b)
                sums(a, HG - 1)
                output_b(b, 0)
                spread(a, HG - 1)
                output_b(b, 1)
                output_a(a, 0)
                final_tokens(b)
                output_a(a, 1)
                rotation(b)
                if more:
                    normed_a(a + 1)
                logits(b)
                if b is None:
                    pe.wait_ge(s["setup"], 5)

            pe.wait_ge(s["consts"], 32)
            for c in range(4 * ND):
                last = pe.matmul(bank(7)[:, c * NB:(c + 1) * NB], cw[:, c * P:(c + 1) * P],
                                 co[0:64, CO["cond"][0]:CO["cond"][1]], start=True, stop=True)
            last.then_inc(s["setup_pe"], 1)
            normed_a(0)
            pe.wait_ge(s["w_first"], 16)
            batches(pe, body)

        @block.vector
        def _(dve):
            n_link = [0]

            def link(ins):
                n_link[0] += 1
                ins.then_inc(s["link"], 1)
                dve.wait_ge(s["link"], n_link[0])

            dve.memset(stack_k[32:64, :, :].bitcast(F32), 0.0).then_inc(s["cleared"], 1)
            dve.memset(stack_k[96:KST, :, :].bitcast(F32), -1.0).then_inc(s["cleared"], 1)
            dve.wait_ge(s["consts"], 32)
            dve.wait_ge(s["setup_pe"], 1)
            link(dve.tensor_tensor(gb, bank(7)[:, 0:4 * ND * NB].rearrange("p (k b) -> p k b", b=NB),
                                   const("cb")[:, :, None].to_broadcast([P, 4 * ND, NB]), ALU.add))

            def tables():
                ql, qr = const("qleft"), const("qright")
                link(dve.tensor_tensor(temp[:, 0:NB], ql, ql, ALU.mult))
                link(dve.tensor_tensor(temp[:, NB:NB + 4], qr, qr, ALU.mult))
                link(dve.tensor_reduce(nrm[:, 0:1], temp[:, 0:NB], AX, ALU.add))
                link(dve.tensor_reduce(nrm[:, 1:2], temp[:, NB:NB + 4], AX, ALU.add))
                dve.tensor_scalar(nrm[:, 0:1], nrm[:, 0:1], 1e-8, None, ALU.add).then_inc(s["setup"], 1)
                dve.tensor_scalar(nrm[:, 1:2], nrm[:, 1:2], 1e-8, None, ALU.add).then_inc(s["setup"], 1)
                dve.wait_ge(s["setup_pool"], 5)
                link(dve.tensor_scalar(lrot, ql[:, 0:4], nrm[:, 2:3], None, ALU.mult))
                link(dve.tensor_scalar(rrot, qr, nrm[:, 3:4], const("sg"), ALU.mult, ALU.mult))
                link(dve.tensor_tensor(rrot, rrot, const("sign"), ALU.mult))
                w_, x_, y_, z_ = range(4)
                left = (((w_, 1), (x_, -1), (y_, -1), (z_, -1)), ((x_, 1), (w_, 1), (z_, -1), (y_, 1)),
                        ((y_, 1), (z_, 1), (w_, 1), (x_, -1)), ((z_, 1), (y_, -1), (x_, 1), (w_, 1)))
                right = (((w_, 1), (x_, -1), (y_, -1), (z_, -1)), ((x_, 1), (w_, 1), (z_, 1), (y_, -1)),
                         ((y_, 1), (z_, -1), (w_, 1), (x_, 1)), ((z_, 1), (y_, 1), (x_, -1), (w_, 1)))
                for m, (table, src) in enumerate(((left, lrot), (right, rrot))):
                    for a in range(4):
                        for b in range(4):
                            q, sgn = table[a][b]
                            last = dve.tensor_scalar(coef[:, m, a, b:b + 1], src[:, q:q + 1], float(sgn), None, ALU.mult)
                link(last)
                for k in range(4):
                    o = coef[:, 2 if k == 0 else 3, :, :]
                    link(dve.tensor_tensor(o, coef[:, 0, :, k:k + 1].to_broadcast([P, 4, 4]),
                                           coef[:, 1, k:k + 1, :].to_broadcast([P, 4, 4]), ALU.mult))
                    if k:
                        link(dve.tensor_tensor(coef[:, 2, :, :], coef[:, 2, :, :], coef[:, 3, :, :], ALU.add))
                for k in range(ND):
                    for hh in range(2):
                        p = slice(64 * hh, 64 * hh + 64)
                        j = 2 * k + hh
                        cm = co[p, CO["cmask"][0]:CO["cmask"][1]]
                        for o in range(4):
                            dve.tensor_scalar(rot[p, k, o, :], cm, coef[p, 2, o, j:j + 1], None, ALU.mult)
                            last = dve.tensor_scalar(rot_t[p, k, o, :], cm, coef[p, 2, j, o:o + 1], None, ALU.mult)
                last.then_inc(s["setup"], 1)
                dve.wait_ge(s["setup_pe"], 2)
                dve.tensor_copy(wc[:, :, :], bank(7)[:, 0:4 * G].rearrange("p (k n) -> p k n", k=ND))\
                    .then_inc(s["setup"], 1)
                link(dve.tensor_copy(kmask[:, :, :], co[0:LW, None, CO["bmask"][0]:CO["bmask"][1]]
                                     .to_broadcast([LW, 2 * NU, LH])))
                dve.tensor_copy(causal_b[:, :], const("causal"))
                dve.tensor_copy(all_b[:, :], const("all"))
                dve.tensor_copy(ident_b[:, :], ident).then_inc(s["setup"], 1)

            LINKS = 31
            at = [0]

            def chain(b, ins):
                at[0] += 1
                ins.then_inc(s["link"], 1)
                dve.wait_ge(s["link"], b * LINKS + n_link[0] + at[0])

            def scale_shift(i, side, base, out):
                if i is None:
                    return
                c0 = 0 if side == "a" else 4
                need(dve, f"hT{side}_ready", i * 2)
                cols = slice(i, i + 1) if isinstance(i, int) else bass.ds(i, 1)
                dve.tensor_copy(gbc[:, c0:c0 + 4], gb[:, c0:c0 + 4, cols].rearrange("p k b -> p (k b)"))\
                    .then_inc(s[f"gbc_{side}"], 1)
                dve.wait_ge(s[f"gbc_{side}"], i + 1)
                for d in range(ND):
                    dve.wait_ge(s[f"hT{side}_ps"], i * 2 + d + 1)
                    dve.tensor_scalar(out[:, d, :], bank(base + d), gbc[:, c0 + d:c0 + d + 1],
                                      gbc[:, c0 + 2 + d:c0 + 3 + d], ALU.mult, ALU.add)\
                        .then_inc(s[f"hT{side}_ready"], 1)

            def values(i, c, buf, base, ps_name, ready):
                if i is None:
                    return
                dve.wait_ge(s[ps_name], i * 2 + c + 1)
                dve.tensor_copy(buf[:, 2 * c:2 * c + 2, :, 0:DH],
                                bank(base + c).rearrange("p (t h d) -> p t h d", t=2, h=H))\
                    .then_inc(s[ready], 1)

            def low_parts(a, o):
                if a is None:
                    return
                dve.wait_ge(s["hi_ready"], a * 4 + o + 1)
                if o >= 2:
                    dve.wait_ge(s["parts_stored"], a * 64 + 32)
                dve.tensor_tensor(qk_lo[:, o % 2, :], bank((2 + o) % 4), qk_hi[:, o % 2, :].bitcast(F32),
                                  ALU.subtract).then_inc(s["lo_ready"], 1)

            def maxima(a, n):
                if a is None:
                    return
                dve.wait_ge(s["s_ps"], a * 32 + n + 1)
                dve.tensor_reduce(mtok[:, 2 * (n % 2):2 * (n % 2) + 2, n // 2], halves(bank(2 * (n % 2), 2)),
                                  AX, ALU.max).then_inc(s["smax"], 1)

            def reciprocals(a, g):
                if a is None:
                    return
                dve.wait_ge(s["den_ps"], a * 4 + g + 1)
                dve.reciprocal(rden, bank(5)[:, 0:16]).then_inc(s["rden_ready"], 1)
                dve.wait_ge(s["rden_ready"], a * 4 + g + 1)
                dve.tensor_copy(rspread.rearrange("p (c n) -> p c n", n=STRIP),
                                rden[:, :, None].to_broadcast([P, 16, STRIP])).then_inc(s["rspread_ready"], 1)

            def normalized(a, g):
                if a is None:
                    return
                dve.wait_ge(s["rb_ps"], a * 4 + g + 1)
                dve.tensor_tensor(heads_t[:, g, :], osb[:, g % 2, :], bank(5), ALU.mult)\
                    .then_inc(s["oT_ready"], 1)

            def attended(a, c):
                if a is None:
                    return
                dve.wait_ge(s["ao_ps"], a * 2 + c + 1)
                dve.wait_ge(s["x_loaded"], a * 16 + 16)
                need(dve, "xc_ready", a * 2)
                dve.tensor_tensor(xm[:, 2 * c:2 * c + 2, :], x_in[:, 2 * c:2 * c + 2, :],
                                  halves(bank(c)), ALU.add).then_inc(s["xm_ready"], 1)

            def swiglu(b, m):
                if b is None:
                    return
                dve.wait_ge(s["tg_ready"], b * NM + m + 1)
                if m >= 2:
                    dve.wait_ge(s["sg_done"], b * NM + m - 1)
                if m == 0:
                    need(dve, "x2_stored", b * 16)
                    need(dve, "lg_stored", b * 32)
                dve.scalar_tensor_tensor(tg2[:, m % 2, :], tg[:, m % 2, :], 1.0, bank(6),
                                         ALU.add, ALU.mult).then_inc(s["tg2_ready"], 1)
                dve.wait_ge(s["tg2_ready"], b * NM + m + 1)
                dve.wait_ge(s["gh_ps"], b * 2 * NM + 2 * m + 2)
                dve.scalar_tensor_tensor(gT[:, m, :], tg2[:, m % 2, :], 0.5, bank(7),
                                         ALU.mult, ALU.mult).then_inc(s["sg_done"], 1)

            def conditioned(b, c):
                if b is None:
                    return
                dve.wait_ge(s["dn_ps"], b * 2 + c + 1)
                dve.tensor_tensor(xc[:, 2 * c:2 * c + 2, :], xm[:, 2 * c:2 * c + 2, :],
                                  halves(bank(6 + c)), ALU.add).then_inc(s["xc_ready"], 1)

            def linear_parts(b, u):
                if b is None:
                    return
                dve.wait_ge(s["k_parts"], b * NT + u + 1)
                q_ps = bank(6 + u % 2)[:, 0:NLIN * DH].rearrange("p (h d) -> p h d", d=DH)
                m = qmx[:, NLIN * u:NLIN * (u + 1)]
                chain(b, dve.tensor_reduce(m, q_ps, AX, ALU.max))
                dve.tensor_tensor(q_e[:, u, :].rearrange("p (h d) -> p h d", d=DH), q_ps,
                                  m[:, :, None].to_broadcast([P, NLIN, DH]), ALU.subtract)\
                    .then_inc(s["lin_read"], 1)

            def linear_keys(b):
                if b is None:
                    return
                dve.wait_ge(s["ke_ready"], b + 1)
                dve.tensor_tensor(k_e, k_pos, k_e, ALU.add).then_inc(s["kk_ready"], 1)

            def linear_queries(b):
                if b is None:
                    return
                q4 = q_e.rearrange("p t (h d) -> p t h d", d=DH)
                dve.wait_ge(s["qe_ready"], b + 1)
                chain(b, dve.tensor_reduce(qsum, q4, AX, ALU.add))
                chain(b, dve.reciprocal(qrec, qsum))
                dve.tensor_tensor(q4, q4, qrec.rearrange("p (t h) -> p t h", t=NT)[:, :, :, None]
                                  .to_broadcast([P, NT, NLIN, DH]), ALU.mult).then_inc(s["qn_ready"], 1)

            def context_sums(b, r):
                if b is None:
                    return
                dve.wait_ge(s["ctx_ps"], b * 2 + r + 1)
                wide = 2 * LH * CW
                for u in range(4 * r, min(4 * r + 4, NU)):
                    src = bank(6 + u % 2)[0:LW, (u // 2 % 2) * wide:(u // 2 % 2 + 1) * wide]
                    if u:
                        last = dve.tensor_tensor(cum[:, u, :], src, cum[:, u - 1, :], ALU.add)
                    else:
                        dve.wait_ge(s["kk_ready"], b + 1)
                        last = dve.tensor_copy(cum[:, 0, :], src)
                    if u % 4 < 3 and u < NU - 1:
                        chain(b, last)
                last.then_inc(s["ctx_read"], 1)
                dve.wait_ge(s["ctx_read"], b * 2 + r + 1)

            def context_norm(b):
                if b is None:
                    return
                cum5 = cum.rearrange("p u (a h c) -> p (u a) h c", a=2, h=LH)
                chain(b, dve.tensor_scalar(ks, cum5[:, :, 0, DH], 1e-6, None, ALU.add))
                chain(b, dve.reciprocal(krec, ks))
                chain(b, dve.tensor_tensor(kmask2[:, :, :], kmask[:, :, :],
                                           krec[:, :, None].to_broadcast([LW, 2 * NU, LH]), ALU.mult))
                dve.tensor_tensor(ctxn.rearrange("p v (h c) -> p v h c", h=LH), cum5[:, :, :, 0:DH],
                                  kmask2[:, :, :, None].to_broadcast([LW, 2 * NU, LH, DH]),
                                  ALU.mult).then_inc(s["ctx_ready"], 1)

            def linear_out(b):
                if b is None:
                    return
                dve.wait_ge(s["ql_ps"], b * 2 + 2)
                chain(b, dve.memset(hT[0:LW, :, 0:BLK], 0.0))
                for a in range(2):
                    dve.wait_ge(s["lin_out_ps"], b * 2 + a + 1)
                    dve.tensor_copy(linT[:, a, BLK:], bank(6 + a)[0:LW, BLK:]).then_inc(s["linT_ready"], 1)

            def local_max(b, v):
                if b is None:
                    return
                dve.wait_ge(s["ls_ps"], b * NV + v + 1)
                c = slice(2 * v, 2 * v + 2)
                chain(b, dve.tensor_reduce(lmax[:, c], halves(bank(6 + v % 2)), AX, ALU.max))
                dve.tensor_scalar(lneg[:, c], lmax[:, c], -0.25, None, ALU.mult)\
                    .then_inc(s["lneg_ready"], 1)

            def local_norm(b, v):
                if b is None:
                    return
                dve.wait_ge(s["lexp"], b * 2 * NV + 2 * v + 2)
                c = slice(2 * v, 2 * v + 2)
                chain(b, dve.reciprocal(lrec[:, c], lden[:, c]))
                for u in range(2):
                    dve.tensor_scalar(lp[:, v % 2, u, :], lp[:, v % 2, u, :],
                                      lrec[:, 2 * v + u:2 * v + u + 1], None, ALU.mult)\
                        .then_inc(s["lnorm"], 1)

            def local_back(b, v):
                if b is None:
                    return
                dve.wait_ge(s["lt_ps"], b * NV + v + 1)
                dve.tensor_copy(lpT(v), bank(6 + v % 2)
                                .rearrange("p (u c n) -> p u c n", u=2, c=2)).then_inc(s["lt_ready"], 1)

            def final_tokens(b):
                if b is None:
                    return
                dve.wait_ge(s["bias_added"], b * NT + NT)
                for c in range(2):
                    dve.wait_ge(s["y_ps"], b * 2 + c + 1)
                    dve.tensor_tensor(x1[:, 2 * c:2 * c + 2, :], x1[:, 2 * c:2 * c + 2, :],
                                      halves(bank(7 - c)), ALU.add).then_inc(s["x1_ready"], 1)

            def body(a, b, more):
                at[0] = 0
                low_parts(a, 0)
                low_parts(a, 1)
                scale_shift(b, "b", 6, hT)
                low_parts(a, 2)
                low_parts(a, 3)
                swiglu(b, 0)
                for c in range(2):
                    values(a, c, va, 4, "v_ps", "va_ready")
                for m in range(1, NM):
                    swiglu(b, m)
                for n in range(2 * H):
                    maxima(a, n)
                    if n == 9:
                        conditioned(b, 0)
                    elif n == 17:
                        conditioned(b, 1)
                    elif n >= 25 and n % 2:
                        linear_parts(b, (n - 25) // 2)
                linear_keys(b)
                for c in range(2):
                    values(b, c, vb, 6, "lv_ps", "lv_ready")
                linear_queries(b)
                for step in range(NT * HG):
                    if step < 2:
                        context_sums(b, step)
                    if step == 1:
                        context_norm(b)
                        if b is None:
                            tables()
                    elif step == 4:
                        linear_out(b)
                    if LOCAL0 <= step < LOCAL0 + NV:
                        local_max(b, step - LOCAL0)
                    if step % 4 == 2 and step > 4:
                        reciprocals(a, step // 4 - 1)
                    if step % 4 == 3 and step > 4:
                        normalized(a, step // 4 - 1)
                    if LOCAL0 < step <= LOCAL0 + NV:
                        local_back(b, step - LOCAL0 - 1)
                    if LOCAL0 <= step < LOCAL0 + NV:
                        local_norm(b, step - LOCAL0)
                reciprocals(a, HG - 1)
                normalized(a, HG - 1)
                final_tokens(b)
                attended(a, 0)
                attended(a, 1)
                if more:
                    scale_shift(a + 1, "a", 0, hT_a)
                if b is not None:
                    assert at[0] == LINKS, at[0]

            scale_shift(0, "a", 0, hT_a)
            batches(dve, body)


def phase_route(nc, t, dr):
    R = 2 * NB * G
    RQ = NB * G
    with ExitStack() as ctx:
        def sb(name, shape, dt=F32):
            return ctx.enter_context(nc.sbuf_tensor(name, shape, dt))

        def sem(name):
            return ctx.enter_context(nc.semaphore(name))

        ps, co, cr, place = t["ps"], t["co"], t["cr"], t["place"]

        def const(name):
            if name in CR:
                return cr[:, CR[name][0]:CR[name][1]]
            return co[:, CO[name][0]:CO[name][1]]

        def bank(k):
            return ps[:, k * BANK:(k + 1) * BANK]

        ident = const("ident")
        logits = sb("logits", [R, L])
        left = sb("left", [R, L])
        top = sb("top", [R, NQ // 8, 8])
        limit = sb("limit", [R, 1])
        above = sb("above", [R, L])
        equal = sb("equal", [R, L])
        both = sb("both", [P, 2, NT, R])
        need = sb("need", [P, R])
        pick = sb("pick", [P, NT, R])
        rows = sb("rows", [R, L])
        sig = sb("sigmoids", [P, NT * R])
        sig_hi, sig_lo = (t["sig"][:, :, :, part].rearrange("p t r -> p (t r)") for part in range(2))

        loaded, vec, flags_ps, both_ready, count_ps, pick_ready, order_ps, place_ready, rows_ps, \
            rows_ready, stored = (sem(n) for n in (
                "r_loaded", "r_vec", "r_flags_ps", "r_both", "r_count_ps", "r_pick", "r_order_ps",
                "r_place", "r_rows_ps", "r_rows", "r_stored"))
        raw_loaded, high_ready, low_ready, rest_loaded = (
            sem(n) for n in ("r_raw_loaded", "r_high", "r_low", "r_rest_loaded"))
        columns_ps, tanh_ready, sig_ready, sig_hi_ready = (
            sem(n) for n in ("r_columns_ps", "r_tanh", "r_sig", "r_sig_hi"))

        block = ctx.enter_context(nc.Block())

        @block.sync
        def _(sp):
            for c in range(2):
                sp.dma_start(logits[RQ * c:RQ * c + RQ, :], dr["logits"][c].rearrange("b g n -> (b g) n"))\
                    .then_inc(loaded, 16)
            sp.dma_start(cr[:, :], dr["cr"]).then_inc(loaded, 16)
            for g in range(G):
                if g:
                    sp.wait_ge(low_ready, g)
                sp.dma_start(t["w_raw"][:, :], dr["ws"][g]).then_inc(raw_loaded, 16)
            sp.dma_start(t["wall"][:, :, :], dr["wc"].rearrange("g p n -> p g n")).then_inc(rest_loaded, 16)
            sp.dma_start(t["null"][:, :], dr["null"].to_broadcast([P, D])).then_inc(rest_loaded, 16)
            sp.wait_ge(rows_ready, 1)
            sp.dma_start(dr["place"], rows[0:RQ, :]).then_inc(stored, 16)
            sp.wait_ge(stored, 16)
            sp.wait_ge(rest_loaded, 32)

        @block.scalar
        def _(act):
            act.wait_ge(columns_ps, 1)
            act.activation(sig[:, :], bank(5)[:, 0:NT * R], ACT.Tanh, scale=0.5).then_inc(tanh_ready, 1)
            act.wait_ge(sig_ready, 1)
            act.activation(sig_hi, sig[:, :], ACT.Copy).then_inc(sig_hi_ready, 1)
            for g in range(G):
                act.wait_ge(raw_loaded, 16 * (g + 1))
                act.activation(t["w_hi"][:, g, :], t["w_raw"][:, :], ACT.Copy).then_inc(high_ready, 1)

        @block.gpsimd
        def _(pool):
            for g in range(G):
                pool.wait_ge(high_ready, g + 1)
                pool.tensor_tensor(t["w_lo"][:, g, :], t["w_raw"][:, :], t["w_hi"][:, g, :].bitcast(F32),
                                   ALU.subtract).then_inc(low_ready, 1)

        @block.vector
        def _(dve):
            n = [0]

            def link(ins):
                n[0] += 1
                ins.then_inc(vec, 1)
                dve.wait_ge(vec, n[0])

            dve.wait_ge(loaded, 48)
            link(dve.tensor_copy(left[:, :], logits[:, :]))
            dve.wait_ge(tanh_ready, 1)
            dve.tensor_scalar(sig[:, :], sig[:, :], 1.0, 0.5, ALU.add, ALU.mult).then_inc(sig_ready, 1)
            dve.wait_ge(sig_hi_ready, 1)
            dve.tensor_tensor(sig_lo, sig[:, :], sig_hi.bitcast(F32), ALU.subtract)
            for k in range(NQ // 8):
                r = R if k < NK // 8 else RQ
                link(dve.max(top[0:r, k, :], left[0:r, :]))
                if k < NQ // 8 - 1:
                    link(dve.match_replace(left[0:r, :], top[0:r, k, :], left[0:r, :], -3.0e38))
            dve.tensor_copy(limit[0:RQ, :], top[0:RQ, NQ // 8 - 1, 7:8])
            link(dve.tensor_copy(limit[RQ:R, :], top[RQ:R, NK // 8 - 1, 7:8]))
            link(dve.tensor_scalar(above[:, :], logits[:, :], limit[:, 0:1], None, ALU.is_gt))
            link(dve.tensor_scalar(equal[:, :], logits[:, :], limit[:, 0:1], None, ALU.is_equal))
            dve.wait_ge(flags_ps, 1)
            dve.tensor_copy(both[:, :, :, :], bank(0)[:, 0:2 * NT * R].rearrange("p (a t r) -> p a t r", a=2, t=NT))\
                .then_inc(both_ready, 1)
            dve.wait_ge(count_ps, 1)
            link(dve.tensor_tensor(need[:, :], const("kvec"), bank(1)[:, 0:R], ALU.subtract))
            link(dve.tensor_tensor(pick[:, :, :], bank(2)[:, 0:NT * R].rearrange("p (t r) -> p t r", t=NT),
                                   need[:, None, :].to_broadcast([P, NT, R]), ALU.is_lt))
            link(dve.tensor_tensor(pick[:, :, :], pick[:, :, :], both[:, 1, :, :], ALU.mult))
            dve.tensor_tensor(pick[:, :, :], pick[:, :, :], both[:, 0, :, :], ALU.add).then_inc(pick_ready, 1)
            dve.wait_ge(order_ps, 1)
            link(dve.scalar_tensor_tensor(place[:, :, :], bank(3)[:, 0:NT * R].rearrange("p (t r) -> p t r", t=NT),
                                          1.0, pick[:, :, :], ALU.add, ALU.mult))
            dve.tensor_scalar(place[:, :, :], place[:, :, :], 1.0, None, ALU.subtract).then_inc(place_ready, 1)
            dve.wait_ge(rows_ps, 1)
            dve.tensor_copy(rows[:, :], bank(4)[0:R, :]).then_inc(rows_ready, 1)

        @block.tensor
        def _(pe):
            pe.wait_ge(loaded, 48)
            for k in range(NT):
                last = pe.transpose(bank(5)[:, k * R:(k + 1) * R], logits[:, k * P:(k + 1) * P], ident[0:R, 0:R])
            last.then_inc(columns_ps, 1)
            pe.wait_ge(vec, 1 + 2 * (NQ // 8) - 1 + 3)
            for a, src in enumerate((above, equal)):
                for k in range(NT):
                    c = (a * NT + k) * R
                    last = pe.transpose(bank(0)[:, c:c + R], src[:, k * P:(k + 1) * P], ident[0:R, 0:R])
            last.then_inc(flags_ps, 1)

            def before(out, src):
                for k in range(NT):
                    for m in range(k + 1):
                        last = pe.matmul(out[:, k * R:(k + 1) * R], const("ones") if m < k else const("before"),
                                         src(m), start=(m == 0), stop=(m == k))
                return last

            pe.wait_ge(both_ready, 1)
            for k in range(NT):
                pe.matmul(bank(1)[:, 0:R], const("ones"), both[:, 0, k, :], start=(k == 0), stop=(k == NT - 1))
            before(bank(2), lambda m: both[:, 1, m, :]).then_inc(count_ps, 1)
            pe.wait_ge(pick_ready, 1)
            before(bank(3), lambda m: pick[:, m, :]).then_inc(order_ps, 1)
            pe.wait_ge(place_ready, 1)
            for k in range(NT):
                last = pe.transpose(bank(4)[0:R, k * P:(k + 1) * P], place[:, k, :], ident)
            last.then_inc(rows_ps, 1)


def phase_routed(nc, t, dr):
    with ExitStack() as ctx:
        def sb(name, shape, dt=F32):
            return ctx.enter_context(nc.sbuf_tensor(name, shape, dt))

        def sem(name):
            return ctx.enter_context(nc.semaphore(name))

        ps, co, cr, place = t["ps"], t["co"], t["cr"], t["place"]
        wall, null, w_hi, w_lo = t["wall"], t["null"], t["w_hi"], t["w_lo"]

        def const(name):
            if name in CR:
                return cr[:, CR[name][0]:CR[name][1]]
            return co[:, CO[name][0]:CO[name][1]]

        def bank(k, n=1):
            return ps[:, k * BANK:(k + n) * BANK]

        ident = const("ident")
        W2 = NQ + NK
        S1 = NK + 1
        nvw = sb("nvw", [FH, G, D])
        x1 = sb("c_x1", [P, NT, D])
        x2 = sb("c_x2", [P, NT, D])
        x2_hi = sb("x2_hi", [P, NT, D], F32R)
        x2_lo = sb("x2_lo", [P, NT, D], F32R)
        prow = sb("prow", [P, 2, L])
        pl = sb("pl", [P, NT, 2, G])
        sg = sb("sg", [P, NT, 2, G, 2], F32R)
        hot = sb("hot", [P, NT, W2], F32R)
        xg_hi = sb("xg_hi", [P, ND, W2], F32R)
        xg_lo = sb("xg_lo", [P, ND, W2], F32R)
        score = sb("score", [P, 2, 4])
        qT = sb("qT", [P, 2, NE, NQ])
        kT = sb("kT", [P, 2, NE, 2, S1])
        v = sb("v", [P, 2, E])
        p = sb("p", [P, 2, FH, S1])
        pT = sb("pT", [P, FH, NQ])
        pnT = sb("pnT", [FH, NQ])
        oT = sb("oT", [P, NE, NQ])
        oq_hi = sb("oq_hi", [P, 2, D], F32R)
        oq_lo = sb("oq_lo", [P, 2, D], F32R)
        hot_t = sb("hot_t", [P, 2, L], F32R)
        fmax = sb("fmax", [P, 16])
        fneg = sb("fneg", [P, 16])
        fden = sb("fden", [P, 16])
        frec = sb("frec", [P, 16])
        seen = sb("seen", [P, NT, G])
        cnt = sb("cnt", [P, 4, NT])

        def wg(g, name, k):
            a, b = WC[name]
            return wall[:, g, a:b].rearrange("p (k n) -> p k n", k=k)

        def ws(part, g, name):
            a, b = WS[name]
            return part[:, g, a:b].rearrange("p (k n) -> p k n", k=ND)

        s = {n: sem("c_" + n) for n in (
            "x1_loaded", "kT_clear", "nvw_ps", "nvw_ready", "x2_loaded", "x2_hi", "x2_lo",
            "place_back0", "place_back1", "pl_ready", "hot", "xg_ps", "xg_ready", "sg_ready", "score_ps",
            "score_ready", "q_ps", "k_ps", "v_ps", "qT_ready", "kT_ready", "v_ready", "s_ps",
            "fmax_link", "fneg_ready", "exp_done", "frec_link", "p_ready", "pT_ps", "pT_ready",
            "pn_ps", "pn_ready", "o_ps", "oT_ready", "out_ps", "oq_hi", "oq_lo", "hot_t", "sum_ps",
            "counts", "fin_link", "fin", "stored")}

        def need(eng, name, value):
            if not isinstance(value, int) or value > 0:
                eng.wait_ge(s[name], value)

        def batches(eng, body):
            body(0)
            with eng.Fori(1, NB - 1) as i:
                body(i)
            body(NB - 1)

        def is_first(i):
            return isinstance(i, int) and i == 0

        def is_last(i):
            return isinstance(i, int) and i == NB - 1

        def tiles(ap, i):
            one = ap[i:i + 1] if isinstance(i, int) else ap[bass.ds(i, 1)]
            return one.rearrange("a (t p) d -> p (a t) d", p=P)

        block = ctx.enter_context(nc.Block())

        @block.sync
        def _(sp):
            def load_x2(i):
                need(sp, "x2_lo", i)
                sp.dma_start(x2[:, :, :], tiles(dr["x2"], i)).then_inc(s["x2_loaded"], 16)

            def body(i):
                if not is_last(i):
                    load_x2(i + 1)
                for g in range(G):
                    n = i * G + g
                    need(sp, "hot_t", (n - 1) * 2)
                    row = dr["place"][n:n + 1] if isinstance(i, int) else dr["place"][bass.ds(n, 1)]
                    sp.dma_start(prow[:, g % 2, :], row.to_broadcast([P, L]))\
                        .then_inc(s[f"place_back{g % 2}"], 16)
                    if g == 1:
                        if not is_first(i):
                            need(sp, "fin", i * NT)
                            sp.dma_start(tiles(dr["out"], i - 1), x1[:, :, :]).then_inc(s["stored"], 16)
                            sp.wait_ge(s["stored"], i * 16)
                        sp.dma_start(x1[:, :, :], tiles(dr["x1"], i)).then_inc(s["x1_loaded"], 16)

            load_x2(0)
            batches(sp, body)
            sp.wait_ge(s["fin"], NB * NT)
            sp.dma_start(tiles(dr["out"], NB - 1), x1[:, :, :]).then_inc(s["stored"], 16)
            sp.wait_ge(s["stored"], NB * 16)

        @block.gpsimd
        def _(pool):
            pool.memset(kT[:, :, :, :, :], 0.0).then_inc(s["kT_clear"], 1)

            def body(i):
                for g in range(G):
                    n = i * G + g
                    for c in range(2):
                        pool.wait_ge(s["frec_link"], 2 * n + c + 1)
                        pool.tensor_tensor(p[:, c, :, :], p[:, c, :, :],
                                           frec[:, FH * c:FH * c + FH, None].to_broadcast([P, FH, S1]),
                                           ALU.mult).then_inc(s["p_ready"], 1)

            batches(pool, body)

        @block.scalar
        def _(act):
            def split_x2(i):
                act.wait_ge(s["x2_loaded"], i * 16 + 16)
                need(act, "xg_ps", i * 4 * G)
                act.activation(x2_hi[:, :, :], x2[:, :, :], ACT.Copy).then_inc(s["x2_hi"], 1)

            def null_keys(n, g):
                need(act, "s_ps", (n - 1) * 4)
                for hh in range(2):
                    r = slice(64 * hh, 64 * hh + 64)
                    act.activation(kT[r, g % 2, :, hh, NK:S1], wg(g, "nk", NE)[r, :, :], ACT.Copy)

            def gathered(n, d):
                for c, part in enumerate((xg_hi, xg_lo)):
                    act.wait_ge(s["xg_ps"], n * 4 + 2 * d + c + 1)
                    if d == 0 and c == 0:
                        need(act, "v_ps", n)
                    act.activation(part[:, d, :], bank(5 - c)[:, 0:W2], ACT.Copy).then_inc(s["xg_ready"], 1)

            def queries(n, g):
                for c in range(2):
                    act.wait_ge(s["q_ps"], n * 2 + c + 1)
                    act.activation(qT[:, g % 2, 2 * c:2 * c + 2, :], bank(4 + c).rearrange("p (a n) -> p a n", a=2),
                                   ACT.Copy).then_inc(s["qT_ready"], 1)

            def values(n, g):
                act.wait_ge(s["score_ready"], n + 1)
                act.wait_ge(s["v_ps"], n + 1)
                need(act, "o_ps", (n - 1) * 2)
                act.activation(v[:, g % 2, :], bank(4), ACT.Copy, scale=score[:, g % 2, 2:3])\
                    .then_inc(s["v_ready"], 1)

            def exps(n, u):
                act.wait_ge(s["fneg_ready"], n * 4 + u + 1)
                if u == 0:
                    need(act, "pT_ps", n * 4)
                    need(act, "pn_ps", n)
                for a in range(4):
                    h, c = 4 * (u % 2) + a, 4 * u + a
                    act.activation(p[:, u // 2, h, :],
                                   bank(2 * (u % 2) + a // 2)[:, (a % 2) * S1:(a % 2 + 1) * S1],
                                   ACT.Exp, scale=FD ** -0.5, bias=fneg[:, c:c + 1],
                                   accum_out=fden[:, c:c + 1]).then_inc(s["exp_done"], 1)

            def outputs(n, g):
                need(act, "sum_ps", n)
                for c in range(2):
                    act.wait_ge(s["out_ps"], n * 2 + c + 1)
                    act.activation(oq_hi[:, c, :], bank(5 - c)[:, 0:D], ACT.Copy,
                                   scale=score[:, g % 2, c:c + 1]).then_inc(s["oq_hi"], 1)

            act.wait_ge(s["nvw_ps"], 1)
            act.activation(nvw[:, :, :], bank(0, 2)[0:FH, :].rearrange("p (g n) -> p g n", g=G), ACT.Copy)\
                .then_inc(s["nvw_ready"], 1)
            act.wait_ge(s["kT_clear"], 1)
            split_x2(0)
            null_keys(0, 0)
            gathered(0, 0)
            gathered(0, 1)
            queries(0, 0)
            values(0, 0)

            def body(i):
                for g in range(G):
                    n = i * G + g
                    more = not (is_last(i) and g == G - 1)
                    exps(n, 0)
                    if g == G - 1 and more:
                        split_x2(i + 1)
                    if not (is_first(i) and g == 0):
                        outputs(n - 1, (g - 1) % G)
                    if more:
                        gathered(n + 1, 0)
                    exps(n, 1)
                    if more:
                        gathered(n + 1, 1)
                    exps(n, 2)
                    exps(n, 3)
                    if more:
                        null_keys(n + 1, (g + 1) % G)
                        queries(n + 1, (g + 1) % G)
                    act.wait_ge(s["pn_ps"], n + 1)
                    if more:
                        act.wait_ge(s["score_ready"], n + 2)
                    act.activation(pnT[:, :], bank(5)[0:FH, 0:NQ], ACT.Copy).then_inc(s["pn_ready"], 1)
                    if more:
                        values(n + 1, (g + 1) % G)
                    for c in range(2):
                        act.wait_ge(s["o_ps"], n * 2 + c + 1)
                        act.activation(oT[:, 2 * c:2 * c + 2, :], bank(5 - c).rearrange("p (a n) -> p a n", a=2),
                                       ACT.Copy).then_inc(s["oT_ready"], 1)

            batches(act, body)
            outputs(NB * G - 1, G - 1)

        @block.tensor
        def _(pe):
            def parts(out, pairs):
                for k, (a, b) in enumerate(pairs):
                    last = pe.matmul(out, a, b, start=(k == 0), stop=(k == len(pairs) - 1))
                return last

            def three(hi_lo, other):
                (ah, al), (bh, bl) = hi_lo, other
                return [(ah, bh), (ah, bl), (al, bh)]

            def gather(n, g, d, c, i):
                if d == 0 and c == 0:
                    need(pe, "v_ready", n)
                    need(pe, "score_ready", n)
                    need(pe, "oT_ready", (n - 1) * 2)
                    pe.wait_ge(s["hot"], (n + 1) * 8)
                    if g == 0:
                        pe.wait_ge(s["x2_lo"], i + 1)
                if d == 0:
                    need(pe, "oq_lo", (n - 2) * 2 + c + 1)
                part = (x2_hi, x2_lo)[c]
                if d == 1:
                    pe.wait_ge(s["xg_ready"], n * 4 + c + 1)
                for k in range(NT):
                    last = pe.matmul(bank(5 - c)[:, 0:W2], part[:, k, d * P:(d + 1) * P], hot[:, k, :],
                                     start=(k == 0), stop=(k == NT - 1))
                last.then_inc(s["xg_ps"], 1)

            def query_proj(n, g):
                pe.wait_ge(s["xg_ready"], n * 4 + 4)
                for c in range(2):
                    for b in range(2):
                        e = slice((2 * c + b) * P, (2 * c + b + 1) * P)
                        last = parts(bank(4 + c)[:, b * NQ:(b + 1) * NQ],
                                     [x for d in range(ND) for x in three(
                                         (ws(w_hi, g, "wq")[:, d, e], ws(w_lo, g, "wq")[:, d, e]),
                                         (xg_hi[:, d, 0:NQ], xg_lo[:, d, 0:NQ]))])
                    last.then_inc(s["q_ps"], 1)

            def key_proj(n, g):
                pe.wait_ge(s["qT_ready"], n * 2 + 1)
                for e in range(NE):
                    es = slice(e * P, (e + 1) * P)
                    last = parts(bank(4)[:, e * NK:(e + 1) * NK],
                                 [x for d in range(ND) for x in three(
                                     (ws(w_hi, g, "wk")[:, d, es], ws(w_lo, g, "wk")[:, d, es]),
                                     (xg_hi[:, d, NQ:W2], xg_lo[:, d, NQ:W2]))])
                last.then_inc(s["k_ps"], 1)

            def route_scores(n, g, c, i):
                pe.wait_ge(s["qT_ready"], n * 2 + 2)
                pe.wait_ge(s["sg_ready"], i + 1)
                for k in range(NT):
                    last = pe.matmul(bank(5)[:, 256 + 2 * c:258 + 2 * c], hot[:, k, c * P:(c + 1) * P],
                                     sg[:, k, c // 2, g, :], start=(k == 0), stop=(k == NT - 1))
                if c == 2:
                    last.then_inc(s["score_ps"], 1)

            def value_proj(n, g):
                pe.wait_ge(s["kT_ready"], n * 2 + 2)
                parts(bank(4), [x for d in range(ND) for x in three(
                    (xg_hi[:, d, NQ:W2], xg_lo[:, d, NQ:W2]),
                    (ws(w_hi, g, "wv")[:, d, :], ws(w_lo, g, "wv")[:, d, :]))]).then_inc(s["v_ps"], 1)

            def scores(n, g, u):
                if u == 0:
                    need(pe, "pT_ready", n * 4 - 2)
                    pe.wait_ge(s["qT_ready"], n * 2 + 2)
                    pe.wait_ge(s["kT_ready"], n * 2 + 2)
                elif u == 1:
                    need(pe, "pT_ready", n * 4)
                else:
                    pe.wait_ge(s["exp_done"], n * 16 + 4 * (u - 1))
                for b in range(2):
                    e = 2 * (u % 2) + b
                    last = pe.matmul(bank(2 * (u % 2) + b)[:, 0:2 * S1],
                                     qT[:, g % 2, e, (u // 2) * P:(u // 2 + 1) * P],
                                     kT[:, g % 2, e, :, :].rearrange("p a n -> p (a n)"), start=True, stop=True)
                last.then_inc(s["s_ps"], 1)

            def to_keys(n, c, b):
                pe.wait_ge(s["p_ready"], n * 2 + c + 1)
                pe.wait_ge(s["exp_done"], n * 16 + 12 + 4 * c)
                for a in range(4):
                    last = pe.transpose(bank(2 * c + b)[:, a * P:(a + 1) * P], p[:, c, 4 * b + a, 0:NK], ident)
                last.then_inc(s["pT_ps"], 1)

            def null_to_rows(n):
                pe.wait_ge(s["p_ready"], n * 2 + 2)
                for c in range(2):
                    last = pe.transpose(bank(5)[0:FH, c * P:(c + 1) * P], p[:, c, :, NK], ident)
                last.then_inc(s["pn_ps"], 1)

            def weigh(n, g):
                for c in range(2):
                    pe.wait_ge(s["pT_ready"], n * 4 + 4)
                    if c == 0:
                        pe.wait_ge(s["pn_ready"], n + 1)
                        pe.wait_ge(s["v_ready"], n + 1)
                    else:
                        pe.wait_ge(s["v_ready"], n + 1 if n_is_final(n) else n + 2)
                    for b in range(2):
                        for hh in range(2):
                            h = 2 * (2 * c + b) + hh
                            last = pe.matmul(bank(5 - c)[64 * hh:64 * hh + 64, b * NQ:(b + 1) * NQ],
                                             v[:, g % 2, h * FD:(h + 1) * FD], pT[:, h, :], start=True, stop=True)
                    last.then_inc(s["o_ps"], 1)

            def n_is_final(n):
                return isinstance(n, int) and n == NB * G - 1

            def output(n, g):
                pe.wait_ge(s["oT_ready"], n * 2 + 2)
                for c in range(2):
                    out = bank(5 - c)[:, 0:D]
                    for e in range(NE):
                        pe.matmul(out, oT[:, e, c * P:(c + 1) * P], wg(g, "wo", NE)[:, e, :],
                                  start=(e == 0), stop=False)
                    pe.matmul(out, pnT[:, c * P:(c + 1) * P], nvw[:, g, :], start=False, stop=True)\
                        .then_inc(s["out_ps"], 1)

            def scatter(n, g, done):
                if g == 0:
                    need(pe, "fin", done)
                pe.wait_ge(s["oq_lo"], n * 2 + 2)
                pe.wait_ge(s["hot_t"], n * 2 + 2)
                for k in range(NT):
                    for c in range(2):
                        for part in (oq_hi, oq_lo):
                            last = pe.matmul(bank(6 + k // 2)[:, (k % 2) * D:(k % 2 + 1) * D],
                                             hot_t[:, c, k * P:(k + 1) * P], part[:, c, :],
                                             start=(g == 0 and c == 0 and k % 2 == 0 and part is oq_hi),
                                             stop=(g == G - 1 and c == 1 and k % 2 == 1 and part is oq_lo),
                                             skip_group_check=True)
                last.then_inc(s["sum_ps"], 1)

            for g in range(G):
                for e in range(NE):
                    last = pe.matmul(bank(g // 2)[0:FH, (g % 2) * D:(g % 2 + 1) * D], wg(g, "nv", NE)[:, e, :],
                                     wg(g, "wo", NE)[:, e, :], start=(e == 0), stop=(e == NE - 1))
            last.then_inc(s["nvw_ps"], 1)
            pe.wait_ge(s["nvw_ready"], 1)
            for d in range(ND):
                for c in range(2):
                    gather(0, 0, d, c, 0)
            query_proj(0, 0)
            key_proj(0, 0)
            for c in range(3):
                route_scores(0, 0, c, 0)
            value_proj(0, 0)

            def body(i):
                for g in range(G):
                    n = i * G + g
                    g1 = (g + 1) % G
                    more = not (is_last(i) and g == G - 1)
                    scores(n, g, 0)
                    scores(n, g, 1)
                    if not (is_first(i) and g == 0):
                        output(n - 1, (g - 1) % G)
                    scores(n, g, 2)
                    if more:
                        gather(n + 1, g1, 0, 0, i + 1)
                        gather(n + 1, g1, 0, 1, i + 1)
                    if not (is_first(i) and g == 0):
                        scatter(n - 1, (g - 1) % G, i * NT)
                    if more:
                        gather(n + 1, g1, 1, 0, i + 1)
                        gather(n + 1, g1, 1, 1, i + 1)
                    scores(n, g, 3)
                    if more:
                        query_proj(n + 1, g1)
                    to_keys(n, 0, 0)
                    to_keys(n, 0, 1)
                    if more:
                        key_proj(n + 1, g1)
                        pe.wait_ge(s["qT_ready"], n * 2 + 4)
                    null_to_rows(n)
                    for c in range(3):
                        if more:
                            route_scores(n + 1, g1, c, i + 1 if g == G - 1 else i)
                        if c < 2:
                            to_keys(n, 1, c)
                    if more:
                        value_proj(n + 1, g1)
                    weigh(n, g)

            batches(pe, body)
            output(NB * G - 1, G - 1)
            scatter(NB * G - 1, G - 1, 0)

        @block.vector
        def _(dve):
            def places(i):
                need(dve, "hot", i * G * 8)
                need(dve, "counts", i * 5)
                cols = slice(i * G, i * G + G) if isinstance(i, int) else bass.ds(i * G, G)
                dve.tensor_copy(pl[:, :, :, :], place[:, :, :].rearrange("p t (c r) -> p t c r", c=2)
                                [:, :, :, cols]).then_inc(s["pl_ready"], 1)
                dve.wait_ge(s["pl_ready"], i + 1)

            def place_scores(i):
                need(dve, "score_ps", i * G)
                cols = slice(i * G, i * G + G) if isinstance(i, int) else bass.ds(i * G, G)
                dve.tensor_copy(sg[:, :, :, :, :].rearrange("p t c g a -> p (t c) g a"),
                                t["sig"][:, :, :, :].rearrange("p t (c r) a -> p (t c) r a", c=2)
                                [:, :, cols, :].bitcast(F32)).then_inc(s["sg_ready"], 1)

            def low_x2(i):
                dve.wait_ge(s["x2_hi"], i + 1)
                dve.tensor_tensor(x2_lo[:, :, :], x2[:, :, :], x2_hi[:, :, :].bitcast(F32), ALU.subtract)\
                    .then_inc(s["x2_lo"], 1)

            def counts(i):
                dve.tensor_scalar(seen[:, :, :], pl[:, :, 0, :], 0.0, None, ALU.is_ge).then_inc(s["counts"], 1)
                dve.wait_ge(s["counts"], i * 5 + 1)
                dve.tensor_reduce(cnt[:, 0, :], seen[:, :, :], AX, ALU.add).then_inc(s["counts"], 1)
                dve.wait_ge(s["counts"], i * 5 + 2)
                dve.tensor_scalar(cnt[:, 1, :], cnt[:, 0, :], 1e-5, None, ALU.max).then_inc(s["counts"], 1)
                dve.tensor_scalar(cnt[:, 3, :], cnt[:, 0, :], 0.0, None, ALU.is_equal).then_inc(s["counts"], 1)
                dve.wait_ge(s["counts"], i * 5 + 4)
                dve.reciprocal(cnt[:, 2, :], cnt[:, 1, :]).then_inc(s["counts"], 1)

            def one_hot(n, g):
                need(dve, "score_ps", n)
                for k in range(NT):
                    dve.tensor_scalar(hot[:, k, 0:NQ], const("iota"), pl[:, k, 0, g:g + 1], None,
                                      ALU.is_equal).then_inc(s["hot"], 1)
                    dve.tensor_scalar(hot[:, k, NQ:W2], const("iota")[:, 0:NK], pl[:, k, 1, g:g + 1], None,
                                      ALU.is_equal).then_inc(s["hot"], 1)

            def one_hot_back(n, g, i):
                dve.wait_ge(s[f"place_back{g % 2}"], i * 32 + (g // 2) * 16 + 16)
                need(dve, "sum_ps", n)
                for c in range(2):
                    dve.tensor_scalar(hot_t[:, c, :], prow[:, g % 2, :], const("part")[:, c:c + 1], None,
                                      ALU.is_equal).then_inc(s["hot_t"], 1)

            def keys(n, g):
                dve.wait_ge(s["k_ps"], n + 1)
                need(dve, "s_ps", (n - 1) * 4)
                for hh in range(2):
                    r = slice(64 * hh, 64 * hh + 64)
                    dve.tensor_copy(kT[r, g % 2, :, hh, 0:NK], bank(4)[r, :].rearrange("p (e n) -> p e n", e=NE))\
                        .then_inc(s["kT_ready"], 1)

            def route_scores(n, g):
                dve.wait_ge(s["score_ps"], n + 1)
                need(dve, "oq_lo", (n - 1) * 2)
                dve.tensor_reduce(score[:, g % 2, 0:3], bank(5)[:, 256:262].rearrange("p (c a) -> p c a", a=2),
                                  AX, ALU.add).then_inc(s["score_ready"], 1)

            def maxima(n, u):
                dve.wait_ge(s["s_ps"], n * 4 + u + 1)
                need(dve, "exp_done", n * 16 - 4 * (3 - u))
                dve.tensor_reduce(fmax[:, 4 * u:4 * u + 4].rearrange("p (a c) -> p a c", a=2),
                                  bank(2 * (u % 2), 2).rearrange("p (a n) -> p a n", a=2)[:, :, 0:2 * S1]
                                  .rearrange("p a (c n) -> p a c n", c=2), AX, ALU.max)\
                    .then_inc(s["fmax_link"], 1)
                dve.wait_ge(s["fmax_link"], n * 4 + u + 1)
                dve.tensor_scalar(fneg[:, 4 * u:4 * u + 4], fmax[:, 4 * u:4 * u + 4], -FD ** -0.5, None,
                                  ALU.mult).then_inc(s["fneg_ready"], 1)

            def reciprocals(n, c):
                dve.wait_ge(s["exp_done"], n * 16 + 8 * c + 8)
                need(dve, "p_ready", n * 2 - 1 + c)
                dve.reciprocal(frec[:, FH * c:FH * c + FH], fden[:, FH * c:FH * c + FH])\
                    .then_inc(s["frec_link"], 1)

            def turned(n, c):
                need(dve, "o_ps", n * 2)
                for b in range(2):
                    dve.wait_ge(s["pT_ps"], n * 4 + 2 * c + b + 1)
                    dve.tensor_copy(pT[:, 4 * b:4 * b + 4, c * P:(c + 1) * P],
                                    bank(2 * c + b).rearrange("p (a n) -> p a n", a=4)).then_inc(s["pT_ready"], 1)

            def low_outputs(n, g):
                for c in range(2):
                    dve.wait_ge(s["oq_hi"], n * 2 + c + 1)
                    dve.scalar_tensor_tensor(oq_lo[:, c, :], bank(5 - c)[:, 0:D],
                                             score[:, g % 2, c:c + 1], oq_hi[:, c, :].bitcast(F32),
                                             ALU.mult, ALU.subtract).then_inc(s["oq_lo"], 1)

            def finish(i):
                dve.wait_ge(s["x1_loaded"], i * 16 + 16)
                dve.wait_ge(s["sum_ps"], i * G + G)
                dve.wait_ge(s["counts"], i * 5 + 5)
                for k in range(NT):
                    dve.scalar_tensor_tensor(x1[:, k, :], null[:, :], cnt[:, 3, k:k + 1], x1[:, k, :],
                                             ALU.mult, ALU.add).then_inc(s["fin_link"], 1)
                for k in range(NT):
                    dve.wait_ge(s["fin_link"], i * NT + k + 1)
                    dve.scalar_tensor_tensor(x1[:, k, :], bank(6 + k // 2)[:, (k % 2) * D:(k % 2 + 1) * D],
                                             cnt[:, 2, k:k + 1], x1[:, k, :], ALU.mult, ALU.add)\
                        .then_inc(s["fin"], 1)

            places(0)
            one_hot(0, 0)
            place_scores(0)
            low_x2(0)
            keys(0, 0)
            route_scores(0, 0)
            one_hot(1, 1)

            def body(i):
                for g in range(G):
                    n = i * G + g
                    g1 = (g + 1) % G
                    more = not (is_last(i) and g == G - 1)
                    maxima(n, 0)
                    maxima(n, 1)
                    if g == G - 1 and more:
                        low_x2(i + 1)
                        place_scores(i + 1)
                    if not (is_first(i) and g == 0):
                        low_outputs(n - 1, (g - 1) % G)
                    maxima(n, 2)
                    reciprocals(n, 0)
                    maxima(n, 3)
                    if g == 0:
                        if not is_first(i):
                            finish(i - 1)
                        counts(i)
                    one_hot_back(n, g, i)
                    reciprocals(n, 1)
                    turned(n, 0)
                    if more:
                        keys(n + 1, g1)
                    turned(n, 1)
                    if more:
                        route_scores(n + 1, g1)
                    if g == G - 2 and not is_last(i):
                        places(i + 1)
                    if not (is_last(i) and g >= G - 2):
                        one_hot(n + 2, (g + 2) % G)

            batches(dve, body)
            low_outputs(NB * G - 1, G - 1)
            finish(NB - 1)


def build(nc, x, co_d, cr_d, cw_d, wa_d, wb_d, bo_d, ws_d, wc_d, null_d, out):
    def scratch(name, shape):
        return nc.dram_tensor(name, shape, F32).ap()

    dr = dict(x=x, co=co_d, cr=cr_d, cw=cw_d, wa=wa_d, wb=wb_d, bo=bo_d, ws=ws_d, wc=wc_d, null=null_d, out=out,
              parts=scratch("parts", (2, 2, D, L)), x1=scratch("x1_d", (NB, L, D)),
              x2=scratch("x2_d", (NB, L, D)), logits=scratch("logits_d", (2, NB, G, L)),
              place=scratch("place_d", (NB * G, L)))
    with ExitStack() as ctx:
        t = dict(ps=ctx.enter_context(nc.psum_tensor("ps", [P, 8 * BANK], F32)),
                 co=ctx.enter_context(nc.sbuf_tensor("co", [P, CO_N], F32)),
                 place=ctx.enter_context(nc.sbuf_tensor("place", [P, NT, 2 * NB * G], F32)))
        phase_dense(nc, t, dr)
        t["cr"] = ctx.enter_context(nc.sbuf_tensor("cr", [P, CR_N], F32))
        for name, shape, dt in (("wall", [P, G, WC_N], F32), ("null", [P, D], F32),
                                ("sig", [P, NT, 2 * NB * G, 2], F32R), ("w_hi", [P, G, WS_N], F32R), ("w_lo", [P, G, WS_N], F32R)):
            t[name] = ctx.enter_context(nc.sbuf_tensor(name, shape, dt))
        with nc.sbuf_tensor("w_raw", [P, WS_N], F32) as w_raw:
            t["w_raw"] = w_raw
            phase_route(nc, t, dr)
        phase_routed(nc, t, dr)




def by_tile(a):
    k = a.shape[0] // P
    return np.ascontiguousarray(a.reshape(k, P, a.shape[1]).transpose(1, 0, 2)).reshape(P, -1)


def strips_cols(a, heads):
    out = np.zeros((a.shape[0], heads, STRIP), np.float32)
    out[:, :, :DH] = a.reshape(a.shape[0], heads, DH)
    return out.reshape(a.shape[0], heads * STRIP)


def pack(cols, n, parts, lead=()):
    out = np.zeros((*lead, P, n), np.float32)
    for name, (a, b) in cols.items():
        v = parts[name]
        out[..., :v.shape[-2], a:b] = v
    return out


def kernel(**inputs):
    import concourse.bacc as bacc
    from concourse.bass_utils import run_bass_kernel_spmd

    f = {k: np.asarray(v) for k, v in inputs.items()}
    c, a, r = ({k[len(pre):]: v for k, v in f.items() if k.startswith(pre)}
               for pre in ("L0_cond_", "L0_attn_", "L0_ffn_"))
    wa = pack(WA, WA_N, dict(
        wq=by_tile(c["Wq"].T), wk=by_tile(c["Wk"].T), wv=by_tile(c["Wv"].T),
        wo=by_tile(strips_cols(c["Wo"], H).T), gate=by_tile(c["gate_w"].T), hid=by_tile(c["hid_w"].T),
        down=by_tile(c["out_w"].T)))
    lin = np.concatenate([a["Wq"][:, NLOC * DH:], a["Wk"][:, NLOC * DH:]], axis=1)
    wo_lin = a["Wo"][NLOC * DH:].reshape(2, LW, D).transpose(1, 0, 2).reshape(LW, 2 * D)
    wb = pack(WB, WB_N, dict(
        lq=by_tile(strips_cols(a["Wq"][:, :NLOC * DH], NLOC)),
        lk=by_tile(strips_cols(a["Wk"][:, :NLOC * DH], NLOC)), lin=by_tile(lin), wv=by_tile(a["Wv"]),
        wo_loc=strips_cols(np.ascontiguousarray(a["Wo"][:NLOC * DH].T), NLOC).T, wo_lin=wo_lin))
    wkv = r["w_kv"]
    nk, nv = r["null_kv"][:, :, :, 0, :]
    spread = np.zeros((G, FH, FD, FH), np.float32)
    for h in range(FH):
        spread[:, h, :, h] = nv[:, h]
    ws = np.stack([pack(WS, WS_N, dict(
        wq=by_tile(r["w_q"][g].T), wk=by_tile(wkv[g, :E].T), wv=by_tile(wkv[g, E:].T))) for g in range(G)])
    wc = np.stack([pack(WC, WC_N, dict(
        wo=by_tile(r["w_out"][g].T), nk=by_tile(nk[g].reshape(E, 1)),
        nv=by_tile(spread[g].reshape(E, FH)))) for g in range(G)])
    row, part = np.arange(P), np.arange(P)
    tri = row[None, :] > part[:, None]
    cq = f["cond_256"]
    ks = np.zeros((P, 2 * NB * G), np.float32)
    ks[:, :NB * G], ks[:, NB * G:] = NQ, NK
    co = pack(CO, CO_N, dict(
        ident=np.eye(P), causal=np.where(tri, -CBIG, 0.0), all=np.full((P, P), -CBIG),
        hmask=(part[:, None] // STRIP == np.arange(NLOC)), dsel=(part[:, None] == STRIP * np.arange(4) + DH),
        cmask=(part[:, None] % 64 == np.arange(64)), bmask=(part[:, None] // DH == np.arange(LH)),
        qleft=np.tile(cq.T, (2, 1)),
        qright=np.tile(f["L0_cond2_q_right"].T, (2, 1)),
        sg=np.tile(f["L0_cond2_spectral_gate"].reshape(64, 1), (2, 1)),
        sign=np.tile(np.array([1, -1, -1, -1]), (P, 1)),
        wr=by_tile(np.concatenate([r["w_qr"], r["w_kvr"]]).T),
        cb=np.concatenate([c[n].reshape(ND, P).T for n in ("g1b", "b1b", "g2b", "b2b")], axis=1),
        cond=cq.T))
    cr = pack(CR, CR_N, dict(iota=np.tile(np.arange(NQ), (P, 1)), part=part[:, None] + P * np.arange(2),
                             before=tri, ones=np.ones((P, P)), kvec=ks))
    cw = np.concatenate([c[n].T for n in ("g1w", "b1w", "g2w", "b2w")], axis=1)
    arrays = dict(x=f["x"], co=co, cr=cr, cw=cw, wa=wa, wb=wb, bo=a["bo"].reshape(1, D), ws=ws, wc=wc,
                  null=r["null_token"].reshape(1, D))
    arrays = {f"in_{k}": np.ascontiguousarray(v) for k, v in arrays.items()}

    nc = bacc.Bacc("TRN2", target_bir_lowering=False, num_devices=1)
    args = [nc.dram_tensor(k, v.shape, mybir.dt.from_np(v.dtype), kind="ExternalInput").ap()
            for k, v in arrays.items()]
    out = nc.dram_tensor("out", (NB, L, D), F32, kind="ExternalOutput").ap()
    build(nc, *args, out)
    got = run_bass_kernel_spmd(nc, [arrays], core_ids=[0])
    return got.results[0]["out"]
```

```python
from contextlib import ExitStack

import numpy as np
import concourse.bass as bass
from concourse import mybir

F32 = mybir.dt.float32
F32R = mybir.dt.float32r
BF16 = mybir.dt.bfloat16
ALU = mybir.AluOpType
ACT = mybir.ActivationFunctionType
AX = mybir.AxisListType.X

P = 128
NB, L, D = 8, 512, 256
NT, ND = L // P, D // P
H, DH = 16, 16
STRIP = 32
HG = H * STRIP // P
HID = 4 * D
NM = HID // P
NLOC, NLIN = 4, 12
LH = NLIN // 2
LW = LH * DH
BLK = 64
NU = L // BLK - 1
CW = DH + 1
G, NQ, NK = 4, 256, 128
FH, FD = 8, 64
E = FH * FD
NE = E // P
SROW = 64 + 3 * DH
KST = SROW + 1
NV = 2 * NLOC
EARLY = 6
LOCAL0 = 5
BANK = 512
CBIG = 1e30



def columns(parts):
    at, out = 0, {}
    for name, n in parts:
        out[name] = (at, at + n)
        at += n
    return out, at


WA, WA_N = columns([("wq", ND * D), ("wk", ND * D), ("wv", ND * D), ("wo", ND * D),
                    ("hid", ND * HID), ("down", NM * D), ("gate", ND * HID)])
WA_KEPT = WA["gate"][0]
WB, WB_N = columns([("lq", ND * P), ("lk", ND * P), ("lin", ND * 2 * NLIN * DH), ("wv", ND * D),
                    ("wo_loc", D), ("wo_lin", 2 * D)])
WS, WS_N = columns([("wq", ND * E), ("wk", ND * E), ("wv", ND * E)])
WC, WC_N = columns([("wo", NE * D), ("nk", NE), ("nv", NE * FH)])
CO, CO_N = columns([("ident", P), ("causal", P), ("all", P), ("hmask", NLOC), ("dsel", 8), ("odd", 2),
                    ("cmask", 64), ("bmask", LH), ("qleft", NB), ("qright", 4), ("sg", 1),
                    ("sign", 4), ("wr", ND * 2 * G), ("cb", 4 * ND), ("cond", NB)])
CR, CR_N = columns([("iota", NQ), ("part", 2), ("before", P), ("ones", P), ("kvec", 2 * NB * G)])
CW4 = 4 * D


def phase_dense(nc, t, dr):
    with ExitStack() as ctx:
        def sb(name, shape, dt=F32):
            return ctx.enter_context(nc.sbuf_tensor(name, shape, dt))

        def sem(name):
            return ctx.enter_context(nc.semaphore(name))

        ps = t["ps"]

        def bank(k, n=1):
            return ps[:, k * BANK:(k + n) * BANK]

        def halves(ap):
            return ap.rearrange("p (a n) -> p a n", a=2)

        co = t["co"]

        def const(name):
            return co[:, CO[name][0]:CO[name][1]]

        ident = const("ident")
        wa = sb("wa", [P, WA_KEPT])
        gate_hi = sb("gate_hi", [P, ND, HID], F32R)
        gate_lo = sb("gate_lo", [P, ND, HID], F32R)
        wb = sb("wb", [P, WB_N])
        bo = sb("bo", [P, D])
        stack_q = sb("stack_q", [KST, H, L], F32R)
        stack_k = sb("stack_k", [KST, H // 2, L], F32R)
        qk_hi = sb("qk_hi", [P, 2, L], F32R)
        qk_lo = sb("qk_lo", [P, 2, L], F32R)
        with nc.sbuf_tensor("gate_in", [P, 2, ND, L], F32R) as gate_in:
            hTb_hi, hTb_lo = gate_in[:, 0, :, :], gate_in[:, 1, :, :]
        pt = sb("pt", [P, 8 * L])
        big = sb("big", [P, NM * L])
        va = sb("va", [P, NT, H, STRIP])
        vb = sb("vb", [P, NT, H, STRIP])
        heads_t = sb("heads_t", [P, HG // 2, L])
        x_in = sb("x_in", [P, NT, D])
        x_next = sb("x_next", [P, NT, D])
        hn_a = sb("hn_a", [P, NT, D])
        xm = sb("xm", [P, NT, D])
        xc = sb("xc", [P, NT, D])
        x1 = sb("x1", [P, NT, D])
        hT = sb("hT", [P, ND, L])
        temp = sb("temp", [P, 2 * NU * (LH * CW + LW)])
        mrow = sb("mrow", [H, L], F32R)
        small = sb("small", [P, 436])
        causal_b = sb("causal_b", [P, P], BF16)
        all_b = sb("all_b", [P, P], BF16)
        ident_b = sb("ident_b", [P, P], BF16)
        rot = sb("rot", [P, ND, 4, 64])
        wc = sb("wc", [P, ND, 2 * G])

        def w(pack, cols, name, k):
            a, b = cols[name]
            return pack[:, a:b].rearrange("p (k n) -> p k n", k=k)

        wq, wk, wv = (w(wa, WA, n, ND) for n in ("wq", "wk", "wv"))
        wo, wdown = w(wa, WA, "wo", ND), w(wa, WA, "down", NM)
        whid = w(wa, WA, "hid", ND)
        blq, blk, blin, bwv = (w(wb, WB, n, ND) for n in ("lq", "lk", "lin", "wv"))
        bwo_loc = wb[:, WB["wo_loc"][0]:WB["wo_loc"][1]]
        bwo_lin = w(wb, WB, "wo_lin", 2)

        p_t = pt[:, :].rearrange("p (s j n) -> p s j n", s=2, j=4)
        hT_a = pt[:, 2 * NT * D:3 * NT * D].rearrange("p (d n) -> p d n", d=ND)
        hn_b = pt[:, 3 * NT * D:4 * NT * D].rearrange("p (t d) -> p t d", t=NT)
        gT = big[:, :].rearrange("p (m n) -> p m n", m=NM)
        lp = big[:, 0:1024].rearrange("p (s u n) -> p s u n", s=2, u=2)
        locT = big[:, 1024:1536]
        logit = big[0:2 * G, 1536:2048]
        q_e = big[:, 2048:2816].rearrange("p (t n) -> p t n", t=NT)
        k_e = big[:, 2816:3584].rearrange("p (t n) -> p t n", t=NT)
        lkT = big[:, 3584:4096]
        cw = big[0:64, 0:CW4]
        rot_t = big[:, CW4:CW4 + ND * D].rearrange("p (k i c) -> p k i c", k=ND, i=4)
        gate_raw = big[:, 2048:4096].rearrange("p (k n) -> p k n", k=ND)
        osb = qk_hi[:, :, :].bitcast(F32)
        rspread = qk_lo[:, 0, :].bitcast(F32)
        tg = temp[:, 1024:2048].rearrange("p (s n) -> p s n", s=2)
        k_pos = temp[:, 0:NT * NLIN * DH].rearrange("p (t n) -> p t n", t=NT)
        cum = temp[0:LW, 0:2 * NU * LH * CW].rearrange("p (u n) -> p u n", u=NU)
        ctxn = temp[0:LW, 2 * NU * LH * CW:].rearrange("p (v n) -> p v n", v=2 * NU)
        qlT = xc[0:LW, :, :].rearrange("p t n -> p (t n)").rearrange("p (a n) -> p a n", a=2)
        linT = hT[0:LW, :, :]

        def lqm(h):
            return (xm, x1)[h // 2][:, 2 * (h % 2):2 * (h % 2) + 2, :].rearrange("p t n -> p (t n)")

        def lpT(v):
            out = big[:, 2048 + v * L:2048 + (v + 1) * L] if v < 3 else temp[:, (v - 3) * L:(v - 2) * L]
            return out.rearrange("p (u c n) -> p u c n", u=2, c=2)
        x2 = xc
        tg2 = xc[:, :, :].rearrange("p (s a) n -> p s (a n)", s=2)
        mtok = small[:, 0:64].rearrange("p (t h) -> p t h", t=NT)
        ms, msn, inv, half = (small[:, 64 + 4 * k:68 + 4 * k] for k in range(4))
        rden = small[:, 280:312]
        eps = small[:, 420:424]
        ms_b, msn_b, inv_b = (small[:, 424 + 4 * k:428 + 4 * k] for k in range(3))
        gb = small[:, 96:160].rearrange("p (k b) -> p k b", b=NB)
        gbc = small[:, 160:168]
        lmax, lneg, lden, lrec = (small[:, 168 + 16 * k:184 + 16 * k] for k in range(4))
        qmx = qsum = small[:, 232:280]
        qrec = small[:, 328:376]
        ks = small[0:LW, 376:390]
        krec = small[0:LW, 390:404]
        nrm, lrot = small[:, 408:412], small[:, 412:416]
        rrot = small[:, 416:420]
        kmask = sb("kmask", [LW, 2 * NU, LH])
        kmask2 = big[0:LW, 0:2 * NU * LH].rearrange("p (v h) -> p v h", h=LH)
        coef = temp[:, P:P + 64].rearrange("p (m a b) -> p m a b", m=4, a=4)

        s = {n: sem(n) for n in (
            "consts", "w_first", "w_rest", "setup", "setup_pe", "setup_pool", "setup_act", "cleared", "link",
            "x_loaded", "next_loaded", "squares_a", "inv_a", "hn_a", "hTa_ps", "gbc_a", "hTa_ready",
            "qk_ps", "v_ps", "hi_ready", "lo_ready", "va_ready", "parts_stored", "stacked",
            "s_ps", "smax", "m_ps", "mrow_ready", "mrow_back", "st_ps", "exp_done", "pv_done",
            "osb_ready", "even_out", "odd_out", "den_ps", "rspread_ready", "rb_ps", "oT_ready", "ao_ps",
            "xm_ready",
            "x1_loaded", "squares_b", "inv_b", "hn_b", "hTb_ps", "gbc_b", "hTb_ready", "hTb_high", "hTb_low",
            "gh_ps", "tg_ready", "tg2_ready", "sg_done", "dn_ps", "xc_ready", "yT_ps",
            "yT_ready", "lqk_ps", "lqk_ready", "lin_ps", "k_parts", "lin_read", "lv_ps",
            "lv_ready", "ke_ready", "qe_ready", "kk_ready", "qn_ready", "ctx_ps", "ctx_read",
            "ctx_ready", "ql_ps", "ql_ready", "lin_out_ps", "linT_ready", "ls_ps", "lneg_ready",
            "lexp", "lnorm", "lt_ps", "lt_ready", "lo_ps", "locT_ready", "bias_added", "y_ps",
            "x1_ready", "x1T_ps", "x1T_ready", "x2_ps", "x2_ready", "lg_ps", "lg_ready",
            "x1_stored", "x2_lg_stored")}

        def need(eng, name, value):
            if not isinstance(value, int) or value > 0:
                eng.wait_ge(s[name], value)

        def batches(eng, body):
            body(0, None, True)
            with eng.Fori(0, NB - 2) as i:
                body(i + 1, i, True)
            body(NB - 1, NB - 2, False)
            body(None, NB - 1, False)

        def one(ap, i):
            return ap[i:i + 1] if isinstance(i, int) else ap[bass.ds(i, 1)]

        def tiles(ap, i):
            return one(ap, i).rearrange("a (t p) d -> p (a t) d", p=P)

        def early_scores(m):
            m -= NM - EARLY // 2
            return range(2 * m, 2 * m + 2) if m >= 0 else ()

        block = ctx.enter_context(nc.Block())

        @block.sync
        def _(sp):
            def load_x(a):
                need(sp, "xm_ready", a * 2)
                sp.dma_start(x_in[:, :, :], tiles(dr["x"], a)).then_inc(s["x_loaded"], 16)

            def load_next(a):
                need(sp, "hn_a", a * 4)
                sp.dma_start(x_next[:, :, :], tiles(dr["x"], a)).then_inc(s["next_loaded"], 16)

            def stacks(a):
                for o in range(2):
                    sp.wait_ge(s["hi_ready"], a * 4 + 2 * o + 2)
                    sp.dma_start(dr["parts"][o, 0].rearrange("(m p) n -> p m n", p=P),
                                 qk_hi[:, :, :].bitcast(F32)).then_inc(s["parts_stored"], 16)
                    sp.wait_ge(s["lo_ready"], a * 4 + 2 * o + 2)
                    sp.dma_start(dr["parts"][o, 1].rearrange("(m p) n -> p m n", p=P),
                                 qk_lo[:, :, :].bitcast(F32)).then_inc(s["parts_stored"], 16)
                    sp.wait_ge(s["parts_stored"], a * 64 + 32 * o + 32)
                    for r, part in enumerate(((0, 1, 0), (0, 0, 1))[o]):
                        for e in range(2):
                            row = 64 * e + DH * r
                            out = stack_k[row:row + DH, :, :] if o else stack_q[row:row + DH, e::2, :]
                            sp.dma_start(out.bitcast(F32), dr["parts"][o, part]
                                         .rearrange("(h e d) n -> e d h n", e=2, d=DH)[e])\
                                .then_inc(s["stacked"], 16)

            load_next(0)
            sp.dma_start(co[:, :], dr["co"]).then_inc(s["consts"], 16)
            sp.dma_start(cw[:, :], dr["cw"]).then_inc(s["consts"], 16)
            first = WA["wo"][0]
            sp.dma_start(wa[:, 0:first], dr["wa"][:, 0:first]).then_inc(s["w_first"], 16)
            load_x(0)
            sp.dma_start(wa[:, first:], dr["wa"][:, first:WA_KEPT]).then_inc(s["w_rest"], 16)
            sp.dma_start(big[:, 2048:4096], dr["wa"][:, WA_KEPT:]).then_inc(s["w_rest"], 16)
            sp.dma_start(wb[:, :], dr["wb"]).then_inc(s["w_rest"], 16)
            sp.dma_start(bo[:, :], dr["bo"].to_broadcast([P, D])).then_inc(s["w_rest"], 16)
            sp.wait_ge(s["cleared"], 3)

            def body(a, b, more):
                if b is not None and a is not None:
                    load_x(a)
                if more:
                    load_next(a + 1)
                if a is not None:
                    stacks(a)
                    sp.wait_ge(s["mrow_ready"], a + 1)
                    sp.dma_start(stack_q[SROW:SROW + 1, :, :].bitcast(F32), mrow[:, :].bitcast(F32))\
                        .then_inc(s["mrow_back"], 16)
                if b is not None:
                    sp.wait_ge(s["ls_ps"], b * NV + NV)
                    sp.dma_start(x1[:, :, :], tiles(dr["x"], b)).then_inc(s["x1_loaded"], 16)
                    sp.wait_ge(s["x1_ready"], b * 2 + 2)
                    sp.dma_start(tiles(dr["x1"], b), x1[:, :, :]).then_inc(s["x1_stored"], 16)
                if b is not None:
                    sp.wait_ge(s["x2_ready"], b * 2 + 2)
                    sp.dma_start(tiles(dr["x2"], b), x2[:, :, :]).then_inc(s["x2_lg_stored"], 16)
                    sp.wait_ge(s["lg_ready"], b + 1)
                    for c in range(2):
                        sp.dma_start(one(dr["logits"][c], b).rearrange("a g n -> (a g) n"),
                                     logit[G * c:G * c + G, :]).then_inc(s["x2_lg_stored"], 16)

            batches(sp, body)
            sp.wait_ge(s["x1_stored"], NB * 16)
            sp.wait_ge(s["x2_lg_stored"], NB * 48)

        @block.gpsimd
        def _(pool):
            pool.memset(eps, 1e-6).then_inc(s["setup_pool"], 1)
            pool.memset(half[:, :], -0.5).then_inc(s["setup_pool"], 1)
            pool.memset(va[:, :, :, :], 1.0).then_inc(s["setup_pool"], 1)
            pool.wait_ge(s["setup_pool"], 3)

            def inverse(i, side, mean, mean_eps, out):
                pool.wait_ge(s[f"squares_{side}"], i * 4 + 4)
                pool.tensor_tensor(mean_eps, mean, eps, ALU.add).then_inc(s[f"inv_{side}"], 1)
                pool.wait_ge(s[f"inv_{side}"], i * 2 + 1)
                pool.tensor_tensor(out, mean_eps, half, ALU.pow).then_inc(s[f"inv_{side}"], 1)

            def body(a, b, more):
                if more:
                    inverse(a + 1, "a", ms, msn, inv)
                if b is None:
                    pool.wait_ge(s["setup"], 2)
                    pool.tensor_tensor(nrm[:, 2:4], nrm[:, 0:2], half[:, 0:2], ALU.pow)\
                        .then_inc(s["setup_pool"], 1)
                if b is not None:
                    pool.wait_ge(s["x1_loaded"], b * 16 + 16)
                    for k in range(NT):
                        pool.tensor_tensor(x1[:, k, :], x1[:, k, :], bo[:, :], ALU.add)\
                            .then_inc(s["bias_added"], 1)
                if a is not None:
                    inverse(a, "b", ms_b, msn_b, inv_b)

            inverse(0, "a", ms, msn, inv)
            pool.memset(stack_q[:, :, :].bitcast(F32), 0.0).then_inc(s["cleared"], 1)
            pool.memset(vb[:, :, :, :], 1.0).then_inc(s["setup_pool"], 1)
            pool.wait_ge(s["w_rest"], 64)
            batches(pool, body)

        @block.scalar
        def _(act):
            def norm(i, side, src, out, mean, inverse):
                for k in range(NT):
                    act.activation(out[:, k, :], src[:, k, :], ACT.Square, scale=D ** -0.5,
                                   accum_out=mean[:, k:k + 1]).then_inc(s[f"squares_{side}"], 1)
                act.wait_ge(s[f"inv_{side}"], i * 2 + 2)
                for k in range(NT):
                    act.activation(out[:, k, :], src[:, k, :], ACT.Copy, scale=inverse[:, k:k + 1])\
                        .then_inc(s[f"hn_{side}"], 1)

            def norm_a(a):
                act.wait_ge(s["next_loaded"], a * 16 + 16)
                need(act, "hTa_ps", a * 2)
                norm(a, "a", x_next, hn_a, ms, inv)

            def norm_b(b):
                if b is None:
                    return
                act.wait_ge(s["xm_ready"], b * 2 + 2)
                norm(b, "b", xm, hn_b, ms_b, inv_b)

            def high_parts(a, o):
                if a is None:
                    return
                act.wait_ge(s["qk_ps"], a * 4 + o + 1)
                if o >= 2:
                    act.wait_ge(s["parts_stored"], a * 64 + 32)
                act.activation(qk_hi[:, o % 2, :], bank((2 + o) % 4), ACT.Copy).then_inc(s["hi_ready"], 1)

            def maxima_row(a):
                if a is None:
                    return
                act.wait_ge(s["m_ps"], a + 1)
                act.activation(mrow[:, :], bank(4)[0:H, :], ACT.Copy).then_inc(s["mrow_ready"], 1)

            def heads_out(a, g):
                if a is None:
                    return
                act.wait_ge(s["pv_done"], a * 16 + 4 * g + 4)
                if g >= 2:
                    act.wait_ge(s["den_ps"], a * 4 + g - 1)
                act.activation(osb[:, g % 2, :], bank(4), ACT.Copy).then_inc(s["osb_ready"], 1)
                if g % 2 == 0:
                    act.activation(heads_t[:, g // 2, :], bank(4), ACT.Copy, scale=const("odd")[:, 0:1])\
                        .then_inc(s["even_out"], 1)

            def exps(a, step):
                if a is None:
                    return
                for c in range(2):
                    u = 2 * step + c
                    act.wait_ge(s["st_ps"], a * 32 + u + 1)
                    if step >= 2 and c == 0:
                        act.wait_ge(s["pv_done"], a * 16 + step - 1)
                    act.activation(p_t[:, step % 2, 2 * c:2 * c + 2, :], halves(bank(2 * (u % 2), 2)),
                                   ACT.Exp, scale=0.25).then_inc(s["exp_done"], 1)

            def high_gate_input(b):
                if b is None:
                    return
                for d in range(ND):
                    act.wait_ge(s["hTb_ready"], b * 2 + d + 1)
                    act.activation(hTb_hi[:, d, :], hT[:, d, :], ACT.Copy).then_inc(s["hTb_high"], 1)

            def gate_tanh(b, m):
                if b is None:
                    return
                act.wait_ge(s["gh_ps"], b * 2 * NM + 2 * m + 1)
                if m >= 2:
                    act.wait_ge(s["tg2_ready"], b * NM + m - 1)
                act.activation(tg[:, m % 2, :], bank(6), ACT.Tanh, scale=0.5).then_inc(s["tg_ready"], 1)

            def turned(b, ps_name, ready):
                if b is None:
                    return
                for d in range(ND):
                    act.wait_ge(s[ps_name], b * 2 + d + 1)
                    act.activation(hT[:, d, :], bank(6 + d), ACT.Copy).then_inc(s[ready], 1)

            def local_qk(b):
                if b is None:
                    return
                act.wait_ge(s["lqk_ps"], b * 2 + 1)
                need(act, "x1_stored", b * 16)
                for h in range(NLOC):
                    act.activation(lqm(h), bank(6), ACT.Copy, scale=const("hmask")[:, h:h + 1])\
                        .then_inc(s["lqk_ready"], 1)
                act.wait_ge(s["lqk_ps"], b * 2 + 2)
                act.activation(lkT, bank(7), ACT.Copy).then_inc(s["lqk_ready"], 1)

            def linear_keys(b, u):
                if b is None:
                    return
                act.wait_ge(s["lin_ps"], b * NT + u + 1)
                k_ps = bank(6 + u % 2)[:, NLIN * DH:2 * NLIN * DH]
                act.activation(k_pos[:, u, :], k_ps, ACT.Relu)
                act.activation(k_e[:, u, :], k_ps, ACT.Relu, scale=-1.0).then_inc(s["k_parts"], 1)

            def key_exp(b):
                if b is None:
                    return
                act.wait_ge(s["k_parts"], b * NT + NT)
                act.activation(k_e, k_e, ACT.Exp, scale=-1.0).then_inc(s["ke_ready"], 1)

            def query_exp(b):
                if b is None:
                    return
                act.wait_ge(s["lin_read"], b * NT + NT)
                act.activation(q_e, q_e, ACT.Exp).then_inc(s["qe_ready"], 1)

            def linear_queries(b):
                if b is None:
                    return
                for a in range(2):
                    act.wait_ge(s["ql_ps"], b * 2 + a + 1)
                    act.activation(qlT[:, a, :], bank(6 + a)[0:LW, :], ACT.Copy).then_inc(s["ql_ready"], 1)

            def local_exp(b, v):
                if b is None:
                    return
                act.wait_ge(s["lneg_ready"], b * NV + v + 1)
                if v >= 2:
                    act.wait_ge(s["lt_ps"], b * NV + v - 1)
                for u in range(2):
                    c = 2 * v + u
                    act.activation(lp[:, v % 2, u, :], bank(6 + v % 2)[:, 2 * P * u:2 * P * u + 2 * P],
                                   ACT.Exp, scale=0.25, bias=lneg[:, c:c + 1],
                                   accum_out=lden[:, c:c + 1]).then_inc(s["lexp"], 1)

            def local_out(b):
                if b is None:
                    return
                act.wait_ge(s["lo_ps"], b + 1)
                act.activation(locT[:, :], bank(6), ACT.Copy).then_inc(s["locT_ready"], 1)

            def rotated(b):
                if b is None:
                    return
                for c in range(2):
                    act.wait_ge(s["x2_ps"], b * 2 + c + 1)
                    act.activation(x2[:, 2 * c:2 * c + 2, :], halves(bank(6 + c)), ACT.Copy)\
                        .then_inc(s["x2_ready"], 1)
                act.wait_ge(s["lg_ps"], b + 1)
                act.activation(logit[:, :], bank(5)[0:2 * G, :], ACT.Copy).then_inc(s["lg_ready"], 1)

            def body(a, b, more):
                high_parts(a, 0)
                high_parts(a, 1)
                high_gate_input(b)
                high_parts(a, 2)
                high_parts(a, 3)
                if b is None:
                    act.wait_ge(s["w_rest"], 64)
                    act.activation(gate_hi[:, :, :], gate_raw, ACT.Copy).then_inc(s["setup_act"], 1)
                for m in range(NM):
                    gate_tanh(b, m)
                if more:
                    norm_a(a + 1)
                turned(b, "yT_ps", "yT_ready")
                local_qk(b)
                for u in range(NT):
                    linear_keys(b, u)
                key_exp(b)
                maxima_row(a)
                query_exp(b)
                for step in range(NT * HG):
                    exps(a, step)
                    if step % 4 == 0 and step:
                        heads_out(a, step // 4 - 1)
                    if step == 3:
                        linear_queries(b)
                    if LOCAL0 <= step < LOCAL0 + NV:
                        local_exp(b, step - LOCAL0)
                heads_out(a, HG - 1)
                local_out(b)
                turned(b, "x1T_ps", "x1T_ready")
                norm_b(a)
                rotated(b)

            norm_a(0)
            act.wait_ge(s["consts"], 32)
            batches(act, body)

        @block.tensor
        def _(pe):
            def transposes(i, src, base, ready):
                for d in range(ND):
                    for k in range(NT):
                        last = pe.transpose(bank(base + d)[:, k * P:(k + 1) * P],
                                            src[:, k, d * P:(d + 1) * P], ident)
                    last.then_inc(s[ready], 1)

            def normed_a(a):
                if a is None:
                    return
                pe.wait_ge(s["hn_a"], a * 4 + 4)
                need(pe, "xm_ready", a * 2)
                transposes(a, hn_a, 0, "hTa_ps")

            def queries_keys(a, o):
                if a is None:
                    return
                pe.wait_ge(s["hTa_ready"], a * 2 + 2)
                for k in range(ND):
                    last = pe.matmul(bank((2 + o) % 4), (wq, wk)[o // 2][:, k, (o % 2) * P:(o % 2 + 1) * P],
                                     hT_a[:, k, :], start=(k == 0), stop=(k == ND - 1))
                last.then_inc(s["qk_ps"], 1)

            def values_a(a):
                if a is None:
                    return
                for c in range(2):
                    if c:
                        need(pe, "lg_ready", a - 1)
                    for b in range(2):
                        for k in range(ND):
                            last = pe.matmul(bank(4 + c)[:, b * D:(b + 1) * D],
                                             hT_a[:, k, (2 * c + b) * P:(2 * c + b + 1) * P], wv[:, k, :],
                                             start=(k == 0), stop=(k == ND - 1))
                    last.then_inc(s["v_ps"], 1)

            def scores(a, n):
                if a is None:
                    return
                h, c = n // 2, n % 2
                if n == 0:
                    pe.wait_ge(s["stacked"], a * 192 + 192)
                if n >= 2:
                    pe.wait_ge(s["smax"], a * 32 + n - 1)
                for b in range(2):
                    last = pe.matmul(bank(2 * (n % 2) + b),
                                     stack_q[0:SROW, h, (2 * c + b) * P:(2 * c + b + 1) * P],
                                     stack_k[0:SROW, h // 2, :], start=True, stop=True)
                last.then_inc(s["s_ps"], 1)

            def maxima(a):
                if a is None:
                    return
                pe.wait_ge(s["smax"], a * 32 + 32)
                pe.wait_ge(s["va_ready"], a * 4 + 4)
                for k in range(NT):
                    last = pe.transpose(bank(4)[0:H, k * P:(k + 1) * P], mtok[:, k, :], ident)
                last.then_inc(s["m_ps"], 1)

            def scores_less_max(a, step):
                if a is None:
                    return
                g, kt = step // 4, step % 4
                if step == 0:
                    pe.wait_ge(s["mrow_back"], a * 16 + 16)
                for c in range(2):
                    u = 2 * step + c
                    if u >= 2:
                        pe.wait_ge(s["exp_done"], a * 32 + u - 1)
                    for b in range(2):
                        h = 4 * g + 2 * c + b
                        last = pe.matmul(bank(2 * (u % 2) + b), stack_k[:, h // 2, kt * P:(kt + 1) * P],
                                         stack_q[:, h, :], start=True, stop=True)
                    last.then_inc(s["st_ps"], 1)

            def weigh(a, step):
                if a is None:
                    return
                g, kt = step // 4, step % 4
                pe.wait_ge(s["exp_done"], a * 32 + 2 * step + 2)
                if kt == 0 and g:
                    pe.wait_ge(s[("odd_out", "even_out")[g % 2]], a * 2 + (g + 1) // 2)
                for j in range(4):
                    last = pe.matmul(bank(4)[STRIP * j:STRIP * (j + 1), :],
                                     va[:, kt, 4 * g + j, :], p_t[:, step % 2, j, :],
                                     start=(kt == 0), stop=(kt == NT - 1))
                last.then_inc(s["pv_done"], 1)

            def sums(a, g):
                if a is None:
                    return
                pe.wait_ge(s["osb_ready"], a * 4 + g + 1)
                if g == 2:
                    pe.wait_ge(s["oT_ready"], a * 2 + 1)
                odd = g % 2
                for k in range(NT):
                    last = pe.matmul(bank(5)[:, 16 * odd + 4 * k:16 * odd + 4 * k + 4],
                                     osb[:, odd, k * P:(k + 1) * P], const("dsel")[:, 4 * odd:4 * odd + 4],
                                     start=True, stop=True)
                last.then_inc(s["den_ps"], 1)

            def spread(a, pair):
                if a is None:
                    return
                pe.wait_ge(s["rspread_ready"], a * 4 + 2 * pair + 2)
                for k in range(NT):
                    last = pe.matmul(bank(5)[:, k * P:(k + 1) * P],
                                     rspread[:, k * P:(k + 1) * P], ident, start=True, stop=True)
                last.then_inc(s["rb_ps"], 1)

            def output_a(a, c):
                if a is None:
                    return
                pe.wait_ge(s["oT_ready"], a * 2 + 2)
                for b in range(2):
                    k = 2 * c + b
                    for pair in range(HG // 2):
                        last = pe.matmul(bank(c)[:, b * D:(b + 1) * D],
                                         heads_t[:, pair, k * P:(k + 1) * P], wo[:, pair, :],
                                         start=(pair == 0), stop=(pair == HG // 2 - 1))
                last.then_inc(s["ao_ps"], 1)

            def normed_b(b):
                if b is None:
                    return
                pe.wait_ge(s["hn_b"], b * 4 + 4)
                need(pe, "x2_ready", b * 2)
                transposes(b, hn_b, 6, "hTb_ps")

            def gate_hidden(b, m):
                if b is None:
                    return
                if m == 0:
                    pe.wait_ge(s["hTb_low"], b * 2 + 2)
                else:
                    pe.wait_ge(s["tg2_ready"], b * NM + m)
                cols = slice(m * P, (m + 1) * P)
                terms = [x for k in range(ND) for x in ((gate_hi[:, k, cols], hTb_hi[:, k, :]),
                                                        (gate_hi[:, k, cols], hTb_lo[:, k, :]),
                                                        (gate_lo[:, k, cols], hTb_hi[:, k, :]))]
                for k, (wt, x) in enumerate(terms):
                    last = pe.matmul(bank(6), wt, x, start=(k == 0), stop=(k == len(terms) - 1))
                last.then_inc(s["gh_ps"], 1)
                if m:
                    pe.wait_ge(s["sg_done"], b * NM + m)
                for k in range(ND):
                    last = pe.matmul(bank(7), whid[:, k, cols], hT[:, k, :], start=(k == 0), stop=(k == ND - 1))
                last.then_inc(s["gh_ps"], 1)

            def down(b, piece):
                if b is None:
                    return
                if piece == 0:
                    pe.wait_ge(s["sg_done"], b * NM + NM)
                k, m0 = piece // 4, 2 * (piece % 4)
                for m in (m0, m0 + 1):
                    last = pe.matmul(bank(6 + k // 2)[:, (k % 2) * D:(k % 2 + 1) * D], gT[:, m, k * P:(k + 1) * P],
                                     wdown[:, m, :], start=(m == 0), stop=(m == NM - 1))
                if piece % 8 == 7:
                    last.then_inc(s["dn_ps"], 1)

            def conditioned(b):
                if b is None:
                    return
                pe.wait_ge(s["xc_ready"], b * 2 + 2)
                transposes(b, xc, 6, "yT_ps")

            def local_proj(b, o):
                if b is None:
                    return
                pe.wait_ge(s["yT_ready"], b * 2 + 2)
                for k in range(ND):
                    last = pe.matmul(bank(6 + o), (blq, blk)[o][:, k, :], hT[:, k, :],
                                     start=(k == 0), stop=(k == ND - 1))
                last.then_inc(s["lqk_ps"], 1)

            def linear_proj(b, u):
                if b is None:
                    return
                if u == 0:
                    pe.wait_ge(s["lqk_ready"], b * (NLOC + 1) + NLOC)
                elif u == 1:
                    pe.wait_ge(s["lqk_ready"], b * (NLOC + 1) + NLOC + 1)
                else:
                    pe.wait_ge(s["lin_read"], b * NT + u - 1)
                for k in range(ND):
                    last = pe.matmul(bank(6 + u % 2)[:, 0:2 * NLIN * DH], hT[:, k, u * P:(u + 1) * P],
                                     blin[:, k, :], start=(k == 0), stop=(k == ND - 1))
                last.then_inc(s["lin_ps"], 1)

            def values_b(b, c):
                if b is None:
                    return
                pe.wait_ge(s["lin_read"], b * NT + 3 + c)
                for h in range(2):
                    for k in range(ND):
                        last = pe.matmul(bank(6 + c)[:, h * D:(h + 1) * D],
                                         hT[:, k, (2 * c + h) * P:(2 * c + h + 1) * P], bwv[:, k, :],
                                         start=(k == 0), stop=(k == ND - 1))
                last.then_inc(s["lv_ps"], 1)

            def contexts(b, r):
                if b is None:
                    return
                if r == 0:
                    pe.wait_ge(s["lv_ready"], b * 2 + 2)
                    pe.wait_ge(s["kk_ready"], b + 1)
                else:
                    pe.wait_ge(s["ctx_read"], b * 2 + 1)
                for u in range(4 * r, min(4 * r + 4, NU)):
                    for a in range(2):
                        row = BLK * (u % 2)
                        c = (2 * (u // 2 % 2) + a) * LH * CW
                        last = pe.matmul(bank(6 + u % 2)[0:LW, c:c + LH * CW],
                                         k_e[row:row + BLK, u // 2, a * LW:(a + 1) * LW],
                                         vb[row:row + BLK, u // 2, NLOC + LH * a:NLOC + LH * (a + 1), 0:CW],
                                         start=True, stop=True)
                last.then_inc(s["ctx_ps"], 1)

            def linear_queries(b):
                if b is None:
                    return
                pe.wait_ge(s["qn_ready"], b + 1)
                pe.wait_ge(s["ctx_read"], b * 2 + 2)
                for a in range(2):
                    for k in range(NT):
                        last = pe.transpose(bank(6 + a)[0:LW, k * P:(k + 1) * P],
                                            q_e[:, k, a * LW:(a + 1) * LW], ident)
                    last.then_inc(s["ql_ps"], 1)

            def linear_out(b):
                if b is None:
                    return
                pe.wait_ge(s["ql_ready"], b * 2 + 2)
                pe.wait_ge(s["ctx_ready"], b + 1)
                for a in range(2):
                    for u in range(NU):
                        last = pe.matmul(bank(6 + a)[0:LW, BLK * (u + 1):BLK * (u + 2)],
                                         ctxn[:, 2 * u + a, :], qlT[:, a, BLK * (u + 1):BLK * (u + 2)],
                                         start=True, stop=True)
                    last.then_inc(s["lin_out_ps"], 1)

            def local_scores(b, v):
                if b is None:
                    return
                if v < 2:
                    pe.wait_ge(s["linT_ready"], b * 2 + v + 1)
                else:
                    pe.wait_ge(s["lt_ready"], b * NV + v - 1)
                for u in (2 * (v % 2), 2 * (v % 2) + 1):
                    out = bank(6 + v % 2)[:, 2 * P * (u % 2):2 * P * (u % 2 + 1)]
                    q = lqm(v // 2)[:, u * P:(u + 1) * P]
                    if u:
                        pe.matmul(out, q, lkT[:, (u - 1) * P:(u + 1) * P], start=True, stop=False)
                    else:
                        pe.matmul(out[:, 0:P], ident_b[:, :], all_b[:, :], start=True, stop=True)
                        pe.matmul(out[:, P:], q, lkT[:, 0:P], start=True, stop=False)
                    last = pe.matmul(out[:, P:], ident_b[:, :], causal_b[:, :], start=False, stop=True)
                last.then_inc(s["ls_ps"], 1)

            def local_transposes(b, v):
                if b is None:
                    return
                pe.wait_ge(s["lnorm"], b * 2 * NV + 2 * v + 2)
                for u in range(2):
                    for c in range(2):
                        last = pe.transpose(bank(6 + v % 2)[:, (2 * u + c) * P:(2 * u + c + 1) * P],
                                            lp[:, v % 2, u, c * P:(c + 1) * P], ident)
                last.then_inc(s["lt_ps"], 1)

            def local_out(b):
                if b is None:
                    return
                pe.wait_ge(s["lt_ready"], b * NV + NV)
                for u in range(NT):
                    for c in ((0, 1) if u else (1,)):
                        for h in range(NLOC):
                            last = pe.matmul(bank(6)[STRIP * h:STRIP * (h + 1), u * P:(u + 1) * P],
                                             vb[:, u - 1 + c, h, :], lpT(2 * h + u // 2)[:, u % 2, c, :],
                                             start=(c == 0 or u == 0), stop=(c == 1))
                last.then_inc(s["lo_ps"], 1)

            def output_b(b, c):
                if b is None:
                    return
                pe.wait_ge(s["locT_ready"], b + 1)
                for j in range(2):
                    k = 2 * c + j
                    out = bank(7 - c)[:, j * D:(j + 1) * D]
                    pe.matmul(out, locT[:, k * P:(k + 1) * P], bwo_loc, start=True, stop=False)
                    pe.matmul(out, linT[:, 0, k * P:(k + 1) * P], bwo_lin[0:LW, 0, :],
                              start=False, stop=False)
                    last = pe.matmul(out, linT[:, 1, k * P:(k + 1) * P], bwo_lin[0:LW, 1, :],
                                     start=False, stop=True)
                last.then_inc(s["y_ps"], 1)

            def final_tokens(b):
                if b is None:
                    return
                pe.wait_ge(s["x1_ready"], b * 2 + 2)
                transposes(b, x1, 6, "x1T_ps")

            def rotation(b):
                if b is None:
                    return
                pe.wait_ge(s["x1T_ready"], b * 2 + 2)
                for c in range(2):
                    for j in range(2):
                        k = 2 * c + j
                        for d in range(ND):
                            last = pe.matmul(bank(6 + c)[:, j * D:(j + 1) * D], hT[:, d, k * P:(k + 1) * P],
                                             rot[:, d, :, :].rearrange("p i c -> p (i c)"),
                                             start=(d == 0), stop=(d == ND - 1))
                    last.then_inc(s["x2_ps"], 1)

            def logits(b):
                if b is None:
                    return
                for d in range(ND):
                    last = pe.matmul(bank(5)[0:2 * G, :], wc[:, d, :], hT[:, d, :],
                                     start=(d == 0), stop=(d == ND - 1))
                last.then_inc(s["lg_ps"], 1)

            def routing_weights():
                pe.wait_ge(s["setup"], 3)
                wr = const("wr").rearrange("p (k n) -> p k n", k=ND)
                for d in range(ND):
                    for k in range(ND):
                        last = pe.matmul(bank(7)[:, d * 2 * G:(d + 1) * 2 * G],
                                         rot_t[:, k, :, :].rearrange("p i c -> p (i c)")[:, d * P:(d + 1) * P],
                                         wr[:, k, :], start=(k == 0), stop=(k == ND - 1))
                last.then_inc(s["setup_pe"], 1)
                pe.wait_ge(s["w_rest"], 64)

            def body(a, b, more):
                queries_keys(a, 0)
                queries_keys(a, 1)
                normed_b(b)
                queries_keys(a, 2)
                queries_keys(a, 3)
                values_a(a)
                for m in range(NM):
                    gate_hidden(b, m)
                    for n in early_scores(m):
                        scores(a, n)
                for n in range(EARLY, 2 * H):
                    if n < EARLY + 16:
                        down(b, n - EARLY)
                    scores(a, n)
                    if n == 24:
                        conditioned(b)
                    elif n in (26, 27):
                        local_proj(b, n - 26)
                    elif n >= 28:
                        linear_proj(b, n - 28)
                maxima(a)
                values_b(b, 0)
                values_b(b, 1)
                for step in range(NT * HG):
                    scores_less_max(a, step)
                    if step:
                        weigh(a, step - 1)
                    if step % 4 == 2 and step > 4:
                        sums(a, step // 4 - 1)
                    if step == 11:
                        spread(a, 0)
                    if step < 2:
                        contexts(b, step)
                    elif step == 3:
                        linear_queries(b)
                    elif step == 4:
                        linear_out(b)
                    if b is None and step == 1:
                        routing_weights()
                    if LOCAL0 <= step < LOCAL0 + NV:
                        local_scores(b, step - LOCAL0)
                    if LOCAL0 < step <= LOCAL0 + NV:
                        local_transposes(b, step - LOCAL0 - 1)
                weigh(a, NT * HG - 1)
                local_out(b)
                sums(a, HG - 1)
                output_b(b, 0)
                spread(a, 1)
                output_b(b, 1)
                output_a(a, 0)
                final_tokens(b)
                output_a(a, 1)
                rotation(b)
                if more:
                    normed_a(a + 1)
                logits(b)
                if b is None:
                    pe.wait_ge(s["setup"], 5)

            pe.wait_ge(s["consts"], 32)
            for c in range(4 * ND):
                last = pe.matmul(bank(7)[:, c * NB:(c + 1) * NB], cw[:, c * P:(c + 1) * P],
                                 co[0:64, CO["cond"][0]:CO["cond"][1]], start=True, stop=True)
            last.then_inc(s["setup_pe"], 1)
            normed_a(0)
            pe.wait_ge(s["w_first"], 16)
            batches(pe, body)

        @block.vector
        def _(dve):
            n_link = [0]

            def link(ins):
                n_link[0] += 1
                ins.then_inc(s["link"], 1)
                dve.wait_ge(s["link"], n_link[0])

            dve.memset(stack_k[32:64, :, :].bitcast(F32), 0.0).then_inc(s["cleared"], 1)
            dve.memset(stack_k[96:KST, :, :].bitcast(F32), -1.0).then_inc(s["cleared"], 1)
            dve.wait_ge(s["consts"], 32)
            dve.wait_ge(s["setup_pe"], 1)
            link(dve.tensor_tensor(gb, bank(7)[:, 0:4 * ND * NB].rearrange("p (k b) -> p k b", b=NB),
                                   const("cb")[:, :, None].to_broadcast([P, 4 * ND, NB]), ALU.add))

            def tables():
                dve.wait_ge(s["setup_act"], 1)
                dve.tensor_tensor(gate_lo[:, :, :], gate_raw, gate_hi[:, :, :].bitcast(F32), ALU.subtract)
                ql, qr = const("qleft"), const("qright")
                link(dve.tensor_tensor(temp[:, 0:NB], ql, ql, ALU.mult))
                link(dve.tensor_tensor(temp[:, NB:NB + 4], qr, qr, ALU.mult))
                link(dve.tensor_reduce(nrm[:, 0:1], temp[:, 0:NB], AX, ALU.add))
                link(dve.tensor_reduce(nrm[:, 1:2], temp[:, NB:NB + 4], AX, ALU.add))
                dve.tensor_scalar(nrm[:, 0:1], nrm[:, 0:1], 1e-8, None, ALU.add).then_inc(s["setup"], 1)
                dve.tensor_scalar(nrm[:, 1:2], nrm[:, 1:2], 1e-8, None, ALU.add).then_inc(s["setup"], 1)
                dve.wait_ge(s["setup_pool"], 5)
                link(dve.tensor_scalar(lrot, ql[:, 0:4], nrm[:, 2:3], None, ALU.mult))
                link(dve.tensor_scalar(rrot, qr, nrm[:, 3:4], const("sg"), ALU.mult, ALU.mult))
                link(dve.tensor_tensor(rrot, rrot, const("sign"), ALU.mult))
                w_, x_, y_, z_ = range(4)
                left = (((w_, 1), (x_, -1), (y_, -1), (z_, -1)), ((x_, 1), (w_, 1), (z_, -1), (y_, 1)),
                        ((y_, 1), (z_, 1), (w_, 1), (x_, -1)), ((z_, 1), (y_, -1), (x_, 1), (w_, 1)))
                right = (((w_, 1), (x_, -1), (y_, -1), (z_, -1)), ((x_, 1), (w_, 1), (z_, 1), (y_, -1)),
                         ((y_, 1), (z_, -1), (w_, 1), (x_, 1)), ((z_, 1), (y_, 1), (x_, -1), (w_, 1)))
                for m, (table, src) in enumerate(((left, lrot), (right, rrot))):
                    for a in range(4):
                        for b in range(4):
                            q, sgn = table[a][b]
                            last = dve.tensor_scalar(coef[:, m, a, b:b + 1], src[:, q:q + 1], float(sgn), None, ALU.mult)
                link(last)
                for k in range(4):
                    o = coef[:, 2 if k == 0 else 3, :, :]
                    link(dve.tensor_tensor(o, coef[:, 0, :, k:k + 1].to_broadcast([P, 4, 4]),
                                           coef[:, 1, k:k + 1, :].to_broadcast([P, 4, 4]), ALU.mult))
                    if k:
                        link(dve.tensor_tensor(coef[:, 2, :, :], coef[:, 2, :, :], coef[:, 3, :, :], ALU.add))
                for k in range(ND):
                    for hh in range(2):
                        p = slice(64 * hh, 64 * hh + 64)
                        j = 2 * k + hh
                        cm = co[p, CO["cmask"][0]:CO["cmask"][1]]
                        for o in range(4):
                            dve.tensor_scalar(rot[p, k, o, :], cm, coef[p, 2, o, j:j + 1], None, ALU.mult)
                            last = dve.tensor_scalar(rot_t[p, k, o, :], cm, coef[p, 2, j, o:o + 1], None, ALU.mult)
                last.then_inc(s["setup"], 1)
                dve.wait_ge(s["setup_pe"], 2)
                dve.tensor_copy(wc[:, :, :], bank(7)[:, 0:4 * G].rearrange("p (k n) -> p k n", k=ND))\
                    .then_inc(s["setup"], 1)
                link(dve.tensor_copy(kmask[:, :, :], co[0:LW, None, CO["bmask"][0]:CO["bmask"][1]]
                                     .to_broadcast([LW, 2 * NU, LH])))
                dve.tensor_copy(causal_b[:, :], const("causal"))
                dve.tensor_copy(all_b[:, :], const("all"))
                dve.tensor_copy(ident_b[:, :], ident).then_inc(s["setup"], 1)

            LINKS = 31
            at = [0]

            def chain(b, ins):
                at[0] += 1
                ins.then_inc(s["link"], 1)
                dve.wait_ge(s["link"], b * LINKS + n_link[0] + at[0])

            def scale_shift(i, side, base, out):
                if i is None:
                    return
                c0 = 0 if side == "a" else 4
                need(dve, f"hT{side}_ready", i * 2)
                cols = slice(i, i + 1) if isinstance(i, int) else bass.ds(i, 1)
                dve.tensor_copy(gbc[:, c0:c0 + 4], gb[:, c0:c0 + 4, cols].rearrange("p k b -> p (k b)"))\
                    .then_inc(s[f"gbc_{side}"], 1)
                dve.wait_ge(s[f"gbc_{side}"], i + 1)
                for d in range(ND):
                    dve.wait_ge(s[f"hT{side}_ps"], i * 2 + d + 1)
                    dve.tensor_scalar(out[:, d, :], bank(base + d), gbc[:, c0 + d:c0 + d + 1],
                                      gbc[:, c0 + 2 + d:c0 + 3 + d], ALU.mult, ALU.add)\
                        .then_inc(s[f"hT{side}_ready"], 1)

            def values_a(a, c):
                if a is None:
                    return
                dve.wait_ge(s["v_ps"], a * 2 + c + 1)
                for odd in range(2):
                    dve.tensor_copy(va[:, 2 * c:2 * c + 2, :, :].rearrange("p t (g o j) d -> p (t g) o j d", g=2, o=2)
                                    [:, :, odd, :, DH * odd:DH * odd + DH],
                                    bank(4 + c).rearrange("p (t o j d) -> p t o j d", t=4, o=2, j=4)[:, :, odd, :, :])\
                        .then_inc(s["va_ready"], 1)

            def values(i, c, buf, base, ps_name, ready):
                if i is None:
                    return
                dve.wait_ge(s[ps_name], i * 2 + c + 1)
                dve.tensor_copy(buf[:, 2 * c:2 * c + 2, :, 0:DH],
                                bank(base + c).rearrange("p (t h d) -> p t h d", t=2, h=H))\
                    .then_inc(s[ready], 1)

            def low_parts(a, o):
                if a is None:
                    return
                dve.wait_ge(s["hi_ready"], a * 4 + o + 1)
                if o >= 2:
                    dve.wait_ge(s["parts_stored"], a * 64 + 32)
                dve.tensor_tensor(qk_lo[:, o % 2, :], bank((2 + o) % 4), qk_hi[:, o % 2, :].bitcast(F32),
                                  ALU.subtract).then_inc(s["lo_ready"], 1)

            def maxima(a, n):
                if a is None:
                    return
                dve.wait_ge(s["s_ps"], a * 32 + n + 1)
                dve.tensor_reduce(mtok[:, 2 * (n % 2):2 * (n % 2) + 2, n // 2], halves(bank(2 * (n % 2), 2)),
                                  AX, ALU.max).then_inc(s["smax"], 1)

            def odd_out(a, g):
                if a is None:
                    return
                dve.wait_ge(s["osb_ready"], a * 4 + g + 1)
                dve.wait_ge(s["even_out"], a * 2 + g // 2 + 1)
                dve.scalar_tensor_tensor(heads_t[:, g // 2, :], bank(4), const("odd")[:, 1:2],
                                         heads_t[:, g // 2, :], ALU.mult, ALU.add).then_inc(s["odd_out"], 1)

            def reciprocals(a, pair):
                if a is None:
                    return
                dve.wait_ge(s["den_ps"], a * 4 + 2 * pair + 2)
                dve.reciprocal(rden, bank(5)[:, 0:32]).then_inc(s["rspread_ready"], 1)
                dve.wait_ge(s["rspread_ready"], a * 4 + 2 * pair + 1)
                dve.tensor_copy(rspread.rearrange("p (c o n) -> p c o n", o=2, n=DH),
                                rden.rearrange("p (o c) -> p c o", o=2)[:, :, :, None].to_broadcast([P, 16, 2, DH]))\
                    .then_inc(s["rspread_ready"], 1)

            def normalized(a, pair):
                if a is None:
                    return
                dve.wait_ge(s["rb_ps"], a * 2 + pair + 1)
                dve.wait_ge(s["odd_out"], a * 2 + pair + 1)
                dve.tensor_tensor(heads_t[:, pair, :], heads_t[:, pair, :], bank(5), ALU.mult)\
                    .then_inc(s["oT_ready"], 1)

            def attended(a, c):
                if a is None:
                    return
                dve.wait_ge(s["ao_ps"], a * 2 + c + 1)
                dve.wait_ge(s["x_loaded"], a * 16 + 16)
                need(dve, "xc_ready", a * 2)
                dve.tensor_tensor(xm[:, 2 * c:2 * c + 2, :], x_in[:, 2 * c:2 * c + 2, :],
                                  halves(bank(c)), ALU.add).then_inc(s["xm_ready"], 1)

            def low_gate_input(b):
                if b is None:
                    return
                for d in range(ND):
                    dve.wait_ge(s["hTb_high"], b * 2 + d + 1)
                    dve.tensor_tensor(hTb_lo[:, d, :], hT[:, d, :], hTb_hi[:, d, :].bitcast(F32), ALU.subtract)\
                        .then_inc(s["hTb_low"], 1)

            def swiglu(b, m):
                if b is None:
                    return
                dve.wait_ge(s["tg_ready"], b * NM + m + 1)
                if m >= 2:
                    dve.wait_ge(s["sg_done"], b * NM + m - 1)
                if m == 0:
                    need(dve, "x2_lg_stored", b * 48)
                dve.scalar_tensor_tensor(tg2[:, m % 2, :], tg[:, m % 2, :], 1.0, bank(6),
                                         ALU.add, ALU.mult).then_inc(s["tg2_ready"], 1)
                dve.wait_ge(s["tg2_ready"], b * NM + m + 1)
                dve.wait_ge(s["gh_ps"], b * 2 * NM + 2 * m + 2)
                dve.scalar_tensor_tensor(gT[:, m, :], tg2[:, m % 2, :], 0.5, bank(7),
                                         ALU.mult, ALU.mult).then_inc(s["sg_done"], 1)

            def conditioned(b, c):
                if b is None:
                    return
                dve.wait_ge(s["dn_ps"], b * 2 + c + 1)
                dve.tensor_tensor(xc[:, 2 * c:2 * c + 2, :], xm[:, 2 * c:2 * c + 2, :],
                                  halves(bank(6 + c)), ALU.add).then_inc(s["xc_ready"], 1)

            def linear_parts(b, u):
                if b is None:
                    return
                dve.wait_ge(s["k_parts"], b * NT + u + 1)
                q_ps = bank(6 + u % 2)[:, 0:NLIN * DH].rearrange("p (h d) -> p h d", d=DH)
                m = qmx[:, NLIN * u:NLIN * (u + 1)]
                chain(b, dve.tensor_reduce(m, q_ps, AX, ALU.max))
                dve.tensor_tensor(q_e[:, u, :].rearrange("p (h d) -> p h d", d=DH), q_ps,
                                  m[:, :, None].to_broadcast([P, NLIN, DH]), ALU.subtract)\
                    .then_inc(s["lin_read"], 1)

            def linear_keys(b):
                if b is None:
                    return
                dve.wait_ge(s["ke_ready"], b + 1)
                dve.tensor_tensor(k_e, k_pos, k_e, ALU.add).then_inc(s["kk_ready"], 1)

            def linear_queries(b):
                if b is None:
                    return
                q4 = q_e.rearrange("p t (h d) -> p t h d", d=DH)
                dve.wait_ge(s["qe_ready"], b + 1)
                chain(b, dve.tensor_reduce(qsum, q4, AX, ALU.add))
                chain(b, dve.reciprocal(qrec, qsum))
                dve.tensor_tensor(q4, q4, qrec.rearrange("p (t h) -> p t h", t=NT)[:, :, :, None]
                                  .to_broadcast([P, NT, NLIN, DH]), ALU.mult).then_inc(s["qn_ready"], 1)

            def context_sums(b, r):
                if b is None:
                    return
                dve.wait_ge(s["ctx_ps"], b * 2 + r + 1)
                wide = 2 * LH * CW
                for u in range(4 * r, min(4 * r + 4, NU)):
                    src = bank(6 + u % 2)[0:LW, (u // 2 % 2) * wide:(u // 2 % 2 + 1) * wide]
                    if u:
                        last = dve.tensor_tensor(cum[:, u, :], src, cum[:, u - 1, :], ALU.add)
                    else:
                        dve.wait_ge(s["kk_ready"], b + 1)
                        last = dve.tensor_copy(cum[:, 0, :], src)
                    if u % 4 < 3 and u < NU - 1:
                        chain(b, last)
                last.then_inc(s["ctx_read"], 1)
                dve.wait_ge(s["ctx_read"], b * 2 + r + 1)

            def context_norm(b):
                if b is None:
                    return
                cum5 = cum.rearrange("p u (a h c) -> p (u a) h c", a=2, h=LH)
                chain(b, dve.tensor_scalar(ks, cum5[:, :, 0, DH], 1e-6, None, ALU.add))
                chain(b, dve.reciprocal(krec, ks))
                chain(b, dve.tensor_tensor(kmask2[:, :, :], kmask[:, :, :],
                                           krec[:, :, None].to_broadcast([LW, 2 * NU, LH]), ALU.mult))
                dve.tensor_tensor(ctxn.rearrange("p v (h c) -> p v h c", h=LH), cum5[:, :, :, 0:DH],
                                  kmask2[:, :, :, None].to_broadcast([LW, 2 * NU, LH, DH]),
                                  ALU.mult).then_inc(s["ctx_ready"], 1)

            def linear_out(b):
                if b is None:
                    return
                dve.wait_ge(s["ql_ps"], b * 2 + 2)
                chain(b, dve.memset(hT[0:LW, :, 0:BLK], 0.0))
                for a in range(2):
                    dve.wait_ge(s["lin_out_ps"], b * 2 + a + 1)
                    dve.tensor_copy(linT[:, a, BLK:], bank(6 + a)[0:LW, BLK:]).then_inc(s["linT_ready"], 1)

            def local_max(b, v):
                if b is None:
                    return
                dve.wait_ge(s["ls_ps"], b * NV + v + 1)
                c = slice(2 * v, 2 * v + 2)
                chain(b, dve.tensor_reduce(lmax[:, c], halves(bank(6 + v % 2)), AX, ALU.max))
                dve.tensor_scalar(lneg[:, c], lmax[:, c], -0.25, None, ALU.mult)\
                    .then_inc(s["lneg_ready"], 1)

            def local_norm(b, v):
                if b is None:
                    return
                dve.wait_ge(s["lexp"], b * 2 * NV + 2 * v + 2)
                c = slice(2 * v, 2 * v + 2)
                chain(b, dve.reciprocal(lrec[:, c], lden[:, c]))
                for u in range(2):
                    dve.tensor_scalar(lp[:, v % 2, u, :], lp[:, v % 2, u, :],
                                      lrec[:, 2 * v + u:2 * v + u + 1], None, ALU.mult)\
                        .then_inc(s["lnorm"], 1)

            def local_back(b, v):
                if b is None:
                    return
                dve.wait_ge(s["lt_ps"], b * NV + v + 1)
                dve.tensor_copy(lpT(v), bank(6 + v % 2)
                                .rearrange("p (u c n) -> p u c n", u=2, c=2)).then_inc(s["lt_ready"], 1)

            def final_tokens(b):
                if b is None:
                    return
                dve.wait_ge(s["bias_added"], b * NT + NT)
                for c in range(2):
                    dve.wait_ge(s["y_ps"], b * 2 + c + 1)
                    dve.tensor_tensor(x1[:, 2 * c:2 * c + 2, :], x1[:, 2 * c:2 * c + 2, :],
                                      halves(bank(7 - c)), ALU.add).then_inc(s["x1_ready"], 1)

            def body(a, b, more):
                at[0] = 0
                low_parts(a, 0)
                low_parts(a, 1)
                scale_shift(b, "b", 6, hT)
                low_gate_input(b)
                low_parts(a, 2)
                low_parts(a, 3)
                for c in range(2):
                    values_a(a, c)
                for m in range(NM):
                    swiglu(b, m)
                    for n in early_scores(m):
                        maxima(a, n)
                for n in range(EARLY, 2 * H):
                    maxima(a, n)
                    if n == EARLY + 9:
                        conditioned(b, 0)
                    elif n == EARLY + 16:
                        conditioned(b, 1)
                    elif n >= 29:
                        linear_parts(b, n - 29)
                linear_parts(b, 3)
                linear_keys(b)
                for c in range(2):
                    values(b, c, vb, 6, "lv_ps", "lv_ready")
                linear_queries(b)
                for step in range(NT * HG):
                    if step < 2:
                        context_sums(b, step)
                    if step == 1:
                        context_norm(b)
                        if b is None:
                            tables()
                    elif step == 4:
                        linear_out(b)
                    if LOCAL0 <= step < LOCAL0 + NV:
                        local_max(b, step - LOCAL0)
                    if step == 8:
                        odd_out(a, 1)
                    elif step == 10:
                        reciprocals(a, 0)
                    elif step == 11:
                        normalized(a, 0)
                    if LOCAL0 < step <= LOCAL0 + NV:
                        local_back(b, step - LOCAL0 - 1)
                    if LOCAL0 <= step < LOCAL0 + NV:
                        local_norm(b, step - LOCAL0)
                odd_out(a, 3)
                reciprocals(a, 1)
                normalized(a, 1)
                final_tokens(b)
                attended(a, 0)
                attended(a, 1)
                if more:
                    scale_shift(a + 1, "a", 0, hT_a)
                if b is not None:
                    assert at[0] == LINKS, at[0]

            scale_shift(0, "a", 0, hT_a)
            batches(dve, body)


def phase_route(nc, t, dr):
    R = 2 * NB * G
    RQ = NB * G
    with ExitStack() as ctx:
        def sb(name, shape, dt=F32):
            return ctx.enter_context(nc.sbuf_tensor(name, shape, dt))

        def sem(name):
            return ctx.enter_context(nc.semaphore(name))

        ps, co, cr, place = t["ps"], t["co"], t["cr"], t["place"]

        def const(name):
            if name in CR:
                return cr[:, CR[name][0]:CR[name][1]]
            return co[:, CO[name][0]:CO[name][1]]

        def bank(k):
            return ps[:, k * BANK:(k + 1) * BANK]

        ident = const("ident")
        logits = sb("logits", [R, L])
        half = L // 2
        SORTED = 2 * (half // 8)
        left = sb("left", [P, half])
        top = sb("top", [P, half // 8, 8])
        first = top[:, :, :].rearrange("p k n -> p (k n)")
        second = sb("second", [R, half])
        cand = sb("cand", [R, half + 1])
        limit = sb("limit", [R, 1])
        above = sb("above", [R, L])
        equal = sb("equal", [R, L])
        both = sb("both", [P, 2, NT, R])
        need = sb("need", [P, R])
        pick = sb("pick", [P, NT, R])
        rows = sb("rows", [R, L])
        sig = sb("sigmoids", [P, NT * R])
        sig_hi, sig_lo = (t["sig"][:, :, :, part].rearrange("p t r -> p (t r)") for part in range(2))

        loaded, vec, flags_ps, both_ready, count_ps, pick_ready, order_ps, place_ready, rows_ps, \
            rows_ready, moved = (sem(n) for n in (
                "r_loaded", "r_vec", "r_flags_ps", "r_both", "r_count_ps", "r_pick", "r_order_ps",
                "r_place", "r_rows_ps", "r_rows", "r_moved"))
        raw_loaded = [sem(f"r_raw_loaded{c}") for c in range(3)]
        high_ready, low_ready, rest_loaded = (sem(n) for n in ("r_high", "r_low", "r_rest_loaded"))

        def piece(c):
            return slice(c * ND * E, (c + 1) * ND * E)

        columns_ps, tanh_ready, sig_ready, sig_hi_ready, nvw_ps = (
            sem(n) for n in ("r_columns_ps", "r_tanh", "r_sig", "r_sig_hi", "r_nvw_ps"))

        block = ctx.enter_context(nc.Block())

        @block.sync
        def _(sp):
            for c in range(2):
                sp.dma_start(logits[RQ * c:RQ * c + RQ, :], dr["logits"][c].rearrange("b g n -> (b g) n"))\
                    .then_inc(loaded, 16)
                for h in range(2):
                    row = R * h + RQ * c
                    sp.dma_start(left[row:row + RQ, :], dr["logits"][c][:, :, half * h:half * (h + 1)]
                                 .rearrange("b g n -> (b g) n")).then_inc(loaded, 16)
            sp.dma_start(cr[:, :], dr["cr"]).then_inc(loaded, 16)
            sp.dma_start(t["wall"][:, :, :], dr["wc"].rearrange("g p n -> p g n")).then_inc(rest_loaded, 16)
            sp.dma_start(t["null"][:, :], dr["null"].to_broadcast([P, D])).then_inc(rest_loaded, 16)
            sp.dma_start(t["x2"][:, :, :], dr["x2"][0].rearrange("(t p) d -> p t d", p=P)).then_inc(rest_loaded, 16)
            for j in range(3 * G):
                g, c = j // 3, j % 3
                if g:
                    sp.wait_ge(low_ready, j - 2)
                if j == 4:
                    sp.wait_ge(vec, SORTED)
                    sp.dma_start(second[:, :], first[R:2 * R, :]).then_inc(moved, 16)
                sp.dma_start(t["w_raw"][:, piece(c)], dr["ws"][g][:, piece(c)]).then_inc(raw_loaded[c], 16)
            sp.wait_ge(rows_ready, 1)
            sp.dma_start(dr["place"], rows[0:RQ, :]).then_inc(moved, 16)
            sp.wait_ge(moved, 32)
            sp.wait_ge(rest_loaded, 48)

        @block.scalar
        def _(act):
            act.wait_ge(columns_ps, 1)
            act.activation(sig[:, :], bank(5)[:, 0:NT * R], ACT.Tanh, scale=0.5).then_inc(tanh_ready, 1)
            act.wait_ge(sig_ready, 1)
            act.activation(sig_hi, sig[:, :], ACT.Copy).then_inc(sig_hi_ready, 1)
            act.wait_ge(rest_loaded, 48)
            act.activation(t["x2_hi"][:, :, :], t["x2"][:, :, :], ACT.Copy).then_inc(high_ready, 1)
            for j in range(3 * G):
                g, c = j // 3, j % 3
                act.wait_ge(raw_loaded[c], 16 * (g + 1))
                act.activation(t["w_hi"][:, g, piece(c)], t["w_raw"][:, piece(c)], ACT.Copy).then_inc(high_ready, 1)
            act.wait_ge(nvw_ps, 1)
            act.activation(t["nvw"][:, :, :], ps[0:FH, 6 * BANK:8 * BANK].rearrange("p (g n) -> p g n", g=G), ACT.Copy)

        @block.gpsimd
        def _(pool):
            pool.memset(t["kT"][:, :], 0.0)
            pool.wait_ge(high_ready, 1)
            pool.tensor_tensor(t["x2_lo"][:, :, :], t["x2"][:, :, :], t["x2_hi"][:, :, :].bitcast(F32), ALU.subtract)
            for j in range(3 * G):
                g, c = j // 3, j % 3
                pool.wait_ge(high_ready, j + 2)
                pool.tensor_tensor(t["w_lo"][:, g, piece(c)], t["w_raw"][:, piece(c)],
                                   t["w_hi"][:, g, piece(c)].bitcast(F32), ALU.subtract).then_inc(low_ready, 1)

        @block.vector
        def _(dve):
            n = [0]

            def link(ins):
                n[0] += 1
                ins.then_inc(vec, 1)
                dve.wait_ge(vec, n[0])

            dve.wait_ge(loaded, 112)
            dve.wait_ge(tanh_ready, 1)
            dve.tensor_scalar(sig[:, :], sig[:, :], 1.0, 0.5, ALU.add, ALU.mult).then_inc(sig_ready, 1)
            dve.wait_ge(sig_hi_ready, 1)
            dve.tensor_tensor(sig_lo, sig[:, :], sig_hi.bitcast(F32), ALU.subtract)
            link(dve.tensor_scalar(left[R:2 * R, :], left[R:2 * R, :], -1.0, None, ALU.mult))
            for k in range(half // 8):
                link(dve.max(top[:, k, :], left[:, :]))
                if k < half // 8 - 1:
                    link(dve.match_replace(left[:, :], top[:, k, :], left[:, :], -3.0e38))
            dve.wait_ge(moved, 16)
            for r0, n_top in ((0, NQ), (RQ, NK)):
                r, at = slice(r0, r0 + RQ), half - n_top
                dve.scalar_tensor_tensor(cand[r, 1:n_top], second[r, at + 1:half], -1.0, first[r, 0:n_top - 1],
                                         ALU.mult, ALU.min)
                dve.tensor_scalar(cand[r, 0:1], second[r, at:at + 1], -1.0, None, ALU.mult)
                last = dve.tensor_copy(cand[r, n_top:n_top + 1], first[r, n_top - 1:n_top])
            link(last)
            dve.tensor_reduce(limit[0:RQ, :], cand[0:RQ, 0:NQ + 1], AX, ALU.max)
            link(dve.tensor_reduce(limit[RQ:R, :], cand[RQ:R, 0:NK + 1], AX, ALU.max))
            link(dve.tensor_scalar(above[:, :], logits[:, :], limit[:, 0:1], None, ALU.is_gt))
            link(dve.tensor_scalar(equal[:, :], logits[:, :], limit[:, 0:1], None, ALU.is_equal))
            dve.wait_ge(flags_ps, 1)
            dve.tensor_copy(both[:, :, :, :], bank(0)[:, 0:2 * NT * R].rearrange("p (a t r) -> p a t r", a=2, t=NT))\
                .then_inc(both_ready, 1)
            dve.wait_ge(count_ps, 1)
            link(dve.tensor_tensor(need[:, :], const("kvec"), bank(1)[:, 0:R], ALU.subtract))
            link(dve.tensor_tensor(pick[:, :, :], bank(2)[:, 0:NT * R].rearrange("p (t r) -> p t r", t=NT),
                                   need[:, None, :].to_broadcast([P, NT, R]), ALU.is_lt))
            link(dve.tensor_tensor(pick[:, :, :], pick[:, :, :], both[:, 1, :, :], ALU.mult))
            dve.tensor_tensor(pick[:, :, :], pick[:, :, :], both[:, 0, :, :], ALU.add).then_inc(pick_ready, 1)
            dve.wait_ge(order_ps, 1)
            link(dve.scalar_tensor_tensor(place[:, :, :], bank(3)[:, 0:NT * R].rearrange("p (t r) -> p t r", t=NT),
                                          1.0, pick[:, :, :], ALU.add, ALU.mult))
            dve.tensor_scalar(place[:, :, :], place[:, :, :], 1.0, None, ALU.subtract).then_inc(place_ready, 1)
            dve.wait_ge(rows_ps, 1)
            dve.tensor_copy(rows[:, :], bank(4)[0:R, :]).then_inc(rows_ready, 1)

        @block.tensor
        def _(pe):
            pe.wait_ge(loaded, 112)
            for k in range(NT):
                last = pe.transpose(bank(5)[:, k * R:(k + 1) * R], logits[:, k * P:(k + 1) * P], ident[0:R, 0:R])
            last.then_inc(columns_ps, 1)
            pe.wait_ge(rest_loaded, 48)
            for g in range(G):
                wo, nv = (t["wall"][:, g, WC[name][0]:WC[name][1]].rearrange("p (k n) -> p k n", k=NE)
                          for name in ("wo", "nv"))
                for e in range(NE):
                    last = pe.matmul(bank(6 + g // 2)[0:FH, (g % 2) * D:(g % 2 + 1) * D], nv[:, e, :],
                                     wo[:, e, :], start=(e == 0), stop=(e == NE - 1))
            last.then_inc(nvw_ps, 1)
            pe.wait_ge(vec, SORTED + 4)
            for a, src in enumerate((above, equal)):
                for k in range(NT):
                    c = (a * NT + k) * R
                    last = pe.transpose(bank(0)[:, c:c + R], src[:, k * P:(k + 1) * P], ident[0:R, 0:R])
            last.then_inc(flags_ps, 1)

            def before(out, src):
                for k in range(NT):
                    for m in range(k + 1):
                        last = pe.matmul(out[:, k * R:(k + 1) * R], const("ones") if m < k else const("before"),
                                         src(m), start=(m == 0), stop=(m == k))
                return last

            pe.wait_ge(both_ready, 1)
            for k in range(NT):
                pe.matmul(bank(1)[:, 0:R], const("ones"), both[:, 0, k, :], start=(k == 0), stop=(k == NT - 1))
            before(bank(2), lambda m: both[:, 1, m, :]).then_inc(count_ps, 1)
            pe.wait_ge(pick_ready, 1)
            before(bank(3), lambda m: pick[:, m, :]).then_inc(order_ps, 1)
            pe.wait_ge(place_ready, 1)
            for k in range(NT):
                last = pe.transpose(bank(4)[0:R, k * P:(k + 1) * P], place[:, k, :], ident)
            last.then_inc(rows_ps, 1)


def phase_routed(nc, t, dr):
    with ExitStack() as ctx:
        def sb(name, shape, dt=F32):
            return ctx.enter_context(nc.sbuf_tensor(name, shape, dt))

        def sem(name):
            return ctx.enter_context(nc.semaphore(name))

        ps, co, cr, place = t["ps"], t["co"], t["cr"], t["place"]
        wall, null, w_hi, w_lo = t["wall"], t["null"], t["w_hi"], t["w_lo"]

        def const(name):
            if name in CR:
                return cr[:, CR[name][0]:CR[name][1]]
            return co[:, CO[name][0]:CO[name][1]]

        def bank(k, n=1):
            return ps[:, k * BANK:(k + n) * BANK]

        ident = const("ident")
        W2 = NQ + NK
        S1 = NK + 1
        nvw, x2, x2_hi, x2_lo = (t[name] for name in ("nvw", "x2", "x2_hi", "x2_lo"))
        kT = t["kT"][:, :].rearrange("p (s e a n) -> p s e a n", s=2, e=NE, a=2)
        x1 = sb("c_x1", [P, NT, D])
        prow = sb("prow", [P, 2, L])
        pl = sb("pl", [P, NT, 2, G])
        sg = sb("sg", [P, NT, 2, G, 2], F32R)
        hot = sb("hot", [P, NT, W2], F32R)
        xg_hi = sb("xg_hi", [P, ND, W2], F32R)
        xg_lo = sb("xg_lo", [P, ND, W2], F32R)
        score = sb("score", [P, 2, 4])
        qT = sb("qT", [P, 2, NE, NQ])
        v = sb("v", [P, 2, E])
        p = sb("p", [P, 2, FH, S1])
        pT = sb("pT", [P, FH, NQ])
        pnT = sb("pnT", [FH, NQ])
        oT = sb("oT", [P, NE, NQ])
        oq_hi = sb("oq_hi", [P, 2, D], F32R)
        oq_lo = sb("oq_lo", [P, 2, D], F32R)
        hot_t = sb("hot_t", [P, 2, L], F32R)
        fmax = sb("fmax", [P, 16])
        fneg = sb("fneg", [P, 16])
        fden = sb("fden", [P, 16])
        frec = sb("frec", [P, 16])
        seen = sb("seen", [P, NT, G])
        cnt = sb("cnt", [P, 4, NT])

        def wg(g, name, k):
            a, b = WC[name]
            return wall[:, g, a:b].rearrange("p (k n) -> p k n", k=k)

        def ws(part, g, name):
            a, b = WS[name]
            return part[:, g, a:b].rearrange("p (k n) -> p k n", k=ND)

        s = {n: sem("c_" + n) for n in (
            "x1_loaded",  "x2_loaded", "x2_hi", "x2_lo",
            "place_back0", "place_back1", "pl_ready", "hot", "xg_ps", "xg_ready", "sg_ready", "score_ps",
            "score_ready", "q_ps", "k_ps", "v_ps", "qT_ready", "kT_ready", "v_ready", "s_ps",
            "fmax_link", "fneg_ready", "exp_done", "frec_link", "p_ready", "pT_ps", "pT_ready",
            "pn_ps", "pn_ready", "o_ps", "oT_ready", "out_ps", "oq_hi", "oq_lo", "hot_t", "sum_ps",
            "counts", "fin_link", "fin", "stored")}

        def need(eng, name, value):
            if not isinstance(value, int) or value > 0:
                eng.wait_ge(s[name], value)

        def batches(eng, body):
            body(0)
            with eng.Fori(1, NB - 1) as i:
                body(i)
            body(NB - 1)

        def is_first(i):
            return isinstance(i, int) and i == 0

        def is_last(i):
            return isinstance(i, int) and i == NB - 1

        def tiles(ap, i):
            one = ap[i:i + 1] if isinstance(i, int) else ap[bass.ds(i, 1)]
            return one.rearrange("a (t p) d -> p (a t) d", p=P)

        block = ctx.enter_context(nc.Block())

        @block.sync
        def _(sp):
            def load_x2(i):
                need(sp, "x2_lo", i - 1)
                sp.dma_start(x2[:, :, :], tiles(dr["x2"], i)).then_inc(s["x2_loaded"], 16)

            def body(i):
                if not is_last(i):
                    load_x2(i + 1)
                for g in range(G):
                    n = i * G + g
                    need(sp, "hot_t", (n - 1) * 2)
                    row = dr["place"][n:n + 1] if isinstance(i, int) else dr["place"][bass.ds(n, 1)]
                    sp.dma_start(prow[:, g % 2, :], row.to_broadcast([P, L]))\
                        .then_inc(s[f"place_back{g % 2}"], 16)
                    if g == 1:
                        if not is_first(i):
                            need(sp, "fin", i * NT)
                            sp.dma_start(tiles(dr["out"], i - 1), x1[:, :, :]).then_inc(s["stored"], 16)
                            sp.wait_ge(s["stored"], i * 16)
                        sp.dma_start(x1[:, :, :], tiles(dr["x1"], i)).then_inc(s["x1_loaded"], 16)

            batches(sp, body)
            sp.wait_ge(s["fin"], NB * NT)
            sp.dma_start(tiles(dr["out"], NB - 1), x1[:, :, :]).then_inc(s["stored"], 16)
            sp.wait_ge(s["stored"], NB * 16)

        @block.gpsimd
        def _(pool):
            def body(i):
                for g in range(G):
                    n = i * G + g
                    for c in range(2):
                        pool.wait_ge(s["frec_link"], 2 * n + c + 1)
                        pool.tensor_tensor(p[:, c, :, :], p[:, c, :, :],
                                           frec[:, FH * c:FH * c + FH, None].to_broadcast([P, FH, S1]),
                                           ALU.mult).then_inc(s["p_ready"], 1)

            batches(pool, body)

        @block.scalar
        def _(act):
            def split_x2(i):
                act.wait_ge(s["x2_loaded"], i * 16)
                need(act, "xg_ps", i * 4 * G)
                act.activation(x2_hi[:, :, :], x2[:, :, :], ACT.Copy).then_inc(s["x2_hi"], 1)

            def null_keys(n, g):
                need(act, "s_ps", (n - 1) * 4)
                for hh in range(2):
                    r = slice(64 * hh, 64 * hh + 64)
                    act.activation(kT[r, g % 2, :, hh, NK:S1], wg(g, "nk", NE)[r, :, :], ACT.Copy)

            def gathered(n, d):
                for c, part in enumerate((xg_hi, xg_lo)):
                    act.wait_ge(s["xg_ps"], n * 4 + 2 * d + c + 1)
                    if d == 0 and c == 0:
                        need(act, "v_ps", n)
                    act.activation(part[:, d, :], bank(5 - c)[:, 0:W2], ACT.Copy).then_inc(s["xg_ready"], 1)

            def queries(n, g):
                for c in range(2):
                    act.wait_ge(s["q_ps"], n * 2 + c + 1)
                    act.activation(qT[:, g % 2, 2 * c:2 * c + 2, :], bank(4 + c).rearrange("p (a n) -> p a n", a=2),
                                   ACT.Copy).then_inc(s["qT_ready"], 1)

            def values(n, g):
                act.wait_ge(s["score_ready"], n + 1)
                act.wait_ge(s["v_ps"], n + 1)
                need(act, "o_ps", (n - 1) * 2)
                act.activation(v[:, g % 2, :], bank(4), ACT.Copy, scale=score[:, g % 2, 2:3])\
                    .then_inc(s["v_ready"], 1)

            def exps(n, u):
                act.wait_ge(s["fneg_ready"], n * 4 + u + 1)
                if u == 0:
                    need(act, "pT_ps", n * 4)
                    need(act, "pn_ps", n)
                for a in range(4):
                    h, c = 4 * (u % 2) + a, 4 * u + a
                    act.activation(p[:, u // 2, h, :],
                                   bank(2 * (u % 2) + a // 2)[:, (a % 2) * S1:(a % 2 + 1) * S1],
                                   ACT.Exp, scale=FD ** -0.5, bias=fneg[:, c:c + 1],
                                   accum_out=fden[:, c:c + 1]).then_inc(s["exp_done"], 1)

            def outputs(n, g):
                need(act, "sum_ps", n)
                for c in range(2):
                    act.wait_ge(s["out_ps"], n * 2 + c + 1)
                    act.activation(oq_hi[:, c, :], bank(5 - c)[:, 0:D], ACT.Copy,
                                   scale=score[:, g % 2, c:c + 1]).then_inc(s["oq_hi"], 1)

            null_keys(0, 0)
            gathered(0, 0)
            gathered(0, 1)
            queries(0, 0)
            values(0, 0)

            def body(i):
                for g in range(G):
                    n = i * G + g
                    more = not (is_last(i) and g == G - 1)
                    exps(n, 0)
                    if g == G - 1 and more:
                        split_x2(i + 1)
                    if not (is_first(i) and g == 0):
                        outputs(n - 1, (g - 1) % G)
                    if more:
                        gathered(n + 1, 0)
                    exps(n, 1)
                    if more:
                        gathered(n + 1, 1)
                    exps(n, 2)
                    exps(n, 3)
                    if more:
                        null_keys(n + 1, (g + 1) % G)
                        queries(n + 1, (g + 1) % G)
                    act.wait_ge(s["pn_ps"], n + 1)
                    if more:
                        act.wait_ge(s["score_ready"], n + 2)
                    act.activation(pnT[:, :], bank(5)[0:FH, 0:NQ], ACT.Copy).then_inc(s["pn_ready"], 1)
                    if more:
                        values(n + 1, (g + 1) % G)
                    for c in range(2):
                        act.wait_ge(s["o_ps"], n * 2 + c + 1)
                        act.activation(oT[:, 2 * c:2 * c + 2, :], bank(5 - c).rearrange("p (a n) -> p a n", a=2),
                                       ACT.Copy).then_inc(s["oT_ready"], 1)

            batches(act, body)
            outputs(NB * G - 1, G - 1)

        @block.tensor
        def _(pe):
            def parts(out, pairs):
                for k, (a, b) in enumerate(pairs):
                    last = pe.matmul(out, a, b, start=(k == 0), stop=(k == len(pairs) - 1))
                return last

            def three(hi_lo, other):
                (ah, al), (bh, bl) = hi_lo, other
                return [(ah, bh), (ah, bl), (al, bh)]

            def gather(n, g, d, c, i):
                if d == 0 and c == 0:
                    need(pe, "v_ready", n)
                    need(pe, "score_ready", n)
                    need(pe, "oT_ready", (n - 1) * 2)
                    pe.wait_ge(s["hot"], (n + 1) * 8)
                    if g == 0:
                        need(pe, "x2_lo", i)
                if d == 0:
                    need(pe, "oq_lo", (n - 2) * 2 + c + 1)
                part = (x2_hi, x2_lo)[c]
                if d == 1:
                    pe.wait_ge(s["xg_ready"], n * 4 + c + 1)
                for k in range(NT):
                    last = pe.matmul(bank(5 - c)[:, 0:W2], part[:, k, d * P:(d + 1) * P], hot[:, k, :],
                                     start=(k == 0), stop=(k == NT - 1))
                last.then_inc(s["xg_ps"], 1)

            def query_proj(n, g):
                pe.wait_ge(s["xg_ready"], n * 4 + 4)
                for c in range(2):
                    for b in range(2):
                        e = slice((2 * c + b) * P, (2 * c + b + 1) * P)
                        last = parts(bank(4 + c)[:, b * NQ:(b + 1) * NQ],
                                     [x for d in range(ND) for x in three(
                                         (ws(w_hi, g, "wq")[:, d, e], ws(w_lo, g, "wq")[:, d, e]),
                                         (xg_hi[:, d, 0:NQ], xg_lo[:, d, 0:NQ]))])
                    last.then_inc(s["q_ps"], 1)

            def key_proj(n, g):
                pe.wait_ge(s["qT_ready"], n * 2 + 1)
                for e in range(NE):
                    es = slice(e * P, (e + 1) * P)
                    last = parts(bank(4)[:, e * NK:(e + 1) * NK],
                                 [x for d in range(ND) for x in three(
                                     (ws(w_hi, g, "wk")[:, d, es], ws(w_lo, g, "wk")[:, d, es]),
                                     (xg_hi[:, d, NQ:W2], xg_lo[:, d, NQ:W2]))])
                last.then_inc(s["k_ps"], 1)

            def route_scores(n, g, c, i):
                pe.wait_ge(s["qT_ready"], n * 2 + 2)
                pe.wait_ge(s["sg_ready"], i + 1)
                for k in range(NT):
                    last = pe.matmul(bank(5)[:, 256 + 2 * c:258 + 2 * c], hot[:, k, c * P:(c + 1) * P],
                                     sg[:, k, c // 2, g, :], start=(k == 0), stop=(k == NT - 1))
                if c == 2:
                    last.then_inc(s["score_ps"], 1)

            def value_proj(n, g):
                pe.wait_ge(s["kT_ready"], n * 2 + 2)
                parts(bank(4), [x for d in range(ND) for x in three(
                    (xg_hi[:, d, NQ:W2], xg_lo[:, d, NQ:W2]),
                    (ws(w_hi, g, "wv")[:, d, :], ws(w_lo, g, "wv")[:, d, :]))]).then_inc(s["v_ps"], 1)

            def scores(n, g, u):
                if u == 0:
                    need(pe, "pT_ready", n * 4 - 2)
                    pe.wait_ge(s["qT_ready"], n * 2 + 2)
                    pe.wait_ge(s["kT_ready"], n * 2 + 2)
                elif u == 1:
                    need(pe, "pT_ready", n * 4)
                else:
                    pe.wait_ge(s["exp_done"], n * 16 + 4 * (u - 1))
                for b in range(2):
                    e = 2 * (u % 2) + b
                    last = pe.matmul(bank(2 * (u % 2) + b)[:, 0:2 * S1],
                                     qT[:, g % 2, e, (u // 2) * P:(u // 2 + 1) * P],
                                     kT[:, g % 2, e, :, :].rearrange("p a n -> p (a n)"), start=True, stop=True)
                last.then_inc(s["s_ps"], 1)

            def to_keys(n, c, b):
                pe.wait_ge(s["p_ready"], n * 2 + c + 1)
                pe.wait_ge(s["exp_done"], n * 16 + 12 + 4 * c)
                for a in range(4):
                    last = pe.transpose(bank(2 * c + b)[:, a * P:(a + 1) * P], p[:, c, 4 * b + a, 0:NK], ident)
                last.then_inc(s["pT_ps"], 1)

            def null_to_rows(n):
                pe.wait_ge(s["p_ready"], n * 2 + 2)
                for c in range(2):
                    last = pe.transpose(bank(5)[0:FH, c * P:(c + 1) * P], p[:, c, :, NK], ident)
                last.then_inc(s["pn_ps"], 1)

            def weigh(n, g):
                for c in range(2):
                    pe.wait_ge(s["pT_ready"], n * 4 + 4)
                    if c == 0:
                        pe.wait_ge(s["pn_ready"], n + 1)
                        pe.wait_ge(s["v_ready"], n + 1)
                    else:
                        pe.wait_ge(s["v_ready"], n + 1 if n_is_final(n) else n + 2)
                    for b in range(2):
                        for hh in range(2):
                            h = 2 * (2 * c + b) + hh
                            last = pe.matmul(bank(5 - c)[64 * hh:64 * hh + 64, b * NQ:(b + 1) * NQ],
                                             v[:, g % 2, h * FD:(h + 1) * FD], pT[:, h, :], start=True, stop=True)
                    last.then_inc(s["o_ps"], 1)

            def n_is_final(n):
                return isinstance(n, int) and n == NB * G - 1

            def output(n, g):
                pe.wait_ge(s["oT_ready"], n * 2 + 2)
                for c in range(2):
                    out = bank(5 - c)[:, 0:D]
                    for e in range(NE):
                        pe.matmul(out, oT[:, e, c * P:(c + 1) * P], wg(g, "wo", NE)[:, e, :],
                                  start=(e == 0), stop=False)
                    pe.matmul(out, pnT[:, c * P:(c + 1) * P], nvw[:, g, :], start=False, stop=True)\
                        .then_inc(s["out_ps"], 1)

            def scatter(n, g, done):
                if g == 0:
                    need(pe, "fin", done)
                pe.wait_ge(s["oq_lo"], n * 2 + 2)
                pe.wait_ge(s["hot_t"], n * 2 + 2)
                for k in range(NT):
                    for c in range(2):
                        for part in (oq_hi, oq_lo):
                            last = pe.matmul(bank(6 + k // 2)[:, (k % 2) * D:(k % 2 + 1) * D],
                                             hot_t[:, c, k * P:(k + 1) * P], part[:, c, :],
                                             start=(g == 0 and c == 0 and k % 2 == 0 and part is oq_hi),
                                             stop=(g == G - 1 and c == 1 and k % 2 == 1 and part is oq_lo),
                                             skip_group_check=True)
                last.then_inc(s["sum_ps"], 1)

            for d in range(ND):
                for c in range(2):
                    gather(0, 0, d, c, 0)
            query_proj(0, 0)
            key_proj(0, 0)
            for c in range(3):
                route_scores(0, 0, c, 0)
            value_proj(0, 0)

            def body(i):
                for g in range(G):
                    n = i * G + g
                    g1 = (g + 1) % G
                    more = not (is_last(i) and g == G - 1)
                    scores(n, g, 0)
                    scores(n, g, 1)
                    if not (is_first(i) and g == 0):
                        output(n - 1, (g - 1) % G)
                    scores(n, g, 2)
                    if more:
                        gather(n + 1, g1, 0, 0, i + 1)
                        gather(n + 1, g1, 0, 1, i + 1)
                    if not (is_first(i) and g == 0):
                        scatter(n - 1, (g - 1) % G, i * NT)
                    if more:
                        gather(n + 1, g1, 1, 0, i + 1)
                        gather(n + 1, g1, 1, 1, i + 1)
                    scores(n, g, 3)
                    if more:
                        query_proj(n + 1, g1)
                    to_keys(n, 0, 0)
                    to_keys(n, 0, 1)
                    if more:
                        key_proj(n + 1, g1)
                        pe.wait_ge(s["qT_ready"], n * 2 + 4)
                    null_to_rows(n)
                    for c in range(3):
                        if more:
                            route_scores(n + 1, g1, c, i + 1 if g == G - 1 else i)
                        if c < 2:
                            to_keys(n, 1, c)
                    if more:
                        value_proj(n + 1, g1)
                    weigh(n, g)

            batches(pe, body)
            output(NB * G - 1, G - 1)
            scatter(NB * G - 1, G - 1, 0)

        @block.vector
        def _(dve):
            def places(i):
                need(dve, "hot", i * G * 8)
                need(dve, "counts", i * 5)
                cols = slice(i * G, i * G + G) if isinstance(i, int) else bass.ds(i * G, G)
                dve.tensor_copy(pl[:, :, :, :], place[:, :, :].rearrange("p t (c r) -> p t c r", c=2)
                                [:, :, :, cols]).then_inc(s["pl_ready"], 1)
                dve.wait_ge(s["pl_ready"], i + 1)

            def place_scores(i):
                need(dve, "score_ps", i * G)
                cols = slice(i * G, i * G + G) if isinstance(i, int) else bass.ds(i * G, G)
                dve.tensor_copy(sg[:, :, :, :, :].rearrange("p t c g a -> p (t c) g a"),
                                t["sig"][:, :, :, :].rearrange("p t (c r) a -> p (t c) r a", c=2)
                                [:, :, cols, :].bitcast(F32)).then_inc(s["sg_ready"], 1)

            def low_x2(i):
                dve.wait_ge(s["x2_hi"], i)
                dve.tensor_tensor(x2_lo[:, :, :], x2[:, :, :], x2_hi[:, :, :].bitcast(F32), ALU.subtract)\
                    .then_inc(s["x2_lo"], 1)

            def counts(i):
                dve.tensor_scalar(seen[:, :, :], pl[:, :, 0, :], 0.0, None, ALU.is_ge).then_inc(s["counts"], 1)
                dve.wait_ge(s["counts"], i * 5 + 1)
                dve.tensor_reduce(cnt[:, 0, :], seen[:, :, :], AX, ALU.add).then_inc(s["counts"], 1)
                dve.wait_ge(s["counts"], i * 5 + 2)
                dve.tensor_scalar(cnt[:, 1, :], cnt[:, 0, :], 1e-5, None, ALU.max).then_inc(s["counts"], 1)
                dve.tensor_scalar(cnt[:, 3, :], cnt[:, 0, :], 0.0, None, ALU.is_equal).then_inc(s["counts"], 1)
                dve.wait_ge(s["counts"], i * 5 + 4)
                dve.reciprocal(cnt[:, 2, :], cnt[:, 1, :]).then_inc(s["counts"], 1)

            def one_hot(n, g):
                need(dve, "score_ps", n)
                for k in range(NT):
                    dve.tensor_scalar(hot[:, k, 0:NQ], const("iota"), pl[:, k, 0, g:g + 1], None,
                                      ALU.is_equal).then_inc(s["hot"], 1)
                    dve.tensor_scalar(hot[:, k, NQ:W2], const("iota")[:, 0:NK], pl[:, k, 1, g:g + 1], None,
                                      ALU.is_equal).then_inc(s["hot"], 1)

            def one_hot_back(n, g, i):
                dve.wait_ge(s[f"place_back{g % 2}"], i * 32 + (g // 2) * 16 + 16)
                need(dve, "sum_ps", n)
                for c in range(2):
                    dve.tensor_scalar(hot_t[:, c, :], prow[:, g % 2, :], const("part")[:, c:c + 1], None,
                                      ALU.is_equal).then_inc(s["hot_t"], 1)

            def keys(n, g):
                dve.wait_ge(s["k_ps"], n + 1)
                need(dve, "s_ps", (n - 1) * 4)
                for hh in range(2):
                    r = slice(64 * hh, 64 * hh + 64)
                    dve.tensor_copy(kT[r, g % 2, :, hh, 0:NK], bank(4)[r, :].rearrange("p (e n) -> p e n", e=NE))\
                        .then_inc(s["kT_ready"], 1)

            def route_scores(n, g):
                dve.wait_ge(s["score_ps"], n + 1)
                need(dve, "oq_lo", (n - 1) * 2)
                dve.tensor_reduce(score[:, g % 2, 0:3], bank(5)[:, 256:262].rearrange("p (c a) -> p c a", a=2),
                                  AX, ALU.add).then_inc(s["score_ready"], 1)

            def maxima(n, u):
                dve.wait_ge(s["s_ps"], n * 4 + u + 1)
                need(dve, "exp_done", n * 16 - 4 * (3 - u))
                dve.tensor_reduce(fmax[:, 4 * u:4 * u + 4].rearrange("p (a c) -> p a c", a=2),
                                  bank(2 * (u % 2), 2).rearrange("p (a n) -> p a n", a=2)[:, :, 0:2 * S1]
                                  .rearrange("p a (c n) -> p a c n", c=2), AX, ALU.max)\
                    .then_inc(s["fmax_link"], 1)
                dve.wait_ge(s["fmax_link"], n * 4 + u + 1)
                dve.tensor_scalar(fneg[:, 4 * u:4 * u + 4], fmax[:, 4 * u:4 * u + 4], -FD ** -0.5, None,
                                  ALU.mult).then_inc(s["fneg_ready"], 1)

            def reciprocals(n, c):
                dve.wait_ge(s["exp_done"], n * 16 + 8 * c + 8)
                need(dve, "p_ready", n * 2 - 1 + c)
                dve.reciprocal(frec[:, FH * c:FH * c + FH], fden[:, FH * c:FH * c + FH])\
                    .then_inc(s["frec_link"], 1)

            def turned(n, c):
                need(dve, "o_ps", n * 2)
                for b in range(2):
                    dve.wait_ge(s["pT_ps"], n * 4 + 2 * c + b + 1)
                    dve.tensor_copy(pT[:, 4 * b:4 * b + 4, c * P:(c + 1) * P],
                                    bank(2 * c + b).rearrange("p (a n) -> p a n", a=4)).then_inc(s["pT_ready"], 1)

            def low_outputs(n, g):
                for c in range(2):
                    dve.wait_ge(s["oq_hi"], n * 2 + c + 1)
                    dve.scalar_tensor_tensor(oq_lo[:, c, :], bank(5 - c)[:, 0:D],
                                             score[:, g % 2, c:c + 1], oq_hi[:, c, :].bitcast(F32),
                                             ALU.mult, ALU.subtract).then_inc(s["oq_lo"], 1)

            def finish(i):
                dve.wait_ge(s["x1_loaded"], i * 16 + 16)
                dve.wait_ge(s["sum_ps"], i * G + G)
                dve.wait_ge(s["counts"], i * 5 + 5)
                for k in range(NT):
                    dve.scalar_tensor_tensor(x1[:, k, :], null[:, :], cnt[:, 3, k:k + 1], x1[:, k, :],
                                             ALU.mult, ALU.add).then_inc(s["fin_link"], 1)
                for k in range(NT):
                    dve.wait_ge(s["fin_link"], i * NT + k + 1)
                    dve.scalar_tensor_tensor(x1[:, k, :], bank(6 + k // 2)[:, (k % 2) * D:(k % 2 + 1) * D],
                                             cnt[:, 2, k:k + 1], x1[:, k, :], ALU.mult, ALU.add)\
                        .then_inc(s["fin"], 1)

            places(0)
            one_hot(0, 0)
            place_scores(0)
            keys(0, 0)
            route_scores(0, 0)
            one_hot(1, 1)

            def body(i):
                for g in range(G):
                    n = i * G + g
                    g1 = (g + 1) % G
                    more = not (is_last(i) and g == G - 1)
                    maxima(n, 0)
                    maxima(n, 1)
                    if g == G - 1 and more:
                        low_x2(i + 1)
                        place_scores(i + 1)
                    if not (is_first(i) and g == 0):
                        low_outputs(n - 1, (g - 1) % G)
                    maxima(n, 2)
                    reciprocals(n, 0)
                    maxima(n, 3)
                    if g == 0:
                        if not is_first(i):
                            finish(i - 1)
                        counts(i)
                    one_hot_back(n, g, i)
                    reciprocals(n, 1)
                    turned(n, 0)
                    if more:
                        keys(n + 1, g1)
                    turned(n, 1)
                    if more:
                        route_scores(n + 1, g1)
                    if g == G - 2 and not is_last(i):
                        places(i + 1)
                    if not (is_last(i) and g >= G - 2):
                        one_hot(n + 2, (g + 2) % G)

            batches(dve, body)
            low_outputs(NB * G - 1, G - 1)
            finish(NB - 1)


def build(nc, x, co_d, cr_d, cw_d, wa_d, wb_d, bo_d, ws_d, wc_d, null_d, out):
    def scratch(name, shape):
        return nc.dram_tensor(name, shape, F32).ap()

    dr = dict(x=x, co=co_d, cr=cr_d, cw=cw_d, wa=wa_d, wb=wb_d, bo=bo_d, ws=ws_d, wc=wc_d, null=null_d, out=out,
              parts=scratch("parts", (2, 2, D, L)), x1=scratch("x1_d", (NB, L, D)),
              x2=scratch("x2_d", (NB, L, D)), logits=scratch("logits_d", (2, NB, G, L)),
              place=scratch("place_d", (NB * G, L)))
    with ExitStack() as ctx:
        t = dict(ps=ctx.enter_context(nc.psum_tensor("ps", [P, 8 * BANK], F32)),
                 co=ctx.enter_context(nc.sbuf_tensor("co", [P, CO_N], F32)),
                 place=ctx.enter_context(nc.sbuf_tensor("place", [P, NT, 2 * NB * G], F32)))
        phase_dense(nc, t, dr)
        t["cr"] = ctx.enter_context(nc.sbuf_tensor("cr", [P, CR_N], F32))
        for name, shape, dt in (("wall", [P, G, WC_N], F32), ("null", [P, D], F32), ("nvw", [FH, G, D], F32), ("x2", [P, NT, D], F32), ("x2_hi", [P, NT, D], F32R),
                                ("x2_lo", [P, NT, D], F32R), ("kT", [P, 4 * NE * (NK + 1)], F32),
                                ("sig", [P, NT, 2 * NB * G, 2], F32R), ("w_hi", [P, G, WS_N], F32R), ("w_lo", [P, G, WS_N], F32R)):
            t[name] = ctx.enter_context(nc.sbuf_tensor(name, shape, dt))
        with nc.sbuf_tensor("w_raw", [P, WS_N], F32) as w_raw:
            t["w_raw"] = w_raw
            phase_route(nc, t, dr)
        phase_routed(nc, t, dr)




def by_tile(a):
    k = a.shape[0] // P
    return np.ascontiguousarray(a.reshape(k, P, a.shape[1]).transpose(1, 0, 2)).reshape(P, -1)


def strips_cols(a, heads):
    out = np.zeros((a.shape[0], heads, STRIP), np.float32)
    out[:, :, :DH] = a.reshape(a.shape[0], heads, DH)
    return out.reshape(a.shape[0], heads * STRIP)


def pack(cols, n, parts, lead=()):
    out = np.zeros((*lead, P, n), np.float32)
    for name, (a, b) in cols.items():
        v = parts[name]
        out[..., :v.shape[-2], a:b] = v
    return out


def kernel(**inputs):
    import concourse.bacc as bacc
    from concourse.bass_utils import run_bass_kernel_spmd

    f = {k: np.asarray(v) for k, v in inputs.items()}
    c, a, r = ({k[len(pre):]: v for k, v in f.items() if k.startswith(pre)}
               for pre in ("L0_cond_", "L0_attn_", "L0_ffn_"))
    wa = pack(WA, WA_N, dict(
        wq=by_tile(c["Wq"].T), wk=by_tile(c["Wk"].T), wv=by_tile(c["Wv"].T),
        wo=by_tile(c["Wo"].T.reshape(2, 2, 4, DH, D).transpose(0, 2, 1, 3, 4).reshape(D, D)), gate=by_tile(c["gate_w"].T), hid=by_tile(c["hid_w"].T),
        down=by_tile(c["out_w"].T)))
    lin = np.concatenate([a["Wq"][:, NLOC * DH:], a["Wk"][:, NLOC * DH:]], axis=1)
    wo_lin = a["Wo"][NLOC * DH:].reshape(2, LW, D).transpose(1, 0, 2).reshape(LW, 2 * D)
    wb = pack(WB, WB_N, dict(
        lq=by_tile(strips_cols(a["Wq"][:, :NLOC * DH], NLOC)),
        lk=by_tile(strips_cols(a["Wk"][:, :NLOC * DH], NLOC)), lin=by_tile(lin), wv=by_tile(a["Wv"]),
        wo_loc=strips_cols(np.ascontiguousarray(a["Wo"][:NLOC * DH].T), NLOC).T, wo_lin=wo_lin))
    wkv = r["w_kv"]
    nk, nv = r["null_kv"][:, :, :, 0, :]
    spread = np.zeros((G, FH, FD, FH), np.float32)
    for h in range(FH):
        spread[:, h, :, h] = nv[:, h]
    ws = np.stack([pack(WS, WS_N, dict(
        wq=by_tile(r["w_q"][g].T), wk=by_tile(wkv[g, :E].T), wv=by_tile(wkv[g, E:].T))) for g in range(G)])
    wc = np.stack([pack(WC, WC_N, dict(
        wo=by_tile(r["w_out"][g].T), nk=by_tile(nk[g].reshape(E, 1)),
        nv=by_tile(spread[g].reshape(E, FH)))) for g in range(G)])
    row, part = np.arange(P), np.arange(P)
    tri = row[None, :] > part[:, None]
    cq = f["cond_256"]
    ks = np.zeros((P, 2 * NB * G), np.float32)
    ks[:, :NB * G], ks[:, NB * G:] = NQ, NK
    co = pack(CO, CO_N, dict(
        ident=np.eye(P), causal=np.where(tri, -CBIG, 0.0), all=np.full((P, P), -CBIG),
        hmask=(part[:, None] // STRIP == np.arange(NLOC)), dsel=(part[:, None] == np.concatenate([STRIP * np.arange(4) + DH, STRIP * np.arange(4)])),
        odd=(part[:, None] // DH % 2 == np.arange(2)),
        cmask=(part[:, None] % 64 == np.arange(64)), bmask=(part[:, None] // DH == np.arange(LH)),
        qleft=np.tile(cq.T, (2, 1)),
        qright=np.tile(f["L0_cond2_q_right"].T, (2, 1)),
        sg=np.tile(f["L0_cond2_spectral_gate"].reshape(64, 1), (2, 1)),
        sign=np.tile(np.array([1, -1, -1, -1]), (P, 1)),
        wr=by_tile(np.concatenate([r["w_qr"], r["w_kvr"]]).T),
        cb=np.concatenate([c[n].reshape(ND, P).T for n in ("g1b", "b1b", "g2b", "b2b")], axis=1),
        cond=cq.T))
    cr = pack(CR, CR_N, dict(iota=np.tile(np.arange(NQ), (P, 1)), part=part[:, None] + P * np.arange(2),
                             before=tri, ones=np.ones((P, P)), kvec=ks))
    cw = np.concatenate([c[n].T for n in ("g1w", "b1w", "g2w", "b2w")], axis=1)
    arrays = dict(x=f["x"], co=co, cr=cr, cw=cw, wa=wa, wb=wb, bo=a["bo"].reshape(1, D), ws=ws, wc=wc,
                  null=r["null_token"].reshape(1, D))
    arrays = {f"in_{k}": np.ascontiguousarray(v) for k, v in arrays.items()}

    nc = bacc.Bacc("TRN2", target_bir_lowering=False, num_devices=1)
    args = [nc.dram_tensor(k, v.shape, mybir.dt.from_np(v.dtype), kind="ExternalInput").ap()
            for k, v in arrays.items()]
    out = nc.dram_tensor("out", (NB, L, D), F32, kind="ExternalOutput").ap()
    build(nc, *args, out)
    got = run_bass_kernel_spmd(nc, [arrays], core_ids=[0])
    return got.results[0]["out"]
```
